# Optimizing a Trainium2 kernel written in Bass

```python
import numpy as np
import jax
import jax.numpy as jnp

def _softmax(x, axis=-1):
    return jax.nn.softmax(x, axis=axis)

def _gelu(x):
    return jax.nn.gelu(x, approximate=True)

def _silu(x):
    return jax.nn.silu(x)

def _sigmoid(x):
    return jax.nn.sigmoid(x)

def _layernorm(x, axis=-1, eps=1e-05):
    m = jnp.mean(x, axis=axis, keepdims=True)
    v = jnp.var(x, axis=axis, keepdims=True)
    return (x - m) / jnp.sqrt(v + eps)

def _scatter_add(tgt, idx, src, axis=0):
    return tgt.at[idx].add(src)

def _segment_sum(src, seg, n):
    return jax.ops.segment_sum(src, seg, n)
kernel_name = 'mk_macaron_d1_jaxref_r2_6da5e8'

def setup_inputs(seed: int=0):
    np.random.seed(seed)
    _w = jnp.asarray

    def _L0_attn_setup():
        import jax, jax.numpy as jnp
        import numpy as np
        D_MODEL = 512
        NHEAD = 16
        HEAD_DIM = D_MODEL // NHEAD
        MAX_POS = 1024

        def _rope_tables(seq_len, dim):
            inv_freq = 1.0 / 10000.0 ** (jnp.arange(0, dim, 2, dtype=jnp.float32) / dim)
            t = jnp.arange(seq_len, dtype=jnp.float32)[:, None]
            freqs = t * inv_freq[None, :]
            emb = jnp.concatenate([freqs, freqs], axis=-1)
            return (jnp.cos(emb), jnp.sin(emb))

        def _rotate_half(x):
            x1, x2 = jnp.split(x, 2, axis=-1)
            return jnp.concatenate([-x2, x1], axis=-1)

        def _apply_rope(x, cos, sin):
            c = cos[None, :, None, :]
            s = sin[None, :, None, :]
            return x * c + _rotate_half(x) * s
        key = jax.random.key(seed)
        ks = jax.random.split(key, 9)
        B, L, D = (4, 1024, D_MODEL)
        lim = 1.0 / np.sqrt(D)

        def lin(k):
            kw, kb = jax.random.split(k)
            W = jax.random.uniform(kw, (D, D), jnp.float32, -lim, lim)
            b = jax.random.uniform(kb, (D,), jnp.float32, -lim, lim)
            return (W, b)
        Wq, bq = lin(ks[0])
        Wk, bk = lin(ks[1])
        Wv, bv = lin(ks[2])
        Wo, bo = lin(ks[3])
        x = jax.random.normal(ks[4], (B, L, D), jnp.float32)
        return {'x': x, 'Wq': Wq, 'bq': bq, 'Wk': Wk, 'bk': bk, 'Wv': Wv, 'bv': bv, 'Wo': Wo, 'bo': bo}
    _L0_attn_in = _L0_attn_setup()

    def _L0_ffn_setup():
        import math
        import jax, jax.numpy as jnp
        import numpy as np
        CAPACITY_FACTOR = 1.25
        key = jax.random.key(seed)
        ks = jax.random.split(key, 5)
        B, S, H, F, E = (4, 2048, 512, 512, 32)
        scale_in = 1.0 / math.sqrt(H)
        scale_mid = 1.0 / math.sqrt(F)
        return {'x': jax.random.normal(ks[0], (B, S, H), dtype=jnp.float32), 'w_router': jax.random.normal(ks[1], (H, E), dtype=jnp.float32) * scale_in, 'w_gate': jax.random.normal(ks[2], (E, H, F), dtype=jnp.float32) * scale_in, 'w_up': jax.random.normal(ks[3], (E, H, F), dtype=jnp.float32) * scale_in, 'w_down': jax.random.normal(ks[4], (E, F, H), dtype=jnp.float32) * scale_mid}
    _L0_ffn_in = _L0_ffn_setup()
    _d = {'L0_attn_x': _L0_attn_in['x'], 'L0_attn_Wq': _L0_attn_in['Wq'], 'L0_attn_bq': _L0_attn_in['bq'], 'L0_attn_Wk': _L0_attn_in['Wk'], 'L0_attn_bk': _L0_attn_in['bk'], 'L0_attn_Wv': _L0_attn_in['Wv'], 'L0_attn_bv': _L0_attn_in['bv'], 'L0_attn_Wo': _L0_attn_in['Wo'], 'L0_attn_bo': _L0_attn_in['bo'], 'L0_ffn_w_router': _L0_ffn_in['w_router'], 'L0_ffn_w_gate': _L0_ffn_in['w_gate'], 'L0_ffn_w_up': _L0_ffn_in['w_up'], 'L0_ffn_w_down': _L0_ffn_in['w_down']}
    _x0 = _d['L0_attn_x']
    _d['L0_attn_x'] = jax.random.normal(jax.random.fold_in(jax.random.key(seed), 1), (8, 1024, 512), dtype=_x0.dtype)
    del _x0
    return _d

def reference(L0_attn_x, L0_attn_Wq, L0_attn_bq, L0_attn_Wk, L0_attn_bk, L0_attn_Wv, L0_attn_bv, L0_attn_Wo, L0_attn_bo, L0_ffn_w_router, L0_ffn_w_gate, L0_ffn_w_up, L0_ffn_w_down):

    def _L0_attn_ref(x, Wq, bq, Wk, bk, Wv, bv, Wo, bo):
        import jax, jax.numpy as jnp
        import numpy as np
        D_MODEL = 512
        NHEAD = 16
        HEAD_DIM = D_MODEL // NHEAD
        MAX_POS = 1024

        def _rope_tables(seq_len, dim):
            inv_freq = 1.0 / 10000.0 ** (jnp.arange(0, dim, 2, dtype=jnp.float32) / dim)
            t = jnp.arange(seq_len, dtype=jnp.float32)[:, None]
            freqs = t * inv_freq[None, :]
            emb = jnp.concatenate([freqs, freqs], axis=-1)
            return (jnp.cos(emb), jnp.sin(emb))

        def _rotate_half(x):
            x1, x2 = jnp.split(x, 2, axis=-1)
            return jnp.concatenate([-x2, x1], axis=-1)

        def _apply_rope(x, cos, sin):
            c = cos[None, :, None, :]
            s = sin[None, :, None, :]
            return x * c + _rotate_half(x) * s
        B, L, D = x.shape
        H, hd = (NHEAD, HEAD_DIM)
        q = (x @ Wq.T + bq).reshape(B, L, H, hd)
        k = (x @ Wk.T + bk).reshape(B, L, H, hd)
        v = (x @ Wv.T + bv).reshape(B, L, H, hd)
        cos, sin = _rope_tables(L, hd)
        q = _apply_rope(q, cos, sin)
        k = _apply_rope(k, cos, sin)
        scores = jnp.einsum('bqhd,bkhd->bhqk', q, k) / np.sqrt(hd).astype(np.float32)
        attn = jax.nn.softmax(scores, axis=-1)
        out = jnp.einsum('bhqk,bkhd->bqhd', attn, v).reshape(B, L, D)
        return out @ Wo.T + bo

    def _L0_ffn_ref(x, w_router, w_gate, w_up, w_down):
        import math
        import jax, jax.numpy as jnp
        import numpy as np
        CAPACITY_FACTOR = 1.25
        B, S, H = x.shape
        E = w_gate.shape[0]
        T = B * S
        C = int(math.ceil(CAPACITY_FACTOR * T / E))
        xt = x.reshape(T, H)
        logits = xt @ w_router
        probs = jax.nn.softmax(logits, axis=-1)
        top1 = jnp.argmax(probs, axis=-1)
        gate = jnp.take_along_axis(probs, top1[:, None], axis=1)[:, 0]
        onehot = jax.nn.one_hot(top1, E, dtype=jnp.int32)
        pos = jnp.cumsum(onehot, axis=0)[jnp.arange(T), top1] - 1
        accepted = pos < C
        slot = jnp.where(accepted, top1 * C + pos, E * C)
        buf = jnp.zeros((E * C + 1, H), dtype=x.dtype).at[slot].set(xt)
        buf = buf[:E * C].reshape(E, C, H)
        g = jnp.einsum('ech,ehf->ecf', buf, w_gate)
        u = jnp.einsum('ech,ehf->ecf', buf, w_up)
        y = jnp.einsum('ecf,efh->ech', jax.nn.silu(g) * u, w_down)
        out_tok = y.reshape(E * C, H)[jnp.clip(slot, 0, E * C - 1)]
        out_tok = jnp.where(accepted[:, None], out_tok * gate[:, None], 0.0)
        return (xt + out_tok).reshape(B, S, H)
    x = L0_attn_x
    x = x + 0.5 * _L0_ffn_ref(_layernorm(x, axis=-1), L0_ffn_w_router, L0_ffn_w_gate, L0_ffn_w_up, L0_ffn_w_down)
    x = x + _L0_attn_ref(_layernorm(x, axis=-1), L0_attn_Wq, L0_attn_bq, L0_attn_Wk, L0_attn_bk, L0_attn_Wv, L0_attn_bv, L0_attn_Wo, L0_attn_bo)
    x = x + 0.5 * _L0_ffn_ref(_layernorm(x, axis=-1), L0_ffn_w_router, L0_ffn_w_gate, L0_ffn_w_up, L0_ffn_w_down)
    return x

_drawn_inputs = setup_inputs


def setup_inputs(seed=0):
    import zlib

    import numpy as np

    out = dict(_drawn_inputs(seed))
    spreads = {}
    factors = {'L0_attn_Wq': 8.0,
     'L0_attn_bq': 8.0,
     'L0_attn_Wk': 8.0,
     'L0_attn_bk': 8.0,
     'L0_attn_Wv': 7.144,
     'L0_attn_bv': 5.339,
     'L0_attn_Wo': 4.475,
     'L0_attn_bo': 20.748}
    for name, (base, spread) in spreads.items():
        noise = np.random.default_rng([zlib.crc32(name.encode()), seed]).standard_normal(out[name].shape)
        drawn = base * np.exp(spread * noise) if base else spread * noise
        out[name] = jnp.asarray(drawn.astype(out[name].dtype))
    for name, factor in factors.items():
        out[name] = (out[name] * factor).astype(out[name].dtype)
    return out
```

```python
import concourse.bass as bass
from concourse import mybir
from contextlib import ExitStack

F32 = mybir.dt.float32
F32R = mybir.dt.float32r
BF16 = mybir.dt.bfloat16
I32 = mybir.dt.int32
U32 = mybir.dt.uint32
ALU = mybir.AluOpType
ACT = mybir.ActivationFunctionType
AX = mybir.AxisListType

P = 128
B, L, D = 8, 1024, 512
T = B * L
NH, HD = 16, 32
E, F = 32, 512
C = (5 * T + 4 * E - 1) // (4 * E)
CT = (C + P - 1) // P
CW = 4 * (-(-C // (4 * CT)))
CP = CT * CW
NOSLOT = E * CP
KD = D // P
KF = F // P
TJ = 4
GROUP = TJ * P
NG = T // GROUP
EPS = 1e-5
BANK = 512


def past(count):
    return max(count, 0) if isinstance(count, int) else count


def work_out(eng, *counts):
    for count in counts:
        if not isinstance(count, int):
            eng.compute_val(count)


def rounds(eng, n, body):
    assert n % 2 == 0 and n >= 4
    body(0, 0)
    body(0, 1)
    if n > 4:
        with eng.Fori(1, n // 2 - 1) as i:
            body(i, 0)
            body(i, 1)
    body(n // 2 - 1, 0)
    body(n // 2 - 1, 1)


def rounds_ahead(eng, n, body):
    def step(i, par, more=True):
        body(i, par, (i, 1) if par == 0 else (i + 1, 0) if more else None)
    step(0, 0)
    step(0, 1)
    with eng.Fori(1, n // 2 - 1) as i:
        step(i, 0)
        step(i, 1)
    step(n // 2 - 1, 0)
    step(n // 2 - 1, 1, False)


class Chain:
    def __init__(self, sem, steps):
        self.sem, self.steps = sem, steps

    def start(self, eng, r):
        self.eng, self.r, self.k = eng, r, 0

    def link(self, ins):
        ins.then_inc(self.sem, 1)
        self.k += 1
        self.eng.wait_ge(self.sem, self.r * self.steps + self.k)

    def end(self):
        assert self.k == self.steps, self.k


class Space:
    def __init__(self, nc, name):
        self.nc, self.name, self.ctx, self.sems = nc, name, ExitStack(), []

    def sb(self, name, shape, dt=F32):
        return self.ctx.enter_context(self.nc.sbuf_tensor(f"{self.name}_{name}", shape, dt))

    def ps(self, name, shape, dt=F32):
        return self.ctx.enter_context(self.nc.psum_tensor(f"{self.name}_{name}", shape, dt))

    def bank(self, name, n):
        return self.ps(name, [P, BANK])[:, 0:n]

    def sem(self, name):
        self.sems.append(self.ctx.enter_context(self.nc.semaphore(f"{self.name}_{name}")))
        return self.sems[-1]

    def pair(self, make, name, *a):
        return [make(f"{name}_{i}", *a) for i in range(2)]

    def clear(self):
        nums = sorted(s.num for s in self.sems)
        lo = nums[0]
        for a, b in zip(nums, nums[1:] + [None]):
            if b != a + 1:
                self.nc.all_engine_barrier(sems_to_clear=range(lo, a + 1))
                lo = b

    def block(self):
        self.ctx.callback(self.clear)
        return self.ctx.enter_context(self.nc.Block())


def matmul3(nc, out, lhs, rhs, start, stop):
    nc.tensor.matmul(out, lhs[0], rhs[0], start=start, stop=False)
    nc.tensor.matmul(out, lhs[0], rhs[1], start=False, stop=False)
    return nc.tensor.matmul(out, lhs[1], rhs[0], start=False, stop=stop)


def tiles(ap):
    return ap.rearrange("(j p) n -> p j n", p=P)


def route(nc, name, moved, x_in, wr, cst, xn_out, table, y_zero, slot_out, gate_out, attn=None):
    S = Space(nc, name)
    sb, ps, sem = S.sb, S.ps, S.sem
    with S.ctx:
        ident = sb("ident", [P, P])
        trif = sb("trif", [P, P])
        tri = sb("tri", [P, P], BF16)
        ones = sb("ones", [P, P], BF16)
        iota = sb("iota", [P, E])
        tokf = sb("tokf", [P, TJ])
        wr_sb = sb("wr", [P, KD, E])
        unset = sb("unset", [P, NOSLOT // P], I32)
        zrow = sb("zrow", [1, D])
        eps = sb("eps", [P, 1])
        run = sb("run", [P, E], BF16)
        x = S.pair(sb, "x", [P, TJ, D])
        xn = S.pair(sb, "xn", [P, TJ, D])
        xnT = S.pair(sb, "xnT", [P, KD, P])
        stats = S.pair(sb, "stats", [P, 6])
        mv = sb("mv", [P, TJ, 2])
        std = sb("std", [P, TJ])
        rstd = sb("rstd", [P, TJ])
        top = sb("top", [P, TJ, 8])
        topi = sb("topi", [P, TJ, 8], U32)
        shifted = sb("shifted", [P, TJ, E])
        ex = sb("ex", [P, TJ, E])
        den = sb("den", [P, TJ])
        gate = sb("gate", [P, TJ])
        idxf = sb("idxf", [P, TJ])
        onehot = sb("onehot", [P, TJ, E], BF16)
        picked = sb("picked", [P, TJ, E])
        pos = sb("pos", [P, TJ])
        ok = sb("ok", [P, TJ])
        slot = sb("slot", [P, TJ])
        slot2 = sb("slot2", [P, TJ])
        seen = sb("seen", [P, E])
        slot_i = S.pair(sb, "slot_i", [P, TJ], I32)
        tok_i = S.pair(sb, "tok_i", [P, TJ], I32)
        gateh = S.pair(sb, "gateh", [P, TJ])
        tp = S.pair(ps, "tp", [P, KD, P])
        logits = S.bank("logits", TJ * E).rearrange("p (j e) -> p j e", e=E)
        posp = S.bank("posp", TJ * E).rearrange("p (j e) -> p j e", e=E)

        s_const = sem("s_const")
        s_memset = sem("s_memset")
        s_setup = sem("s_setup")
        s_unset = sem("s_unset")
        s_x = S.pair(sem, "s_x")
        s_stats = sem("s_stats")
        s_mv = sem("s_mv")
        s_std = sem("s_std")
        s_rstd = sem("s_rstd")
        s_xn = sem("s_xn")
        s_xn_stored = S.pair(sem, "s_xn_stored")
        s_tp = sem("s_tp")
        s_xnT = sem("s_xnT")
        s_logits = sem("s_logits")
        s_top = sem("s_top")
        s_shifted = sem("s_shifted")
        s_exp = sem("s_exp")
        s_onehot = sem("s_onehot")
        s_pos = sem("s_pos")
        s_slots = sem("s_slots")
        s_run = sem("s_run")
        s_scat = moved
        s_meta = S.pair(sem, "s_meta")
        pick = Chain(sem("s_pick"), 4)
        place = Chain(sem("s_place"), 8)
        n_const = 6
        if attn:
            ao_num, ao_den, woT, bo, x_out = attn
            bo_sb = sb("bo", [P, D])
            wraw = sb("wraw", [P, KD, D])
            wo = S.pair(sb, "wo", [P, KD, D], F32R)
            num = sb("num", [P, KD, GROUP])
            dnm = sb("dnm", [P, KD, GROUP])
            aof = sb("aof", [P, KD, GROUP])
            ao = S.pair(sb, "ao", [P, KD, GROUP], F32R)
            op = S.pair(ps, "op", [P, D])
            s_ao_in = sem("s_ao_in")
            s_rec = sem("s_rec")
            s_aof = sem("s_aof")
            s_ao = sem("s_ao")
            s_wo = sem("s_wo")
            s_xb = sem("s_xb")
            s_op = sem("s_op")
            s_x2 = sem("s_x2")
            s_x2_stored = S.pair(sem, "s_x2_stored")
            n_const = 8
        block = S.block()
        met = (s_const, 16 * n_const)

        def x_ap(ap, i, par):
            return tiles(ap[bass.ds((2 * i + par) * GROUP, GROUP), :])

        def ao_ap(ap, i, par):
            return ap[bass.ds(i, 1), :, par * GROUP:(par + 1) * GROUP].rearrange(
                "o (k p) q -> p (o k) q", p=P)

        @block.sync
        def _(sp):
            sp.dma_start(ident[:, :], cst["ident"]).then_inc(s_const, 16)
            sp.dma_start(trif[:, :], cst["tri"]).then_inc(s_const, 16)
            sp.dma_start(iota[:, :], cst["iota"]).then_inc(s_const, 16)
            sp.dma_start(tokf[:, :], cst["tok"]).then_inc(s_const, 16)
            sp.dma_start(wr_sb[:, :, :], wr.rearrange("(k p) e -> p k e", p=P)).then_inc(s_const, 16)
            if attn:
                sp.dma_start(bo_sb[:, :], bo.rearrange("(o n) -> o n", o=1).broadcast_to([P, D])).then_inc(s_const, 16)
                sp.dma_start(wraw[:, :, :], woT.rearrange("(k p) n -> p k n", p=P)).then_inc(s_const, 16)
            sp.wait_ge(s_memset, 5)
            sp.dma_start(table[0:NOSLOT, :].rearrange("(p n) o -> p (n o)", p=P), unset[:, :]).then_inc(s_unset, 16)
            sp.dma_start(xn_out[T:T + 1, :], zrow[:, :]).then_inc(s_unset, 16)
            sp.dma_start(y_zero, zrow[:, :]).then_inc(s_const, 16)

            def load(i, par):
                if attn:
                    sp.wait_ge(s_x2_stored[par], 16 * i)
                    sp.wait_ge(s_ao, 2 * (2 * i + par))
                    sp.dma_start(num[:, :, :], ao_ap(ao_num, i, par)).then_inc(s_ao_in, 16)
                    sp.dma_start(dnm[:, :, :], ao_ap(ao_den, i, par)).then_inc(s_ao_in, 16)
                sp.wait_ge(s_xn, past(TJ * (2 * i + par - 1)))
                sp.dma_start(x[par][:, :, :], x_ap(x_in, i, par)).then_inc(s_x[par], 16)

            def store(i, par):
                if attn:
                    sp.wait_ge(s_x2, TJ * (2 * i + par + 1))
                    sp.dma_start(x_ap(x_out, i, par), x[par][:, :, :]).then_inc(s_x2_stored[par], 16)
                sp.wait_ge(s_xn, TJ * (2 * i + par + 1))
                sp.dma_start(x_ap(xn_out, i, par), xn[par][:, :, :]).then_inc(s_xn_stored[par], 16)

            def meta(i, par):
                work_out(sp, 2 * i + par + 1)
                sp.wait_ge(*met)
                sp.wait_ge(s_slots, 2 * i + par + 1)
                sp.dma_start(slot_out[bass.ds(2 * i + par, 1), :, :].rearrange("o p j -> (o p) j"),
                             slot_i[par][:, :]).then_inc(s_meta[par], 16)
                sp.dma_start(gate_out[bass.ds(2 * i + par, 1), :, :].rearrange("o p j -> (o p) j"),
                             gateh[par][:, :]).then_inc(s_meta[par], 16)

            def step(i, par, nxt):
                if nxt:
                    load(*nxt)
                store(i, par)
                meta(i, par)

            load(0, 0)
            rounds_ahead(sp, NG, step)
            for par in range(2):
                sp.wait_ge(s_xn_stored[par], 16 * (NG // 2))
                sp.wait_ge(s_meta[par], 32 * (NG // 2))
                if attn:
                    sp.wait_ge(s_x2_stored[par], 16 * (NG // 2))
            sp.wait_ge(s_const, 16 * n_const)
            sp.wait_ge(s_unset, 32)

        @block.gpsimd
        def _(pool):
            nc.gpsimd.memset(ones[:, :], 1.0).then_inc(s_memset, 1)
            nc.gpsimd.memset(unset[:, :], T).then_inc(s_memset, 1)
            nc.gpsimd.memset(zrow[:, :], 0.0).then_inc(s_memset, 1)
            nc.gpsimd.memset(eps[:, :], EPS).then_inc(s_memset, 1)
            nc.gpsimd.memset(run[:, :], 0.0).then_inc(s_memset, 1)
            pool.wait_ge(s_unset, 32)

            def split(i, par):
                r = 2 * i + par
                pool.wait_ge(s_rec, r + 1)
                pool.wait_ge(s_ao, 2 * r)
                nc.gpsimd.tensor_tensor(out=aof[:, :, :], in0=num[:, :, :], in1=dnm[:, :, :],
                                        op=ALU.mult).then_inc(s_aof, 1)
                work_out(pool, r + 1, TJ * r)
                pool.wait_ge(*met)
                pool.wait_ge(s_aof, r + 1)
                pool.wait_ge(s_op, TJ * r)
                nc.gpsimd.tensor_copy(ao[0][:, :, :], aof[:, :, :]).then_inc(s_ao, 1)
                pool.wait_ge(s_ao, 2 * r + 1)
                nc.gpsimd.tensor_tensor(out=ao[1][:, :, :], in0=aof[:, :, :], in1=ao[0][:, :, :].bitcast(F32),
                                        op=ALU.subtract).then_inc(s_ao, 1)

            def scatter(i, par):
                work_out(pool, 2 * i + par + 1)
                pool.wait_ge(*met)
                pool.wait_ge(s_slots, 2 * i + par + 1)
                for j in range(TJ):
                    nc.gpsimd.indirect_dma_start(
                        out=table[0:NOSLOT, :], out_offset=bass.IndirectOffsetOnAxis(ap=slot_i[par][:, j:j + 1], axis=0),
                        in_=tok_i[par][:, j:j + 1], in_offset=None,
                        bounds_check=NOSLOT - 1, oob_is_err=False).then_inc(s_scat[par], 16)

            def step(i, par, nxt):
                if attn and nxt:
                    split(*nxt)
                scatter(i, par)

            if attn:
                pool.wait_ge(s_const, 16 * n_const)
                split(0, 0)
            rounds_ahead(pool, NG, step)
            for par in range(2):
                pool.wait_ge(s_scat[par], 16 * TJ * (NG // 2))

        @block.scalar
        def _(act):
            act.wait_ge(s_memset, 5)

            def norm(i, par):
                r = 2 * i + par
                act.wait_ge(s_mv, TJ * (r + 1))
                nc.scalar.activation(std[:, :], mv[:, :, 1], ACT.Sqrt, bias=eps[:, 0:1]).then_inc(s_std, 1)

            def copies(i, par):
                for j in range(TJ):
                    n = TJ * (2 * i + par) + j
                    act.wait_ge(s_tp, n + 1)
                    act.wait_ge(s_logits, past(n - 1))
                    nc.scalar.activation(xnT[j % 2][:, :, :], tp[j % 2][:, :, :], ACT.Copy).then_inc(s_xnT, 1)

            def exps(i, par):
                r = 2 * i + par
                act.wait_ge(s_shifted, r + 1)
                act.wait_ge(pick.sem, pick.steps * r)
                nc.scalar.activation(ex[:, :, :], shifted[:, :, :], ACT.Exp).then_inc(s_exp, 1)

            def step(i, par, nxt):
                exps(i, par)
                if nxt:
                    norm(*nxt)
                    copies(*nxt)

            norm(0, 0)
            copies(0, 0)
            rounds_ahead(act, NG, step)

        @block.vector
        def _(dve):
            dve.wait_ge(s_const, 16 * n_const)
            dve.wait_ge(s_memset, 5)
            nc.vector.tensor_copy(tri[:, :], trif[:, :]).then_inc(s_setup, 1)
            if attn:
                nc.vector.tensor_copy(wo[0][:, :, :], wraw[:, :, :]).then_inc(s_wo, 1)
                dve.wait_ge(s_wo, 1)
                nc.vector.tensor_tensor(out=wo[1][:, :, :], in0=wraw[:, :, :], in1=wo[0][:, :, :].bitcast(F32),
                                        op=ALU.subtract).then_inc(s_wo, 1)

            def recip(i, par):
                r = 2 * i + par
                dve.wait_ge(s_ao_in, 32 * (r + 1))
                nc.vector.reciprocal(dnm[:, :, :], dnm[:, :, :]).then_inc(s_rec, 1)

            def normalise(i, par):
                r = 2 * i + par
                dve.wait_ge(s_x[par], 16 * (i + 1))
                if attn:
                    nc.vector.tensor_tensor(out=x[par][:, :, :], in0=x[par][:, :, :],
                                            in1=bo_sb[:, :].unsqueeze(1).broadcast_to([P, TJ, D]),
                                            op=ALU.add).then_inc(s_xb, 1)
                    dve.wait_ge(s_xb, r + 1)
                for j in range(TJ):
                    n = TJ * r + j
                    if attn:
                        dve.wait_ge(s_op, n + 1)
                        nc.vector.tensor_tensor(out=x[par][:, j, :], in0=x[par][:, j, :], in1=op[j % 2][:, :],
                                                op=ALU.add).then_inc(s_x2, 1)
                        dve.wait_ge(s_x2, n + 1)
                    dve.wait_ge(s_mv, past(n - 1))
                    nc.vector.bn_stats(stats[j % 2][:, :], x[par][:, j, :]).then_inc(s_stats, 1)
                    work_out(dve, n + 1, r, TJ * r)
                    dve.wait_ge(*met)
                    dve.wait_ge(s_stats, n + 1)
                    dve.wait_ge(s_std, r)
                    dve.wait_ge(s_xn, TJ * r)
                    nc.vector.bn_aggr(mv[:, j, :], stats[j % 2][:, :]).then_inc(s_mv, 1)
                dve.wait_ge(s_std, r + 1)
                dve.wait_ge(s_mv, TJ * (r + 1))
                nc.vector.reciprocal(rstd[:, :], std[:, :]).then_inc(s_rstd, 1)
                dve.wait_ge(s_rstd, r + 1)
                dve.wait_ge(s_xn_stored[par], 16 * i)
                dve.wait_ge(s_tp, past(TJ * r - TJ))
                for j in range(TJ):
                    nc.vector.tensor_scalar(xn[par][:, j, :], x[par][:, j, :], mv[:, j, 0:1], rstd[:, j:j + 1],
                                            ALU.subtract, ALU.mult).then_inc(s_xn, 1)

            def choose(i, par):
                r = 2 * i + par
                work_out(dve, TJ * (r + 1))
                dve.wait_ge(*met)
                dve.wait_ge(s_logits, TJ * (r + 1))
                for j in range(TJ):
                    nc.vector.max(top[:, j, :], logits[:, j, :]).then_inc(s_top, 1)
                work_out(dve, 2 * TJ * r + TJ)
                dve.wait_ge(*met)
                dve.wait_ge(s_top, 2 * TJ * r + TJ)
                for j in range(TJ):
                    nc.vector.max_index(topi[:, j, :], top[:, j, :], logits[:, j, :]).then_inc(s_top, 1)
                nc.vector.tensor_tensor(out=shifted[:, :, :], in0=logits[:, :, :],
                                        in1=top[:, :, 0:1].broadcast_to([P, TJ, E]),
                                        op=ALU.subtract).then_inc(s_shifted, 1)
                dve.wait_ge(s_top, 2 * TJ * (r + 1))
                dve.wait_ge(s_shifted, r + 1)
                pick.start(dve, r)
                pick.link(nc.vector.tensor_copy(idxf[:, :], topi[:, :, 0]))
                dve.wait_ge(s_pos, r)
                nc.vector.tensor_tensor(out=onehot[:, :, :], in0=iota[:, :].unsqueeze(1).broadcast_to([P, TJ, E]),
                                        in1=idxf[:, :].unsqueeze(2).broadcast_to([P, TJ, E]),
                                        op=ALU.is_equal).then_inc(s_onehot, 1)
                dve.wait_ge(s_exp, r + 1)
                pick.link(nc.vector.tensor_reduce(out=den[:, :], in_=ex[:, :, :], axis=AX.X, op=ALU.add))
                pick.link(nc.vector.reciprocal(gate[:, :], den[:, :]))
                dve.wait_ge(s_onehot, r + 1)
                pick.link(nc.vector.tensor_reduce(out=seen[:, :], in_=onehot[:, :, :].rearrange("p j e -> p e j"),
                                                  axis=AX.X, op=ALU.add))

            def slots(i, par):
                r = 2 * i + par
                dve.wait_ge(s_pos, r + 1)
                nc.vector.tensor_tensor(out=run[:, :], in0=run[:, :], in1=seen[:, :], op=ALU.add).then_inc(s_run, 1)
                place.start(dve, r)
                place.link(nc.vector.tensor_tensor(out=picked[:, :, :], in0=posp[:, :, :], in1=onehot[:, :, :],
                                                   op=ALU.mult))
                place.link(nc.vector.tensor_reduce(out=pos[:, :], in_=picked[:, :, :], axis=AX.X, op=ALU.add))
                place.link(nc.vector.tensor_scalar(ok[:, :], pos[:, :], float(C), None, ALU.is_le))
                place.link(nc.vector.scalar_tensor_tensor(slot[:, :], idxf[:, :], float(CP), pos[:, :],
                                                          ALU.mult, ALU.add))
                place.link(nc.vector.scalar_tensor_tensor(slot2[:, :], slot[:, :], -1.0 - NOSLOT, ok[:, :],
                                                          ALU.add, ALU.mult))
                dve.wait_ge(s_scat[par], 16 * TJ * i)
                dve.wait_ge(s_meta[par], 32 * i)
                place.link(nc.vector.tensor_scalar(slot_i[par][:, :], slot2[:, :], float(NOSLOT), None, ALU.add))
                place.link(nc.vector.tensor_copy(tok_i[par][:, :], tokf[:, :]))
                place.link(nc.vector.tensor_scalar(tokf[:, :], tokf[:, :], float(GROUP), None, ALU.add))
                nc.vector.scalar_tensor_tensor(gateh[par][:, :], gate[:, :], 0.5, ok[:, :],
                                               ALU.mult, ALU.mult).then_inc(s_slots, 1)
                work_out(dve, r + 1, r + 1)
                dve.wait_ge(*met)
                dve.wait_ge(s_slots, r + 1)
                dve.wait_ge(s_run, r + 1)

            def step(i, par, nxt):
                choose(i, par)
                if nxt:
                    if attn:
                        recip(*nxt)
                    normalise(*nxt)
                slots(i, par)

            if attn:
                recip(0, 0)
            normalise(0, 0)
            rounds_ahead(dve, NG, step)

        @block.tensor
        def _(pe):
            pe.wait_ge(s_const, 16 * n_const)
            pe.wait_ge(s_memset, 5)
            pe.wait_ge(s_setup, 1)
            if attn:
                pe.wait_ge(s_wo, 2)

            def project(i, par):
                r = 2 * i + par
                pe.wait_ge(s_ao, 2 * (r + 1))
                for j in range(TJ):
                    n = TJ * r + j
                    pe.wait_ge(s_x2, past(n - 1))
                    for k in range(KD):
                        last = matmul3(nc, op[j % 2][:, :], [a[:, k, j * P:(j + 1) * P] for a in ao],
                                       [w[:, k, :] for w in wo], k == 0, k == KD - 1)
                    last.then_inc(s_op, 1)

            def logit(i, par):
                r = 2 * i + par
                for j in range(TJ):
                    n = TJ * r + j
                    pe.wait_ge(s_xn, n + 1)
                    pe.wait_ge(s_xnT, past(n - 1))
                    for k in range(KD):
                        last = nc.tensor.transpose(tp[j % 2][:, k, :], xn[par][:, j, k * P:(k + 1) * P], ident[:, :])
                    last.then_inc(s_tp, 1)
                    if j:
                        products(r, j - 1)
                products(r, TJ - 1)

            def products(r, j):
                pe.wait_ge(s_xnT, TJ * r + j + 1)
                pe.wait_ge(s_shifted, r)
                pe.wait_ge(s_top, 2 * TJ * r)
                for k in range(KD):
                    last = nc.tensor.matmul(logits[:, j, :], xnT[j % 2][:, k, :], wr_sb[:, k, :],
                                            start=k == 0, stop=k == KD - 1)
                last.then_inc(s_logits, 1)

            def positions(i, par):
                r = 2 * i + par
                pe.wait_ge(s_onehot, r + 1)
                pe.wait_ge(s_run, r)
                pe.wait_ge(s_slots, r)
                for j in range(TJ):
                    nc.tensor.matmul(posp[:, j, :], tri[:, :], onehot[:, j, :], start=True, stop=False)
                    for before in range(j):
                        nc.tensor.matmul(posp[:, j, :], ones[:, :], onehot[:, before, :], start=False, stop=False)
                    last = nc.tensor.matmul(posp[:, j, :], ones[:, :], run[:, :], start=False, stop=True)
                last.then_inc(s_pos, 1)

            def step(i, par, nxt):
                if attn and nxt:
                    project(*nxt)
                positions(i, par)
                if nxt:
                    logit(*nxt)

            if attn:
                project(0, 0)
            logit(0, 0)
            rounds_ahead(pe, NG, step)


def experts(nc, name, moved, xn, table, wg, wu, wd, cst, y_out):
    S = Space(nc, name)
    sb, ps, sem = S.sb, S.ps, S.sem
    with S.ctx:
        ident = sb("ident", [P, P])
        raw = [sb(f"raw{w}", [P, KD, F]) for w in range(3)]
        split = [[S.pair(sb, f"w{w}_{par}", [P, KD, F], F32R) for par in range(2)] for w in range(3)]
        idx = S.pair(sb, "idx", [CW, CT], I32)
        xg = S.pair(sb, "xg", [CW, CT, D])
        xT = S.pair(sb, "xT", [P, KD, CP], F32R)
        sg = S.pair(sb, "sg", [P, CP])
        af = S.pair(sb, "af", [P, CP])
        aT = S.pair(sb, "aT", [P, KF, CP], F32R)
        y = sb("y", [CW, CT, D])
        tp = S.pair(S.bank, "tp", CP)
        gp = S.pair(S.bank, "gp", CP)
        up = S.pair(S.bank, "up", CP)
        yp = S.pair(ps, "yp", [CW, D])

        s_const = sem("s_const")
        s_raw = [sem(f"s_raw{w}") for w in range(3)]
        s_hi = sem("s_hi")
        s_lo = sem("s_lo")
        s_idx = S.pair(sem, "s_idx")
        s_xg = moved
        s_tp = sem("s_tp")
        s_xh = sem("s_xh")
        s_xl = sem("s_xl")
        s_gu = sem("s_gu")
        s_sg = sem("s_sg")
        s_af = sem("s_af")
        s_ah = sem("s_ah")
        s_al = sem("s_al")
        s_y = sem("s_y")
        s_yc = sem("s_yc")
        s_stored = sem("s_stored")
        block = S.block()
        met = (s_const, 16)
        weights = [wg, wu, wd]

        def w_ap(w, e):
            return weights[w][bass.ds(e, 1), :, :].rearrange("o (k p) f -> p (o k) f", p=P)

        def load_raw(sp, w, e):
            sp.wait_ge(s_hi, past(3 * (e - 1) + w + 1))
            sp.wait_ge(s_lo, past(3 * (e - 1) + w + 1))
            sp.dma_start(raw[w][:, :, :], w_ap(w, e)).then_inc(s_raw[w], 16)

        @block.sync
        def _(sp):
            sp.dma_start(ident[:, :], cst["ident"]).then_inc(s_const, 16)

            def load_idx(i, par):
                sp.wait_ge(s_xg[par], 16 * CT * i)
                sp.dma_start(idx[par][:, :], table[bass.ds((2 * i + par) * CP, CP), :].rearrange(
                    "(p c) o -> p (c o)", p=CW)).then_inc(s_idx[par], 16)

            def store(i, par):
                e = 2 * i + par
                sp.wait_ge(s_yc, CT * (e + 1))
                sp.dma_start(y_out[bass.ds(e * CP, CP), :].rearrange("(p c) n -> p (c n)", p=CW),
                             y[:, :, :].rearrange("p c n -> p (c n)")).then_inc(s_stored, 16)

            def step(i, par, nxt):
                if nxt:
                    load_idx(*nxt)
                    for w in range(3):
                        load_raw(sp, w, 2 * nxt[0] + nxt[1])
                store(i, par)

            load_idx(0, 0)
            for w in range(3):
                load_raw(sp, w, 0)
            rounds_ahead(sp, E, step)
            sp.wait_ge(s_stored, 16 * E)

        @block.gpsimd
        def _(pool):
            def gather(i, par):
                work_out(pool, 16 * (i + 1), KD * (2 * i + par - 1))
                pool.wait_ge(*met)
                pool.wait_ge(s_idx[par], 16 * (i + 1))
                pool.wait_ge(s_tp, past(KD * (2 * i + par - 1)))
                for c in range(CT):
                    nc.gpsimd.indirect_dma_start(
                        out=xg[par][:, c, :], out_offset=None, in_=xn,
                        in_offset=bass.IndirectOffsetOnAxis(ap=idx[par][:, c:c + 1], axis=0),
                        bounds_check=T, oob_is_err=False).then_inc(s_xg[par], 16)

            rounds(pool, E, gather)

        def hi_weight(act, w, e, par):
            act.wait_ge(s_raw[w], 16 * (e + 1))
            act.wait_ge(s_gu, past(KF * (e - 1)))
            act.wait_ge(s_y, past(CT * (e - 1)))
            nc.scalar.activation(split[w][par][0][:, :, :], raw[w][:, :, :], ACT.Copy).then_inc(s_hi, 1)

        def lo_weight(dve, w, e, par):
            dve.wait_ge(s_hi, 3 * e + w + 1)
            nc.vector.tensor_tensor(out=split[w][par][1][:, :, :], in0=raw[w][:, :, :],
                                    in1=split[w][par][0][:, :, :].bitcast(F32), op=ALU.subtract).then_inc(s_lo, 1)

        @block.scalar
        def _(act):
            def hi_x(i, par):
                e = 2 * i + par
                for k in range(KD):
                    act.wait_ge(s_tp, KD * e + k + 1)
                    act.wait_ge(s_gu, KF * e)
                    nc.scalar.activation(xT[0][:, k, :], tp[k % 2][:, :], ACT.Copy).then_inc(s_xh, 1)

            def store_y(i, par):
                e = 2 * i + par
                for c in range(CT):
                    act.wait_ge(s_y, CT * e + c + 1)
                    act.wait_ge(s_stored, 16 * e)
                    nc.scalar.activation(y[:, c, :], yp[c % 2][:, :], ACT.Copy).then_inc(s_yc, 1)

            def step(i, par, nxt):
                e = 2 * i + par
                for f in range(KF):
                    n = KF * e + f
                    act.wait_ge(s_gu, n + 1)
                    act.wait_ge(s_af, past(n - 1))
                    nc.scalar.activation(sg[f % 2][:, :], gp[f % 2][:, :], ACT.Silu).then_inc(s_sg, 1)
                    if nxt and f < 2:
                        hi_weight(act, f, 2 * nxt[0] + nxt[1], nxt[1])
                if nxt:
                    hi_x(*nxt)
                    hi_weight(act, 2, 2 * nxt[0] + nxt[1], nxt[1])
                store_y(i, par)

            for w in range(3):
                hi_weight(act, w, 0, 0)
            hi_x(0, 0)
            rounds_ahead(act, E, step)

        @block.vector
        def _(dve):
            def lo_x(i, par):
                e = 2 * i + par
                for k in range(KD):
                    dve.wait_ge(s_xh, KD * e + k + 1)
                    nc.vector.tensor_tensor(out=xT[1][:, k, :], in0=tp[k % 2][:, :],
                                            in1=xT[0][:, k, :].bitcast(F32), op=ALU.subtract).then_inc(s_xl, 1)

            def step(i, par, nxt):
                e = 2 * i + par
                for f in range(KF):
                    n = KF * e + f
                    dve.wait_ge(s_sg, n + 1)
                    dve.wait_ge(s_al, past(n - 1))
                    nc.vector.tensor_tensor(out=af[f % 2][:, :], in0=up[f % 2][:, :], in1=sg[f % 2][:, :],
                                            op=ALU.mult).then_inc(s_af, 1)
                    dve.wait_ge(s_af, n + 1)
                    dve.wait_ge(s_y, CT * e)
                    nc.vector.tensor_copy(aT[0][:, f, :], af[f % 2][:, :]).then_inc(s_ah, 1)
                    dve.wait_ge(s_ah, n + 1)
                    nc.vector.tensor_tensor(out=aT[1][:, f, :], in0=af[f % 2][:, :],
                                            in1=aT[0][:, f, :].bitcast(F32), op=ALU.subtract).then_inc(s_al, 1)
                    if nxt and f < 2:
                        lo_weight(dve, f, 2 * nxt[0] + nxt[1], nxt[1])
                if nxt:
                    lo_x(*nxt)
                    lo_weight(dve, 2, 2 * nxt[0] + nxt[1], nxt[1])

            for w in range(3):
                lo_weight(dve, w, 0, 0)
            lo_x(0, 0)
            rounds_ahead(dve, E, step)

        @block.tensor
        def _(pe):
            pe.wait_ge(s_const, 16)

            def turn(i, par):
                e = 2 * i + par
                pe.wait_ge(s_xg[par], 16 * CT * (i + 1))
                for k in range(KD):
                    pe.wait_ge(s_xl, past(KD * e + k - 1))
                    for c in range(CT):
                        last = nc.tensor.transpose(tp[k % 2][:, c * CW:(c + 1) * CW],
                                                   xg[par][:, c, k * P:(k + 1) * P],
                                                   ident[0:CW, 0:CW])
                    last.then_inc(s_tp, 1)

            def gate_up(i, par):
                e = 2 * i + par
                pe.wait_ge(s_lo, 3 * e + 2)
                for f in range(KF):
                    n = KF * e + f
                    pe.wait_ge(s_af, past(n - 1))
                    for w, out in ((0, gp), (1, up)):
                        for k in range(KD):
                            if f == 0 and w == 0:
                                pe.wait_ge(s_xl, KD * e + k + 1)
                            last = matmul3(nc, out[f % 2][:, :],
                                           [s[:, k, f * P:(f + 1) * P] for s in split[w][par]],
                                           [s[:, k, :] for s in xT], k == 0, k == KD - 1)
                    last.then_inc(s_gu, 1)

            def down(i, par):
                e = 2 * i + par
                pe.wait_ge(s_lo, 3 * e + 3)
                pe.wait_ge(s_al, KF * (e + 1))
                for c in range(CT):
                    n = CT * e + c
                    pe.wait_ge(s_yc, past(n - 1))
                    for f in range(KF):
                        last = matmul3(nc, yp[c % 2][:, :],
                                       [a[:, f, c * CW:(c + 1) * CW] for a in aT],
                                       [s[:, f, :] for s in split[2][par]], f == 0, f == KF - 1)
                    last.then_inc(s_y, 1)

            def step(i, par, nxt):
                if nxt:
                    turn(*nxt)
                down(i, par)
                if nxt:
                    gate_up(*nxt)

            turn(0, 0)
            gate_up(0, 0)
            rounds_ahead(pe, E, step)


def qkv(nc, name, moved, x_in, xn_in, y, slot_in, gate_in, wT, bias, cst, x_out, q_out, k_out, v_out):
    S = Space(nc, name)
    sb, ps, sem = S.sb, S.ps, S.sem
    with S.ctx:
        ident = sb("ident", [P, P])
        eps = sb("eps", [P, 1])
        cos = sb("cos", [P, L])
        sin = sb("sin", [P, L])
        wraw = sb("wraw", [P, KD, D])
        w = [S.pair(sb, f"w{m}", [P, KD, D], F32R) for m in range(3)]
        bqk = [sb(f"b{m}", [P, KD]) for m in range(2)]
        bv = sb("bv", [P, D])
        x = S.pair(sb, "x", [P, TJ, D])
        xn = sb("xn", [P, TJ, D])
        yg = sb("yg", [P, TJ, D])
        xa = sb("xa", [P, TJ, D])
        slot = S.pair(sb, "slot", [P, TJ], I32)
        gateh = S.pair(sb, "gateh", [P, TJ])
        stats = S.pair(sb, "stats", [P, 6])
        mv = sb("mv", [P, TJ, 2])
        std = sb("std", [P, TJ])
        rstd = sb("rstd", [P, TJ])
        xT = [S.pair(sb, f"xT{par}", [P, KD, GROUP], F32R) for par in range(2)]
        qb = S.pair(sb, "qb", [P, GROUP])
        qs = S.pair(sb, "qs", [P, GROUP])
        qc = S.pair(sb, "qc", [P, GROUP])
        qh = S.pair(sb, "qh", [P, GROUP], F32R)
        ql = S.pair(sb, "ql", [P, GROUP], F32R)
        v = S.pair(sb, "v", [P, NH, 2 * HD])
        tp = S.pair(ps, "tp", [P, KD, P])
        pp = S.pair(ps, "pp", [P, GROUP])
        vp = S.pair(ps, "vp", [P, D])

        s_const = sem("s_const")
        s_wraw = sem("s_wraw")
        s_w = sem("s_w")
        s_memset = sem("s_memset")
        s_x = S.pair(sem, "s_x")
        s_xn_in = sem("s_xn_in")
        s_meta = S.pair(sem, "s_meta")
        s_yg = moved[0]
        s_half = sem("s_half")
        s_x1 = sem("s_x1")
        s_x1_stored = S.pair(sem, "s_x1_stored")
        s_stats = sem("s_stats")
        s_mv = sem("s_mv")
        s_std = sem("s_std")
        s_rstd = sem("s_rstd")
        s_xa = sem("s_xa")
        s_tp = sem("s_tp")
        s_xh = sem("s_xh")
        s_xl = sem("s_xl")
        s_pp = sem("s_pp")
        s_qb = sem("s_qb")
        s_qs = sem("s_qs")
        s_qc = sem("s_qc")
        s_rot = sem("s_rot")
        s_qh = sem("s_qh")
        s_ql = sem("s_ql")
        s_q_stored = S.pair(sem, "s_q_stored")
        s_vp = sem("s_vp")
        s_v = sem("s_v")
        s_v_stored = S.pair(sem, "s_v_stored")
        block = S.block()
        met = (s_const, 96)
        NQ = 2 * KD
        SWAP = [(d + HD // 2) % HD for d in range(HD)]

        def rows(ap, i, par):
            return tiles(ap[bass.ds((2 * i + par) * GROUP, GROUP), :])

        def meta(ap, i, par):
            return ap[bass.ds(2 * i + par, 1), :, :].rearrange("o p j -> (o p) j")

        @block.sync
        def _(sp):
            for dst, src in ((ident, cst["ident"]), (cos, cst["cos"]), (sin, cst["sin"])):
                sp.dma_start(dst[:, :], src).then_inc(s_const, 16)
            for m in range(2):
                sp.dma_start(bqk[m][:, :], bias[m]).then_inc(s_const, 16)
            sp.dma_start(bv[:, :], bias[2].rearrange("(o n) -> o n", o=1).broadcast_to([P, D])).then_inc(s_const, 16)

            def load(i, par):
                r = 2 * i + par
                work_out(sp, 16 * TJ * (r - 1))
                sp.wait_ge(*met)
                sp.wait_ge(s_yg, past(16 * TJ * (r - 1)))
                sp.wait_ge(s_x1, past(TJ * (r - 1)))
                sp.dma_start(slot[par][:, :], meta(slot_in, i, par)).then_inc(s_meta[par], 16)
                sp.dma_start(gateh[par][:, :], meta(gate_in, i, par)).then_inc(s_meta[par], 16)
                sp.wait_ge(s_x1_stored[par], 16 * i)
                sp.wait_ge(s_xa, past(TJ * (r - 1)))
                sp.dma_start(x[par][:, :, :], rows(x_in, i, par)).then_inc(s_x[par], 16)
                sp.wait_ge(s_half, r)
                sp.dma_start(xn[:, :, :], rows(xn_in, i, par)).then_inc(s_xn_in, 16)

            load(0, 0)
            for m in range(3):
                sp.wait_ge(s_w, 2 * m)
                sp.dma_start(wraw[:, :, :], wT[m].rearrange("(k p) n -> p k n", p=P)).then_inc(s_wraw, 16)

            def step(i, par, nxt):
                r = 2 * i + par
                if nxt:
                    load(*nxt)
                sp.wait_ge(s_x1, TJ * (r + 1))
                sp.dma_start(rows(x_out, i, par), x[par][:, :, :]).then_inc(s_x1_stored[par], 16)

            rounds_ahead(sp, NG, step)
            for par in range(2):
                sp.wait_ge(s_x1_stored[par], 16 * (NG // 2))

        @block.gpsimd
        def _(pool):
            nc.gpsimd.memset(eps[:, :], EPS).then_inc(s_memset, 1)
            for b in range(2):
                nc.gpsimd.memset(v[b][:, :, HD:2 * HD], 1.0).then_inc(s_memset, 1)

            def gather(i, par):
                r = 2 * i + par
                work_out(pool, 32 * (i + 1), TJ * r)
                pool.wait_ge(*met)
                pool.wait_ge(s_meta[par], 32 * (i + 1))
                pool.wait_ge(s_x1, TJ * r)
                for j in range(TJ):
                    nc.gpsimd.indirect_dma_start(
                        out=yg[:, j, :], out_offset=None, in_=y,
                        in_offset=bass.IndirectOffsetOnAxis(ap=slot[par][:, j:j + 1], axis=0),
                        bounds_check=NOSLOT, oob_is_err=False).then_inc(s_yg, 16)

            def turn(i, par):
                for t in range(NQ):
                    n = NQ * (2 * i + par) + t
                    pool.wait_ge(s_qb, n + 1)
                    pool.wait_ge(s_ql, past(n - 1))
                    nc.gpsimd.tensor_tensor(out=qc[t % 2][:, :], in0=qb[t % 2][:, :],
                                            in1=cos[:, par * GROUP:(par + 1) * GROUP], op=ALU.mult).then_inc(s_qc, 1)
                    pool.wait_ge(s_qs, n + 1)
                    nc.gpsimd.tensor_tensor(out=qs[t % 2][:, :], in0=qs[t % 2][:, :],
                                            in1=sin[:, par * GROUP:(par + 1) * GROUP], op=ALU.mult).then_inc(s_qc, 1)

            def step(i, par, nxt):
                if nxt:
                    gather(*nxt)
                turn(i, par)

            pool.wait_ge(s_const, 96)
            gather(0, 0)
            rounds_ahead(pool, NG, step)

        @block.scalar
        def _(act):
            act.wait_ge(s_memset, 3)
            act.wait_ge(s_const, 96)
            for m in range(3):
                act.wait_ge(s_wraw, 16 * (m + 1))
                nc.scalar.activation(w[m][0][:, :, :], wraw[:, :, :], ACT.Copy).then_inc(s_w, 1)
                act.wait_ge(s_w, 2 * m + 2)

            def norm(i, par):
                r = 2 * i + par
                act.wait_ge(s_mv, TJ * (r + 1))
                nc.scalar.activation(std[:, :], mv[:, :, 1], ACT.Sqrt, bias=eps[:, 0:1]).then_inc(s_std, 1)

            def hi_x(i, par, j):
                n = TJ * (2 * i + par) + j
                act.wait_ge(s_tp, n + 1)
                act.wait_ge(s_vp, past(TJ * (2 * i + par - 1)))
                nc.scalar.activation(xT[par][0][:, :, j * P:(j + 1) * P], tp[j % 2][:, :, :],
                                     ACT.Copy).then_inc(s_xh, 1)

            def copy_q(i, par, t):
                n = NQ * (2 * i + par) + t
                act.wait_ge(s_pp, n + 1)
                act.wait_ge(s_qc, past(2 * (n - 1)))
                nc.scalar.activation(qb[t % 2][:, :], pp[t % 2][:, :], ACT.Identity,
                                     bias=bqk[t // KD][:, t % KD:t % KD + 1]).then_inc(s_qb, 1)

            def store_q(i, par, t):
                r = 2 * i + par
                n = NQ * r + t
                act.wait_ge(s_ql, n + 1)
                out = (q_out, k_out)[t // KD]
                h0 = (t % KD) * P
                for part, s in ((0, qh), (1, ql)):
                    act.dma_start(out[part, bass.ds(i, 1), h0:h0 + P, par * GROUP:(par + 1) * GROUP].rearrange(
                        "o d q -> (o d) q"), s[t % 2][:, :].bitcast(F32)).then_inc(s_q_stored[t % 2], 16)

            def store_v(i, par, j):
                r = 2 * i + par
                n = TJ * r + j
                act.wait_ge(s_v, n + 1)
                act.dma_start(v_out[bass.ds(i, 1), :, par * GROUP + j * P:par * GROUP + (j + 1) * P, :].rearrange(
                    "o g t c -> t (o g) c"), v[j % 2][:, :, :].rearrange("p (g h) c -> p g (h c)", h=2)).then_inc(
                        s_v_stored[j % 2], 16)

            def step(i, par, nxt):
                copy_q(i, par, 0)
                for t in range(NQ):
                    if t + 1 < NQ:
                        copy_q(i, par, t + 1)
                    store_q(i, par, t)
                    if nxt and t == 3:
                        norm(*nxt)
                    if nxt and t >= 4:
                        hi_x(*nxt, t - 4)
                for j in range(TJ):
                    store_v(i, par, j)

            norm(0, 0)
            for j in range(TJ):
                hi_x(0, 0, j)
            rounds_ahead(act, NG, step)
            for b in range(2):
                act.wait_ge(s_q_stored[b], 32 * NG * NQ // 2)
                act.wait_ge(s_v_stored[b], 16 * NG * TJ // 2)

        @block.vector
        def _(dve):
            dve.wait_ge(s_const, 96)
            dve.wait_ge(s_memset, 3)
            for m in range(3):
                dve.wait_ge(s_w, 2 * m + 1)
                nc.vector.tensor_tensor(out=w[m][1][:, :, :], in0=wraw[:, :, :], in1=w[m][0][:, :, :].bitcast(F32),
                                        op=ALU.subtract).then_inc(s_w, 1)

            def combine(i, par):
                r = 2 * i + par
                dve.wait_ge(s_x[par], 16 * (i + 1))
                dve.wait_ge(s_xn_in, 16 * (r + 1))
                nc.vector.scalar_tensor_tensor(x[par][:, :, :].rearrange("p j n -> p (j n)"),
                                               xn[:, :, :].rearrange("p j n -> p (j n)"), 0.5,
                                               x[par][:, :, :].rearrange("p j n -> p (j n)"),
                                               ALU.mult, ALU.add).then_inc(s_half, 1)
                dve.wait_ge(s_half, r + 1)
                dve.wait_ge(s_yg, 16 * TJ * (r + 1))
                dve.wait_ge(s_meta[par], 32 * (i + 1))
                for j in range(TJ):
                    n = TJ * r + j
                    nc.vector.scalar_tensor_tensor(x[par][:, j, :], yg[:, j, :], gateh[par][:, j:j + 1],
                                                   x[par][:, j, :], ALU.mult, ALU.add).then_inc(s_x1, 1)
                    dve.wait_ge(s_x1, n + 1)
                    dve.wait_ge(s_mv, past(n - 1))
                    nc.vector.bn_stats(stats[j % 2][:, :], x[par][:, j, :]).then_inc(s_stats, 1)
                    work_out(dve, n + 1, r, TJ * r)
                    dve.wait_ge(*met)
                    dve.wait_ge(s_stats, n + 1)
                    dve.wait_ge(s_std, r)
                    dve.wait_ge(s_xa, TJ * r)
                    nc.vector.bn_aggr(mv[:, j, :], stats[j % 2][:, :]).then_inc(s_mv, 1)

            def normalise(i, par):
                r = 2 * i + par
                dve.wait_ge(s_std, r + 1)
                dve.wait_ge(s_mv, TJ * (r + 1))
                nc.vector.reciprocal(rstd[:, :], std[:, :]).then_inc(s_rstd, 1)
                dve.wait_ge(s_rstd, r + 1)
                dve.wait_ge(s_tp, TJ * r)
                for j in range(TJ):
                    nc.vector.tensor_scalar(xa[:, j, :], x[par][:, j, :], mv[:, j, 0:1], rstd[:, j:j + 1],
                                            ALU.subtract, ALU.mult).then_inc(s_xa, 1)

            def lo_x(i, par, j):
                n = TJ * (2 * i + par) + j
                dve.wait_ge(s_xh, n + 1)
                nc.vector.tensor_tensor(out=xT[par][1][:, :, j * P:(j + 1) * P], in0=tp[j % 2][:, :, :],
                                        in1=xT[par][0][:, :, j * P:(j + 1) * P].bitcast(F32),
                                        op=ALU.subtract).then_inc(s_xl, 1)

            def swap(i, par, t):
                n = NQ * (2 * i + par) + t
                work_out(dve, n + 1, n - 1)
                dve.wait_ge(*met)
                dve.wait_ge(s_qb, n + 1)
                dve.wait_ge(s_rot, past(n - 1))
                nc.vector.stream_shuffle(qs[t % 2][:, :], qb[t % 2][:, :], SWAP).then_inc(s_qs, 1)

            def rotate(i, par, t):
                n = NQ * (2 * i + par) + t
                dve.wait_ge(s_qc, 2 * (n + 1))
                uses = (NQ // 2) * (2 * i + par) + t // 2
                dve.wait_ge(s_q_stored[t % 2], 32 * uses)
                nc.vector.tensor_tensor(out=qc[t % 2][:, :], in0=qc[t % 2][:, :], in1=qs[t % 2][:, :],
                                        op=ALU.add).then_inc(s_rot, 1)
                dve.wait_ge(s_rot, n + 1)
                nc.vector.tensor_copy(qh[t % 2][:, :], qc[t % 2][:, :]).then_inc(s_qh, 1)
                dve.wait_ge(s_qh, n + 1)
                nc.vector.tensor_tensor(out=ql[t % 2][:, :], in0=qc[t % 2][:, :], in1=qh[t % 2][:, :].bitcast(F32),
                                        op=ALU.subtract).then_inc(s_ql, 1)
                dve.wait_ge(s_ql, n + 1)

            def copy_v(i, par, j):
                n = TJ * (2 * i + par) + j
                dve.wait_ge(s_vp, n + 1)
                dve.wait_ge(s_v_stored[j % 2], 16 * ((TJ // 2) * (2 * i + par) + j // 2))
                nc.vector.tensor_tensor(out=v[j % 2][:, :, 0:HD],
                                        in0=vp[j % 2][:, :].rearrange("p (h d) -> p h d", h=NH),
                                        in1=bv[:, :].rearrange("p (h d) -> p h d", h=NH), op=ALU.add).then_inc(s_v, 1)

            def step(i, par, nxt):
                swap(i, par, 0)
                for t in range(NQ):
                    if t + 1 < NQ:
                        swap(i, par, t + 1)
                    rotate(i, par, t)
                    if nxt and t == 2:
                        combine(*nxt)
                    if nxt and t == 3:
                        normalise(*nxt)
                    if nxt and t >= 4:
                        lo_x(*nxt, t - 4)
                for j in range(TJ):
                    copy_v(i, par, j)

            combine(0, 0)
            normalise(0, 0)
            for j in range(TJ):
                lo_x(0, 0, j)
            rounds_ahead(dve, NG, step)

        @block.tensor
        def _(pe):
            pe.wait_ge(s_const, 96)
            pe.wait_ge(s_w, 6)

            def turn(i, par, j):
                n = TJ * (2 * i + par) + j
                pe.wait_ge(s_xa, n + 1)
                pe.wait_ge(s_xl, past(n - 1))
                for k in range(KD):
                    last = nc.tensor.transpose(tp[j % 2][:, k, :], xa[:, j, k * P:(k + 1) * P], ident[:, :])
                last.then_inc(s_tp, 1)

            def project(i, par, t):
                n = NQ * (2 * i + par) + t
                pe.wait_ge(s_qb, past(n - 1))
                m, c = t // KD, t % KD
                for k in range(KD):
                    last = matmul3(nc, pp[t % 2][:, :], [s[:, k, c * P:(c + 1) * P] for s in w[m]],
                                   [s[:, k, :] for s in xT[par]], k == 0, k == KD - 1)
                last.then_inc(s_pp, 1)

            def values(i, par, j):
                n = TJ * (2 * i + par) + j
                pe.wait_ge(s_v, past(n - 1))
                for k in range(KD):
                    last = matmul3(nc, vp[j % 2][:, :], [s[:, k, j * P:(j + 1) * P] for s in xT[par]],
                                   [s[:, k, :] for s in w[2]], k == 0, k == KD - 1)
                last.then_inc(s_vp, 1)

            def step(i, par, nxt):
                r = 2 * i + par
                pe.wait_ge(s_xl, TJ * (r + 1))
                for t in range(NQ):
                    project(i, par, t)
                    if nxt and t >= 4:
                        turn(*nxt, t - 4)
                for j in range(TJ):
                    values(i, par, j)

            for j in range(TJ):
                turn(0, 0, j)
            rounds_ahead(pe, NG, step)


def attention(nc, name, q_in, k_in, v_in, cst, num_out, den_out):
    S = Space(nc, name)
    sb, ps, sem = S.sb, S.ps, S.sem
    NP = B * NH // 2
    KT = L // P
    HALF = L // 2
    SCALE = 1.0 / float(HD) ** 0.5
    MAXES = [(), (0, 1, 2), (3, 4, 5), (6, 7, 8), (9, 10, 11), (12, 13), (14, 15), ()]
    with S.ctx:
        ident = sb("ident", [P, P])
        identb = sb("identb", [P, P], BF16)
        qst = [S.pair(sb, f"q{h}", [P, L], F32R) for h in range(2)]
        kst = [S.pair(sb, f"k{h}", [P, L], F32R) for h in range(2)]
        v = S.pair(sb, "v", [P, KT, 2, 2 * HD])
        pr = [S.pair(sb, f"p{h}", [P, L]) for h in range(2)]
        big = [sb(f"big{h}", [P, KT]) for h in range(2)]
        parts = [sb(f"parts{h}", [P, KT, HD], BF16) for h in range(2)]
        o = S.pair(sb, "o", [P, L])
        st = [ps(f"st{h}", [P, L]) for h in range(2)]
        mx = ps("mx", [P, L])
        op = ps("op", [P, L])

        s_const = sem("s_const")
        s_memset = sem("s_memset")
        s_identb = sem("s_identb")
        s_in = S.pair(sem, "s_in")
        s_mx = sem("s_mx")
        s_max = sem("s_max")
        s_mhi = sem("s_mhi")
        s_mlo = sem("s_mlo")
        s_row = sem("s_row")
        s_rowq0 = sem("s_rowq0")
        s_rowq1 = sem("s_rowq1")
        s_st = [sem(f"s_st{h}") for h in range(2)]
        s_exp = [sem(f"s_exp{h}") for h in range(2)]
        s_pv = sem("s_pv")
        s_o = sem("s_o")
        s_o_stored = S.pair(sem, "s_o_stored")
        block = S.block()
        N_IN = 2 * 6 + 1

        @block.sync
        def _(sp):
            sp.dma_start(ident[:, :], cst["ident"]).then_inc(s_const, 16)
            sp.wait_ge(s_memset, 6)

            def load(pi, par):
                p = 2 * pi + par
                for h in range(2):
                    sp.wait_ge(s_st[h], past(KT * (p - 1)))
                for h in range(2):
                    row = p * (2 * HD) + h * HD
                    for blk, (qp, kp) in enumerate(((0, 0), (0, 1), (1, 0))):
                        for dst, src, part in ((qst, q_in, qp), (kst, k_in, kp)):
                            sp.dma_start(dst[h][par][blk * HD:(blk + 1) * HD, :].bitcast(F32),
                                         src[part, bass.ds(row, HD), :]).then_inc(s_in[par], 16)
                sp.wait_ge(s_pv, past(KT * (p - 1)))
                sp.dma_start(v[par][:, :, :, :].rearrange("p t h c -> p t (h c)"), v_in[bass.ds(p, 1), :, :].rearrange(
                    "o (t p) c -> p (o t) c", p=P)).then_inc(s_in[par], 16)

            def store(pi, par):
                p = 2 * pi + par
                sp.wait_ge(s_o, p + 1)
                for h in range(2):
                    row = p * (2 * HD) + h * HD
                    sp.dma_start(num_out[bass.ds(row, HD), :], o[par][2 * h * HD:(2 * h + 1) * HD, :]).then_inc(
                        s_o_stored[par], 16)
                    sp.dma_start(den_out[bass.ds(row, HD), :], o[par][(2 * h + 1) * HD:(2 * h + 2) * HD, :]).then_inc(
                        s_o_stored[par], 16)

            def step(i, par, nxt):
                if nxt:
                    load(*nxt)
                store(i, par)

            load(0, 0)
            rounds_ahead(sp, NP, step)
            for par in range(2):
                sp.wait_ge(s_o_stored[par], 64 * (NP // 2))

        @block.gpsimd
        def _(pool):
            for h in range(2):
                nc.gpsimd.memset(parts[h][:, :, :], 0.0).then_inc(s_memset, 1)
            pool.wait_ge(s_memset, 2)
            for h in range(2):
                for par in range(2):
                    nc.gpsimd.memset(kst[h][par][3 * HD:4 * HD, :].bitcast(F32), -1.0).then_inc(s_memset, 1)

        @block.scalar
        def _(act):
            def exps(p, kt, h):
                n = KT * p + kt
                act.wait_ge(s_st[h], n + 1)
                act.wait_ge(s_pv, past(n - 1))
                nc.scalar.activation(pr[h][kt % 2][:, :], st[h][:, :], ACT.Exp, scale=SCALE).then_inc(s_exp[h], 1)

            def step(i, par, nxt):
                p = 2 * i + par
                for kt in range(KT):
                    for h in range(2):
                        exps(p, kt, h)
                if nxt:
                    act.wait_ge(s_row, 1 * (2 * nxt[0] + nxt[1]) + 1)
                    nc.scalar.activation(qst[1][nxt[1]][3 * HD:4 * HD, :], mx[2 * HD:3 * HD, :],
                                         ACT.Copy).then_inc(s_rowq1, 1)
                act.wait_ge(s_pv, KT * (p + 1))
                act.wait_ge(s_o_stored[par], 64 * i)
                nc.scalar.activation(o[par][:, :], op[:, :], ACT.Copy).then_inc(s_o, 1)

            act.wait_ge(s_row, 1)
            nc.scalar.activation(qst[1][0][3 * HD:4 * HD, :], mx[2 * HD:3 * HD, :], ACT.Copy).then_inc(s_rowq1, 1)
            rounds_ahead(act, NP, step)

        @block.vector
        def _(dve):
            dve.wait_ge(s_const, 16)
            dve.wait_ge(s_memset, 6)
            nc.vector.tensor_copy(identb[:, :], ident[:, :]).then_inc(s_identb, 1)

            def maxima(pi, par):
                p = 2 * pi + par
                for n in range(2 * KT):
                    h, qt = n // KT, n % KT
                    dve.wait_ge(s_mx, 2 * KT * p + n + 1)
                    nc.vector.tensor_reduce(out=big[h][:, qt:qt + 1], in_=mx[:, :], axis=AX.X,
                                            op=ALU.max).then_inc(s_max, 1)
                dve.wait_ge(s_max, 2 * KT * (p + 1))
                for h in range(2):
                    nc.vector.tensor_copy(parts[h][:, :, 0], big[h][:, :]).then_inc(s_mhi, 1)
                dve.wait_ge(s_mhi, 2 * p + 2)
                for h in range(2):
                    nc.vector.tensor_tensor(out=parts[h][:, :, 1], in0=big[h][:, :], in1=parts[h][:, :, 0],
                                            op=ALU.subtract).then_inc(s_mlo, 1)
                dve.wait_ge(s_row, p + 1)
                nc.vector.tensor_copy(qst[0][par][3 * HD:4 * HD, :], mx[3 * HD:4 * HD, :]).then_inc(s_rowq0, 1)

            maxima(0, 0)

            def step(i, par, nxt):
                if nxt:
                    maxima(*nxt)

            rounds_ahead(dve, NP, step)

        @block.tensor
        def _(pe):
            pe.wait_ge(s_const, 16)
            pe.wait_ge(s_memset, 6)
            pe.wait_ge(s_identb, 1)

            def rough(pi, par, n):
                p = 2 * pi + par
                h, qt = n // KT, n % KT
                if n == 0:
                    pe.wait_ge(s_in[par], 16 * N_IN * (pi + 1))
                    pe.wait_ge(s_rowq0, p)
                    pe.wait_ge(s_rowq1, p)
                pe.wait_ge(s_max, 2 * KT * p + n)
                for c in range(2):
                    last = nc.tensor.matmul(mx[:, c * HALF:(c + 1) * HALF],
                                            qst[h][par][0:3 * HD, qt * P:(qt + 1) * P],
                                            kst[h][par][0:3 * HD, c * HALF:(c + 1) * HALF], start=True, stop=True)
                last.then_inc(s_mx, 1)

            def row(pi, par):
                p = 2 * pi + par
                pe.wait_ge(s_max, 2 * KT * (p + 1))
                pe.wait_ge(s_mlo, 2 * (p + 1))
                for h in range(2):
                    out = mx[(3 - h) * HD:(4 - h) * HD, :]
                    for qt in range(KT):
                        last = nc.tensor.matmul(out[:, qt * P:(qt + 1) * P], parts[h][:, qt, :], identb[:, :],
                                                start=True, stop=True)
                last.then_inc(s_row, 1)

            def scores(p, par, kt, h):
                n = KT * p + kt
                if kt == 0:
                    pe.wait_ge((s_rowq0, s_rowq1)[h], p + 1)
                pe.wait_ge(s_exp[h], n)
                for c in range(2):
                    last = nc.tensor.matmul(st[h][:, c * HALF:(c + 1) * HALF],
                                            kst[h][par][:, kt * P:(kt + 1) * P],
                                            qst[h][par][:, c * HALF:(c + 1) * HALF], start=True, stop=True)
                last.then_inc(s_st[h], 1)

            def products(p, par, kt):
                for h in range(2):
                    pe.wait_ge(s_exp[h], KT * p + kt + 1)
                if kt == 0:
                    pe.wait_ge(s_o, p)
                for c in range(2):
                    for h in range(2):
                        last = nc.tensor.matmul(op[2 * h * HD:2 * (h + 1) * HD, c * HALF:(c + 1) * HALF],
                                                v[par][:, kt, h, :], pr[h][kt % 2][:, c * HALF:(c + 1) * HALF],
                                                start=kt == 0, stop=kt == KT - 1)
                last.then_inc(s_pv, 1)

            for n in range(2 * KT):
                rough(0, 0, n)
            row(0, 0)

            def step(i, par, nxt):
                p = 2 * i + par
                for kt in range(KT):
                    for h in range(2):
                        scores(p, par, kt, h)
                    if nxt:
                        for n in MAXES[kt]:
                            rough(*nxt, n)
                        if kt == KT - 1:
                            row(*nxt)
                    if kt:
                        products(p, par, kt - 1)
                products(p, par, KT - 1)

            rounds_ahead(pe, NP, step)


def combine(nc, name, moved, x_in, xn_in, y, slot_in, gate_in, x_out):
    S = Space(nc, name)
    sb, sem = S.sb, S.sem
    with S.ctx:
        x = S.pair(sb, "x", [P, TJ, D])
        xn = S.pair(sb, "xn", [P, TJ, D])
        yg = S.pair(sb, "yg", [P, TJ, D])
        slot = S.pair(sb, "slot", [P, TJ], I32)
        gateh = S.pair(sb, "gateh", [P, TJ])
        s_meta = S.pair(sem, "s_meta")
        s_x = S.pair(sem, "s_x")
        s_yg = moved
        s_half = sem("s_half")
        s_x3 = sem("s_x3")
        s_stored = S.pair(sem, "s_stored")
        block = S.block()
        met = (s_meta[0], 32)

        def rows(ap, i, par):
            return tiles(ap[bass.ds((2 * i + par) * GROUP, GROUP), :])

        def meta(ap, i, par):
            return ap[bass.ds(2 * i + par, 1), :, :].rearrange("o p j -> (o p) j")

        @block.sync
        def _(sp):
            def load(i, par):
                work_out(sp, TJ * (2 * i + par - 1))
                if not isinstance(i, int):
                    sp.wait_ge(*met)
                sp.wait_ge(s_x3, past(TJ * (2 * i + par - 1)))
                sp.wait_ge(s_stored[par], 16 * i)
                sp.dma_start(slot[par][:, :], meta(slot_in, i, par)).then_inc(s_meta[par], 16)
                sp.dma_start(gateh[par][:, :], meta(gate_in, i, par)).then_inc(s_meta[par], 16)
                sp.dma_start(x[par][:, :, :], rows(x_in, i, par)).then_inc(s_x[par], 16)
                sp.dma_start(xn[par][:, :, :], rows(xn_in, i, par)).then_inc(s_x[par], 16)

            rounds(sp, NG, load)

        @block.gpsimd
        def _(pool):
            def gather(i, par):
                work_out(pool, 32 * (i + 1), TJ * (2 * i + par - 1))
                pool.wait_ge(*met)
                pool.wait_ge(s_meta[par], 32 * (i + 1))
                pool.wait_ge(s_x3, past(TJ * (2 * i + par - 1)))
                for j in range(TJ):
                    nc.gpsimd.indirect_dma_start(
                        out=yg[par][:, j, :], out_offset=None, in_=y,
                        in_offset=bass.IndirectOffsetOnAxis(ap=slot[par][:, j:j + 1], axis=0),
                        bounds_check=NOSLOT, oob_is_err=False).then_inc(s_yg[par], 16)

            rounds(pool, NG, gather)

        @block.vector
        def _(dve):
            def add(i, par):
                r = 2 * i + par
                dve.wait_ge(s_x[par], 32 * (i + 1))
                flat = x[par][:, :, :].rearrange("p j n -> p (j n)")
                nc.vector.scalar_tensor_tensor(flat, xn[par][:, :, :].rearrange("p j n -> p (j n)"), 0.5, flat,
                                               ALU.mult, ALU.add).then_inc(s_half, 1)
                dve.wait_ge(s_half, r + 1)
                dve.wait_ge(s_yg[par], 16 * TJ * (i + 1))
                for j in range(TJ):
                    nc.vector.scalar_tensor_tensor(x[par][:, j, :], yg[par][:, j, :], gateh[par][:, j:j + 1],
                                                   x[par][:, j, :], ALU.mult, ALU.add).then_inc(s_x3, 1)

            rounds(dve, NG, add)

        @block.scalar
        def _(act):
            def store(i, par):
                act.wait_ge(s_x3, TJ * (2 * i + par + 1))
                act.dma_start(rows(x_out, i, par), x[par][:, :, :]).then_inc(s_stored[par], 16)

            rounds(act, NG, store)
            for par in range(2):
                act.wait_ge(s_stored[par], 16 * (NG // 2))


def macaron(nc, x, wq, bq, wk, bk, wv, bv, wo, bo, w_router, w_gate, w_up, w_down,
            c_ident, c_tri, c_iota, c_tok, c_cos, c_sin, out):
    cst = {"ident": c_ident, "tri": c_tri, "iota": c_iota, "tok": c_tok, "cos": c_cos, "sin": c_sin}

    def dram(name, shape, dt=F32):
        return nc.dram_tensor(name, shape, dt, kind="Internal").ap()

    xn = [dram(f"xn{n}", [T + 1, D]) for n in range(2)]
    table = [dram(f"table{n}", [NOSLOT, 1], I32) for n in range(2)]
    y = [dram(f"y{n}", [NOSLOT + 1, D]) for n in range(2)]
    slot = [dram(f"slot{n}", [NG, P, TJ], I32) for n in range(2)]
    gate = [dram(f"gate{n}", [NG, P, TJ]) for n in range(2)]
    x1 = dram("x1", [T, D])
    x2 = dram("x2", [T, D])
    q = dram("q", [2, B, D, L])
    k = dram("k", [2, B, D, L])
    v = dram("v", [B, NH // 2, L, 4 * HD])
    num = dram("num", [B, D, L])
    den = dram("den", [B, D, L])

    def by_row(ap):
        return ap.rearrange("b d q -> (b d) q")

    moved = {n: [nc.alloc_semaphore(name=f"{n}_moved_{par}") for par in range(2)]
             for n in ("r1", "e1", "qkv", "r2", "e2", "c2")}
    route(nc, "r1", moved["r1"], x, w_router, cst, xn[0], table[0], y[0][NOSLOT:NOSLOT + 1, :], slot[0], gate[0])
    experts(nc, "e1", moved["e1"], xn[0], table[0], w_gate, w_up, w_down, cst, y[0])
    qkv(nc, "qkv", moved["qkv"], x, xn[0], y[0], slot[0], gate[0], (wq, wk, wv), (bq, bk, bv), cst, x1, q, k, v)
    attention(nc, "att", q.rearrange("s b d q -> s (b d) q"), k.rearrange("s b d q -> s (b d) q"),
              v.rearrange("b g t c -> (b g) t c"), cst, by_row(num), by_row(den))
    route(nc, "r2", moved["r2"], x1, w_router, cst, xn[1], table[1], y[1][NOSLOT:NOSLOT + 1, :], slot[1], gate[1],
          attn=(num, den, wo, bo, x2))
    experts(nc, "e2", moved["e2"], xn[1], table[1], w_gate, w_up, w_down, cst, y[1])
    combine(nc, "c2", moved["c2"], x2, xn[1], y[1], slot[1], gate[1], out)


def constants(np):
    inv = (np.float32(1.0) / np.float32(10000.0) ** (np.arange(0, HD, 2, dtype=np.float32) / np.float32(HD))).astype(np.float32)
    angle = np.arange(L, dtype=np.float32)[None, :] * np.tile(inv, 2 * P // HD)[:, None]
    sign = np.where(np.arange(P) % HD < HD // 2, np.float32(-1.0), np.float32(1.0))[:, None]
    t = np.arange(P)
    return {
        "c_ident": np.eye(P, dtype=np.float32),
        "c_tri": (t[:, None] <= t[None, :]).astype(np.float32),
        "c_iota": np.tile(np.arange(E, dtype=np.float32), (P, 1)),
        "c_tok": (t[:, None] + P * np.arange(TJ)[None, :]).astype(np.float32),
        "c_cos": np.cos(angle).astype(np.float32),
        "c_sin": (sign * np.sin(angle)).astype(np.float32),
    }


def kernel(**inputs):
    import numpy as np
    import concourse.bacc as bacc
    from concourse.bass_utils import run_bass_kernel_spmd

    def w(name, turned=False):
        a = inputs[name]
        return np.ascontiguousarray(np.asarray(a).T if turned else np.asarray(a))

    def by_tile(name):
        return np.ascontiguousarray(np.asarray(inputs[name]).reshape(KD, P).T)

    arrays = {
        "x": w("L0_attn_x").reshape(T, D),
        "wq": w("L0_attn_Wq", True), "bq": by_tile("L0_attn_bq"),
        "wk": w("L0_attn_Wk", True), "bk": by_tile("L0_attn_bk"),
        "wv": w("L0_attn_Wv", True), "bv": w("L0_attn_bv"),
        "wo": w("L0_attn_Wo", True), "bo": w("L0_attn_bo"),
        "w_router": w("L0_ffn_w_router"), "w_gate": w("L0_ffn_w_gate"),
        "w_up": w("L0_ffn_w_up"), "w_down": w("L0_ffn_w_down"),
        **constants(np),
    }
    nc = bacc.Bacc("TRN2", target_bir_lowering=False, num_devices=1)
    aps = {n: nc.dram_tensor(f"in_{n}", a.shape, mybir.dt.from_np(a.dtype), kind="ExternalInput").ap()
           for n, a in arrays.items()}
    out = nc.dram_tensor("out", (T, D), F32, kind="ExternalOutput").ap()
    macaron(nc, **aps, out=out)
    r = run_bass_kernel_spmd(nc, [{f"in_{n}": a for n, a in arrays.items()}], core_ids=[0])
    return r.results[0]["out"].reshape(B, L, D)
```

```python
import concourse.bass as bass
from concourse import mybir
from contextlib import ExitStack

F32 = mybir.dt.float32
F32R = mybir.dt.float32r
BF16 = mybir.dt.bfloat16
I32 = mybir.dt.int32
U32 = mybir.dt.uint32
ALU = mybir.AluOpType
ACT = mybir.ActivationFunctionType
AX = mybir.AxisListType

P = 128
B, L, D = 8, 1024, 512
T = B * L
NH, HD = 16, 32
E, F = 32, 512
C = (5 * T + 4 * E - 1) // (4 * E)
CT = (C + P - 1) // P
CW = 4 * (-(-C // (4 * CT)))
CP = CT * CW
NOSLOT = E * CP
KD = D // P
KF = F // P
TJ = 4
GROUP = TJ * P
NG = T // GROUP
EPS = 1e-5
BANK = 512


def past(count):
    return max(count, 0) if isinstance(count, int) else count


def work_out(eng, *counts):
    for count in counts:
        if not isinstance(count, int):
            eng.compute_val(count)


def rounds(eng, n, body):
    assert n % 2 == 0 and n >= 4
    body(0, 0)
    body(0, 1)
    if n > 4:
        with eng.Fori(1, n // 2 - 1) as i:
            body(i, 0)
            body(i, 1)
    body(n // 2 - 1, 0)
    body(n // 2 - 1, 1)


def after_first(i, par):
    return not isinstance(i, int) or 2 * i + par > 0


def rounds_ahead(eng, n, body):
    def pair(i, more=True):
        body(i, 0, (i, 1), (i + 1, 0) if more else None)
        body(i, 1, (i + 1, 0) if more else None, (i + 1, 1) if more else None)
    pair(0)
    with eng.Fori(1, n // 2 - 1) as i:
        pair(i)
    pair(n // 2 - 1, False)


class Chain:
    def __init__(self, sem, steps):
        self.sem, self.steps = sem, steps

    def start(self, eng, r):
        self.eng, self.r, self.k = eng, r, 0

    def link(self, ins):
        ins.then_inc(self.sem, 1)
        self.k += 1
        self.eng.wait_ge(self.sem, self.r * self.steps + self.k)

    def end(self):
        assert self.k == self.steps, self.k


class Space:
    def __init__(self, nc, name):
        self.nc, self.name, self.ctx, self.sems = nc, name, ExitStack(), []

    def sb(self, name, shape, dt=F32):
        return self.ctx.enter_context(self.nc.sbuf_tensor(f"{self.name}_{name}", shape, dt))

    def ps(self, name, shape, dt=F32):
        return self.ctx.enter_context(self.nc.psum_tensor(f"{self.name}_{name}", shape, dt))

    def bank(self, name, n):
        return self.ps(name, [P, BANK])[:, 0:n]

    def sem(self, name):
        self.sems.append(self.ctx.enter_context(self.nc.semaphore(f"{self.name}_{name}")))
        return self.sems[-1]

    def pair(self, make, name, *a):
        return [make(f"{name}_{i}", *a) for i in range(2)]

    def clear(self):
        nums = sorted(s.num for s in self.sems)
        lo = nums[0]
        for a, b in zip(nums, nums[1:] + [None]):
            if b != a + 1:
                self.nc.all_engine_barrier(sems_to_clear=range(lo, a + 1))
                lo = b

    def block(self):
        self.ctx.callback(self.clear)
        return self.ctx.enter_context(self.nc.Block())


def matmul3(nc, out, lhs, rhs, start, stop):
    nc.tensor.matmul(out, lhs[0], rhs[0], start=start, stop=False)
    nc.tensor.matmul(out, lhs[0], rhs[1], start=False, stop=False)
    return nc.tensor.matmul(out, lhs[1], rhs[0], start=False, stop=stop)


def tiles(ap):
    return ap.rearrange("(j p) n -> p j n", p=P)


def route(nc, name, moved, x_in, wr, cst, xn_out, table, y_zero, slot_out, gate_out, attn=None):
    S = Space(nc, name)
    sb, ps, sem = S.sb, S.ps, S.sem
    with S.ctx:
        ident = sb("ident", [P, P])
        trif = sb("trif", [P, P])
        tri = sb("tri", [P, P], BF16)
        ones = sb("ones", [P, P], BF16)
        iota = sb("iota", [P, E])
        tokf = sb("tokf", [P, TJ])
        wr_sb = sb("wr", [P, KD, E])
        unset = sb("unset", [P, NOSLOT // P], I32)
        zrow = sb("zrow", [1, D])
        eps = sb("eps", [P, 1])
        run = sb("run", [P, E], BF16)
        x = S.pair(sb, "x", [P, TJ, D])
        xn = S.pair(sb, "xn", [P, TJ, D])
        xnT = S.pair(sb, "xnT", [P, KD, P])
        stats = S.pair(sb, "stats", [P, 6])
        mv = sb("mv", [P, TJ, 2])
        std = sb("std", [P, TJ])
        rstd = sb("rstd", [P, TJ])
        top = sb("top", [P, TJ, 8])
        topi = sb("topi", [P, TJ, 8], U32)
        shifted = sb("shifted", [P, TJ, E])
        ex = sb("ex", [P, TJ, E])
        den = sb("den", [P, TJ])
        gate = sb("gate", [P, TJ])
        idxf = sb("idxf", [P, TJ])
        onehot = sb("onehot", [P, TJ, E], BF16)
        picked = sb("picked", [P, TJ, E])
        pos = sb("pos", [P, TJ])
        ok = sb("ok", [P, TJ])
        slot = sb("slot", [P, TJ])
        slot2 = sb("slot2", [P, TJ])
        seen = sb("seen", [P, E])
        slot_i = S.pair(sb, "slot_i", [P, TJ], I32)
        tok_i = S.pair(sb, "tok_i", [P, TJ], I32)
        gateh = S.pair(sb, "gateh", [P, TJ])
        tp = S.pair(ps, "tp", [P, KD, P])
        logits = S.bank("logits", TJ * E).rearrange("p (j e) -> p j e", e=E)
        posp = S.bank("posp", TJ * E).rearrange("p (j e) -> p j e", e=E)

        s_const = sem("s_const")
        s_memset = sem("s_memset")
        s_setup = sem("s_setup")
        s_unset = sem("s_unset")
        s_x = S.pair(sem, "s_x")
        s_stats = sem("s_stats")
        s_mv = sem("s_mv")
        s_std = sem("s_std")
        s_rstd = sem("s_rstd")
        s_xn = sem("s_xn")
        s_xn_stored = S.pair(sem, "s_xn_stored")
        s_tp = sem("s_tp")
        s_xnT = sem("s_xnT")
        s_logits = sem("s_logits")
        s_top = sem("s_top")
        s_shifted = sem("s_shifted")
        s_exp = sem("s_exp")
        s_onehot = sem("s_onehot")
        s_pos = sem("s_pos")
        s_slots = sem("s_slots")
        s_run = sem("s_run")
        s_scat = moved
        s_meta = S.pair(sem, "s_meta")
        pick = Chain(sem("s_pick"), 4)
        place = Chain(sem("s_place"), 8)
        n_const = 6
        if attn:
            ao_in, sums_in, inverse, woT, bo, x_out = attn
            bo_sb = sb("bo", [P, D])
            wraw = sb("wraw", [P, KD, D])
            wo = S.pair(sb, "wo", [P, KD, D], F32R)
            sums = sb("sums", [B * NH, L])
            aof = S.pair(sb, "aof", [P, KD, GROUP])
            inv = S.pair(sb, "inv", [P, KD, GROUP])
            s_sums = sem("s_sums")
            s_inv = sem("s_inv")
            s_inv_stored = sem("s_inv_stored")
            s_ao = sem("s_ao")
            ao = [S.pair(sb, f"ao{par}", [P, KD, GROUP], F32R) for par in range(2)]
            op = [ps(f"op{j}", [P, D]) for j in range(TJ)]
            s_ao_in = S.pair(sem, "s_ao_in")
            s_ao_hi = sem("s_ao_hi")
            s_ao_lo = sem("s_ao_lo")
            s_wo = sem("s_wo")
            s_xb = sem("s_xb")
            s_op = sem("s_op")
            s_x2 = sem("s_x2")
            s_x2_stored = S.pair(sem, "s_x2_stored")
            n_const = 8
        block = S.block()
        met = (s_const, 16 * n_const)

        def x_ap(ap, i, par):
            return tiles(ap[bass.ds((2 * i + par) * GROUP, GROUP), :])

        def ao_ap(ap, i, par):
            return ap[bass.ds(i, 1), :, par * GROUP:(par + 1) * GROUP].rearrange(
                "o (k p) q -> p (o k) q", p=P)

        @block.sync
        def _(sp):
            sp.dma_start(ident[:, :], cst["ident"]).then_inc(s_const, 16)
            sp.dma_start(trif[:, :], cst["tri"]).then_inc(s_const, 16)
            sp.dma_start(iota[:, :], cst["iota"]).then_inc(s_const, 16)
            sp.dma_start(tokf[:, :], cst["tok"]).then_inc(s_const, 16)
            sp.dma_start(wr_sb[:, :, :], wr.rearrange("(k p) e -> p k e", p=P)).then_inc(s_const, 16)
            if attn:
                sp.dma_start(bo_sb[:, :], bo.rearrange("(o n) -> o n", o=1).broadcast_to([P, D])).then_inc(s_const, 16)
                sp.dma_start(wraw[:, :, :], woT.rearrange("(k p) n -> p k n", p=P)).then_inc(s_const, 16)
            sp.wait_ge(s_memset, 5)
            sp.dma_start(table[0:NOSLOT, :].rearrange("(p n) o -> p (n o)", p=P), unset[:, :]).then_inc(s_unset, 16)
            sp.dma_start(xn_out[T:T + 1, :], zrow[:, :]).then_inc(s_unset, 16)
            sp.dma_start(y_zero, zrow[:, :]).then_inc(s_const, 16)

            def load(i, par):
                if attn:
                    work_out(sp, 16 * i)
                    sp.wait_ge(*met)
                    sp.wait_ge(s_x2_stored[par], 16 * i)
                sp.wait_ge(s_xn, past(TJ * (2 * i + par - 1)))
                sp.dma_start(x[par][:, :, :], x_ap(x_in, i, par)).then_inc(s_x[par], 16)

            def load_ao(i, par):
                sp.wait_ge(s_ao_lo, past(2 * i + par - 1))
                sp.dma_start(aof[par][:, :, :], ao_ap(ao_in, i, par)).then_inc(s_ao_in[par], 16)
                for h in range(P // HD):
                    sp.dma_start(inv[par][h * HD:(h + 1) * HD, :, :],
                                 inverse[bass.ds(i, 1), :, h, :, par * GROUP:(par + 1) * GROUP].rearrange(
                                     "b k o q -> (b o) k q").broadcast_to([HD, KD, GROUP])).then_inc(s_ao_in[par], 16)

            def store(i, par):
                if attn:
                    sp.wait_ge(s_x2, TJ * (2 * i + par + 1))
                    sp.dma_start(x_ap(x_out, i, par), x[par][:, :, :]).then_inc(s_x2_stored[par], 16)
                sp.wait_ge(s_xn, TJ * (2 * i + par + 1))
                sp.dma_start(x_ap(xn_out, i, par), xn[par][:, :, :]).then_inc(s_xn_stored[par], 16)

            def meta(i, par):
                work_out(sp, 2 * i + par + 1)
                sp.wait_ge(*met)
                sp.wait_ge(s_slots, 2 * i + par + 1)
                sp.dma_start(slot_out[bass.ds(2 * i + par, 1), :, :].rearrange("o p j -> (o p) j"),
                             slot_i[par][:, :]).then_inc(s_meta[par], 16)
                sp.dma_start(gate_out[bass.ds(2 * i + par, 1), :, :].rearrange("o p j -> (o p) j"),
                             gateh[par][:, :]).then_inc(s_meta[par], 16)

            def step(i, par, nxt, far):
                if nxt:
                    load(*nxt)
                if attn and far:
                    load_ao(*far)
                store(i, par)
                meta(i, par)

            if attn:
                sp.dma_start(sums[:, :], sums_in).then_inc(s_sums, 16)
                sp.wait_ge(s_inv, 1)
                sp.dma_start(inverse.rearrange("b k h o q -> (b k h o) q"), sums[:, :]).then_inc(s_inv_stored, 16)
                sp.wait_ge(s_inv_stored, 16)
                load_ao(0, 0)
                load_ao(0, 1)
            load(0, 0)
            rounds_ahead(sp, NG, step)
            for par in range(2):
                sp.wait_ge(s_xn_stored[par], 16 * (NG // 2))
                sp.wait_ge(s_meta[par], 32 * (NG // 2))
                if attn:
                    sp.wait_ge(s_x2_stored[par], 16 * (NG // 2))
            sp.wait_ge(s_const, 16 * n_const)
            sp.wait_ge(s_unset, 32)

        @block.gpsimd
        def _(pool):
            nc.gpsimd.memset(ones[:, :], 1.0).then_inc(s_memset, 1)
            nc.gpsimd.memset(unset[:, :], T).then_inc(s_memset, 1)
            nc.gpsimd.memset(zrow[:, :], 0.0).then_inc(s_memset, 1)
            nc.gpsimd.memset(eps[:, :], EPS).then_inc(s_memset, 1)
            nc.gpsimd.memset(run[:, :], 0.0).then_inc(s_memset, 1)
            pool.wait_ge(s_unset, 32)

            def bias(i, par):
                pool.wait_ge(s_x[par], 16 * (i + 1))
                nc.gpsimd.tensor_tensor(out=x[par][:, :, :], in0=x[par][:, :, :],
                                        in1=bo_sb[:, :].unsqueeze(1).broadcast_to([P, TJ, D]),
                                        op=ALU.add).then_inc(s_xb, 1)

            def divide(i, par):
                pool.wait_ge(s_ao_in[par], 16 * (1 + P // HD) * (i + 1))
                nc.gpsimd.tensor_tensor(out=aof[par][:, :, :], in0=aof[par][:, :, :], in1=inv[par][:, :, :],
                                        op=ALU.mult).then_inc(s_ao, 1)

            def lo_ao(i, par):
                pool.wait_ge(s_ao_hi, 2 * i + par + 1)
                nc.gpsimd.tensor_tensor(out=ao[par][1][:, :, :], in0=aof[par][:, :, :],
                                        in1=ao[par][0][:, :, :].bitcast(F32), op=ALU.subtract).then_inc(s_ao_lo, 1)

            def scatter(i, par):
                work_out(pool, 2 * i + par + 1)
                pool.wait_ge(*met)
                pool.wait_ge(s_slots, 2 * i + par + 1)
                for j in range(TJ):
                    nc.gpsimd.indirect_dma_start(
                        out=table[0:NOSLOT, :], out_offset=bass.IndirectOffsetOnAxis(ap=slot_i[par][:, j:j + 1], axis=0),
                        in_=tok_i[par][:, j:j + 1], in_offset=None,
                        bounds_check=NOSLOT - 1, oob_is_err=False).then_inc(s_scat[par], 16)

            def step(i, par, nxt, far):
                if attn and nxt:
                    bias(*nxt)
                if attn and far:
                    divide(*far)
                scatter(i, par)
                if attn and far:
                    lo_ao(*far)

            if attn:
                pool.wait_ge(s_const, 16 * n_const)
                bias(0, 0)
                for par in range(2):
                    divide(0, par)
                    lo_ao(0, par)
            rounds_ahead(pool, NG, step)
            for par in range(2):
                pool.wait_ge(s_scat[par], 16 * TJ * (NG // 2))

        @block.scalar
        def _(act):
            act.wait_ge(s_memset, 5)

            def norm(i, par):
                r = 2 * i + par
                act.wait_ge(s_mv, TJ * (r + 1))
                nc.scalar.activation(std[:, :], mv[:, :, 1], ACT.Sqrt, bias=eps[:, 0:1]).then_inc(s_std, 1)

            def copies(i, par):
                for j in range(TJ):
                    n = TJ * (2 * i + par) + j
                    act.wait_ge(s_tp, n + 1)
                    act.wait_ge(s_logits, past(n - 1))
                    nc.scalar.activation(xnT[j % 2][:, :, :], tp[j % 2][:, :, :], ACT.Copy).then_inc(s_xnT, 1)

            def exps(i, par):
                r = 2 * i + par
                act.wait_ge(s_shifted, r + 1)
                act.wait_ge(pick.sem, pick.steps * r)
                nc.scalar.activation(ex[:, :, :], shifted[:, :, :], ACT.Exp).then_inc(s_exp, 1)

            def hi_ao(i, par):
                act.wait_ge(s_ao, 2 * i + par + 1)
                act.wait_ge(s_op, past(TJ * (2 * i + par - 1)))
                nc.scalar.activation(ao[par][0][:, :, :], aof[par][:, :, :], ACT.Copy).then_inc(s_ao_hi, 1)

            def step(i, par, nxt, far):
                exps(i, par)
                if attn and far:
                    hi_ao(*far)
                if nxt:
                    norm(*nxt)
                    copies(*nxt)

            if attn:
                hi_ao(0, 0)
                hi_ao(0, 1)
            norm(0, 0)
            copies(0, 0)
            rounds_ahead(act, NG, step)

        @block.vector
        def _(dve):
            dve.wait_ge(s_const, 16 * n_const)
            dve.wait_ge(s_memset, 5)
            nc.vector.tensor_copy(tri[:, :], trif[:, :]).then_inc(s_setup, 1)
            if attn:
                nc.vector.tensor_copy(wo[0][:, :, :], wraw[:, :, :]).then_inc(s_wo, 1)
                dve.wait_ge(s_sums, 16)
                nc.vector.reciprocal(sums[:, :], sums[:, :]).then_inc(s_inv, 1)
                dve.wait_ge(s_wo, 1)
                nc.vector.tensor_tensor(out=wo[1][:, :, :], in0=wraw[:, :, :], in1=wo[0][:, :, :].bitcast(F32),
                                        op=ALU.subtract).then_inc(s_wo, 1)

            def normalise(i, par):
                r = 2 * i + par
                dve.wait_ge(s_x[par], 16 * (i + 1))
                if attn:
                    dve.wait_ge(s_xb, r + 1)
                for j in range(TJ):
                    n = TJ * r + j
                    if attn:
                        dve.wait_ge(s_op, n + 1)
                        nc.vector.tensor_tensor(out=x[par][:, j, :], in0=x[par][:, j, :], in1=op[j][:, :],
                                                op=ALU.add).then_inc(s_x2, 1)
                        dve.wait_ge(s_x2, n + 1)
                    dve.wait_ge(s_mv, past(n - 1))
                    nc.vector.bn_stats(stats[j % 2][:, :], x[par][:, j, :]).then_inc(s_stats, 1)
                    work_out(dve, n + 1, r, TJ * r)
                    dve.wait_ge(*met)
                    dve.wait_ge(s_stats, n + 1)
                    dve.wait_ge(s_std, r)
                    dve.wait_ge(s_xn, TJ * r)
                    nc.vector.bn_aggr(mv[:, j, :], stats[j % 2][:, :]).then_inc(s_mv, 1)
                dve.wait_ge(s_std, r + 1)
                dve.wait_ge(s_mv, TJ * (r + 1))
                nc.vector.reciprocal(rstd[:, :], std[:, :]).then_inc(s_rstd, 1)
                dve.wait_ge(s_rstd, r + 1)
                dve.wait_ge(s_xn_stored[par], 16 * i)
                dve.wait_ge(s_tp, past(TJ * r - TJ))
                for j in range(TJ):
                    nc.vector.tensor_scalar(xn[par][:, j, :], x[par][:, j, :], mv[:, j, 0:1], rstd[:, j:j + 1],
                                            ALU.subtract, ALU.mult).then_inc(s_xn, 1)

            def choose(i, par):
                r = 2 * i + par
                work_out(dve, TJ * (r + 1))
                dve.wait_ge(*met)
                dve.wait_ge(s_logits, TJ * (r + 1))
                for j in range(TJ):
                    nc.vector.max(top[:, j, :], logits[:, j, :]).then_inc(s_top, 1)
                work_out(dve, 2 * TJ * r + TJ)
                dve.wait_ge(*met)
                dve.wait_ge(s_top, 2 * TJ * r + TJ)
                for j in range(TJ):
                    nc.vector.max_index(topi[:, j, :], top[:, j, :], logits[:, j, :]).then_inc(s_top, 1)
                nc.vector.tensor_tensor(out=shifted[:, :, :], in0=logits[:, :, :],
                                        in1=top[:, :, 0:1].broadcast_to([P, TJ, E]),
                                        op=ALU.subtract).then_inc(s_shifted, 1)
                dve.wait_ge(s_top, 2 * TJ * (r + 1))
                dve.wait_ge(s_shifted, r + 1)
                pick.start(dve, r)
                pick.link(nc.vector.tensor_copy(idxf[:, :], topi[:, :, 0]))
                dve.wait_ge(s_pos, r)
                nc.vector.tensor_tensor(out=onehot[:, :, :], in0=iota[:, :].unsqueeze(1).broadcast_to([P, TJ, E]),
                                        in1=idxf[:, :].unsqueeze(2).broadcast_to([P, TJ, E]),
                                        op=ALU.is_equal).then_inc(s_onehot, 1)
                dve.wait_ge(s_exp, r + 1)
                pick.link(nc.vector.tensor_reduce(out=den[:, :], in_=ex[:, :, :], axis=AX.X, op=ALU.add))
                pick.link(nc.vector.reciprocal(gate[:, :], den[:, :]))
                dve.wait_ge(s_onehot, r + 1)
                pick.link(nc.vector.tensor_reduce(out=seen[:, :], in_=onehot[:, :, :].rearrange("p j e -> p e j"),
                                                  axis=AX.X, op=ALU.add))

            def slots(i, par):
                r = 2 * i + par
                dve.wait_ge(s_pos, r + 1)
                nc.vector.tensor_tensor(out=run[:, :], in0=run[:, :], in1=seen[:, :], op=ALU.add).then_inc(s_run, 1)
                place.start(dve, r)
                place.link(nc.vector.tensor_tensor(out=picked[:, :, :], in0=posp[:, :, :], in1=onehot[:, :, :],
                                                   op=ALU.mult))
                place.link(nc.vector.tensor_reduce(out=pos[:, :], in_=picked[:, :, :], axis=AX.X, op=ALU.add))
                place.link(nc.vector.tensor_scalar(ok[:, :], pos[:, :], float(C), None, ALU.is_le))
                place.link(nc.vector.scalar_tensor_tensor(slot[:, :], idxf[:, :], float(CP), pos[:, :],
                                                          ALU.mult, ALU.add))
                place.link(nc.vector.scalar_tensor_tensor(slot2[:, :], slot[:, :], -1.0 - NOSLOT, ok[:, :],
                                                          ALU.add, ALU.mult))
                dve.wait_ge(s_scat[par], 16 * TJ * i)
                dve.wait_ge(s_meta[par], 32 * i)
                place.link(nc.vector.tensor_scalar(slot_i[par][:, :], slot2[:, :], float(NOSLOT), None, ALU.add))
                place.link(nc.vector.tensor_copy(tok_i[par][:, :], tokf[:, :]))
                place.link(nc.vector.tensor_scalar(tokf[:, :], tokf[:, :], float(GROUP), None, ALU.add))
                nc.vector.scalar_tensor_tensor(gateh[par][:, :], gate[:, :], 0.5, ok[:, :],
                                               ALU.mult, ALU.mult).then_inc(s_slots, 1)
                work_out(dve, r + 1, r + 1)
                dve.wait_ge(*met)
                dve.wait_ge(s_slots, r + 1)
                dve.wait_ge(s_run, r + 1)

            def step(i, par, nxt, far):
                choose(i, par)
                if nxt:
                    normalise(*nxt)
                slots(i, par)

            normalise(0, 0)
            rounds_ahead(dve, NG, step)

        @block.tensor
        def _(pe):
            pe.wait_ge(s_const, 16 * n_const)
            pe.wait_ge(s_memset, 5)
            pe.wait_ge(s_setup, 1)
            if attn:
                pe.wait_ge(s_wo, 2)

            def project(i, par):
                r = 2 * i + par
                pe.wait_ge(s_ao_lo, r + 1)
                for j in range(TJ):
                    n = TJ * r + j
                    pe.wait_ge(s_x2, past(n - TJ + 1))
                    for k in range(KD):
                        last = matmul3(nc, op[j][:, :], [a[:, k, j * P:(j + 1) * P] for a in ao[par]],
                                       [w[:, k, :] for w in wo], k == 0, k == KD - 1)
                    last.then_inc(s_op, 1)

            def logit(i, par):
                r = 2 * i + par
                for j in range(TJ):
                    n = TJ * r + j
                    pe.wait_ge(s_xn, n + 1)
                    pe.wait_ge(s_xnT, past(n - 1))
                    for k in range(KD):
                        last = nc.tensor.transpose(tp[j % 2][:, k, :], xn[par][:, j, k * P:(k + 1) * P], ident[:, :])
                    last.then_inc(s_tp, 1)
                    if j:
                        products(r, j - 1)
                products(r, TJ - 1)

            def products(r, j):
                pe.wait_ge(s_xnT, TJ * r + j + 1)
                pe.wait_ge(s_shifted, r)
                pe.wait_ge(s_top, 2 * TJ * r)
                for k in range(KD):
                    last = nc.tensor.matmul(logits[:, j, :], xnT[j % 2][:, k, :], wr_sb[:, k, :],
                                            start=k == 0, stop=k == KD - 1)
                last.then_inc(s_logits, 1)

            def positions(i, par):
                r = 2 * i + par
                pe.wait_ge(s_onehot, r + 1)
                pe.wait_ge(s_run, r)
                pe.wait_ge(s_slots, r)
                for j in range(TJ):
                    nc.tensor.matmul(posp[:, j, :], tri[:, :], onehot[:, j, :], start=True, stop=False)
                    for before in range(j):
                        nc.tensor.matmul(posp[:, j, :], ones[:, :], onehot[:, before, :], start=False, stop=False)
                    last = nc.tensor.matmul(posp[:, j, :], ones[:, :], run[:, :], start=False, stop=True)
                last.then_inc(s_pos, 1)

            def step(i, par, nxt, far):
                if attn and nxt:
                    project(*nxt)
                positions(i, par)
                if nxt:
                    logit(*nxt)

            if attn:
                project(0, 0)
            logit(0, 0)
            rounds_ahead(pe, NG, step)


def experts(nc, name, moved, xn, table, wg, wu, wd, cst, y_out):
    S = Space(nc, name)
    sb, ps, sem = S.sb, S.ps, S.sem
    with S.ctx:
        ident = sb("ident", [P, P])
        raw = [S.pair(sb, f"raw{w}", [P, KD, F]) for w in range(3)]
        split = [[S.pair(sb, f"w{w}_{par}", [P, KD, F], F32R) for par in range(2)] for w in range(3)]
        idx = S.pair(sb, "idx", [CW, CT], I32)
        xg = S.pair(sb, "xg", [CW, CT, D])
        xT = S.pair(sb, "xT", [P, KD, CP], F32R)
        sg = S.pair(sb, "sg", [P, CP])
        af = S.pair(sb, "af", [P, CP])
        aT = S.pair(sb, "aT", [P, KF, CP], F32R)
        y = sb("y", [CW, CT, D])
        tp = S.pair(S.bank, "tp", CP)
        gp = S.pair(S.bank, "gp", CP)
        up = S.pair(S.bank, "up", CP)
        yp = S.pair(ps, "yp", [CW, D])

        s_const = sem("s_const")
        s_raw = [S.pair(sem, f"s_raw{w}") for w in range(3)]
        s_hi = sem("s_hi")
        s_lo = sem("s_lo")
        s_idx = S.pair(sem, "s_idx")
        s_xg = moved
        s_tp = sem("s_tp")
        s_xh = sem("s_xh")
        s_xl = sem("s_xl")
        s_gu = sem("s_gu")
        s_sg = sem("s_sg")
        s_af = sem("s_af")
        s_ah = sem("s_ah")
        s_al = sem("s_al")
        s_y = sem("s_y")
        s_yc = sem("s_yc")
        s_stored = sem("s_stored")
        block = S.block()
        met = (s_const, 16)
        weights = [wg, wu, wd]

        def w_ap(w, e):
            return weights[w][bass.ds(e, 1), :, :].rearrange("o (k p) f -> p (o k) f", p=P)

        def load_raw(sp, i, par):
            e = 2 * i + par
            for w in range(3):
                sp.wait_ge(s_hi, past(3 * (e - 2) + w + 1))
                sp.wait_ge(s_lo, past(3 * (e - 2) + w + 1))
                sp.dma_start(raw[w][par][:, :, :], w_ap(w, e)).then_inc(s_raw[w][par], 16)

        @block.sync
        def _(sp):
            sp.dma_start(ident[:, :], cst["ident"]).then_inc(s_const, 16)

            def load_idx(i, par):
                sp.wait_ge(s_xg[par], 16 * CT * i)
                sp.dma_start(idx[par][:, :], table[bass.ds((2 * i + par) * CP, CP), :].rearrange(
                    "(p c) o -> p (c o)", p=CW)).then_inc(s_idx[par], 16)

            def store(i, par):
                e = 2 * i + par
                sp.wait_ge(s_yc, CT * (e + 1))
                sp.dma_start(y_out[bass.ds(e * CP, CP), :].rearrange("(p c) n -> p (c n)", p=CW),
                             y[:, :, :].rearrange("p c n -> p (c n)")).then_inc(s_stored, 16)

            def step(i, par, nxt, far):
                if nxt:
                    load_idx(*nxt)
                if far:
                    load_raw(sp, *far)
                store(i, par)

            load_idx(0, 0)
            load_raw(sp, 0, 0)
            load_raw(sp, 0, 1)
            rounds_ahead(sp, E, step)
            sp.wait_ge(s_stored, 16 * E)

        @block.gpsimd
        def _(pool):
            def gather(i, par):
                work_out(pool, 16 * (i + 1), KD * (2 * i + par - 1))
                pool.wait_ge(*met)
                pool.wait_ge(s_idx[par], 16 * (i + 1))
                pool.wait_ge(s_tp, past(KD * (2 * i + par - 1)))
                for c in range(CT):
                    nc.gpsimd.indirect_dma_start(
                        out=xg[par][:, c, :], out_offset=None, in_=xn,
                        in_offset=bass.IndirectOffsetOnAxis(ap=idx[par][:, c:c + 1], axis=0),
                        bounds_check=T, oob_is_err=False).then_inc(s_xg[par], 16)

            rounds(pool, E, gather)

        def hi_weight(act, w, i, par):
            e = 2 * i + par
            act.wait_ge(s_raw[w][par], 16 * (i + 1))
            act.wait_ge(s_gu, past(KF * (e - 1)))
            act.wait_ge(s_y, past(CT * (e - 1)))
            nc.scalar.activation(split[w][par][0][:, :, :], raw[w][par][:, :, :], ACT.Copy).then_inc(s_hi, 1)

        def lo_weight(dve, w, i, par):
            e = 2 * i + par
            dve.wait_ge(s_hi, 3 * e + w + 1)
            nc.vector.tensor_tensor(out=split[w][par][1][:, :, :], in0=raw[w][par][:, :, :],
                                    in1=split[w][par][0][:, :, :].bitcast(F32), op=ALU.subtract).then_inc(s_lo, 1)

        @block.scalar
        def _(act):
            def hi_x(i, par, k):
                e = 2 * i + par
                act.wait_ge(s_tp, KD * e + k + 1)
                act.wait_ge(s_gu, KF * e)
                nc.scalar.activation(xT[0][:, k, :], tp[k % 2][:, :], ACT.Copy).then_inc(s_xh, 1)

            def store_y(i, par, c):
                e = 2 * i + par
                act.wait_ge(s_y, CT * e + c + 1)
                act.wait_ge(s_stored, 16 * e)
                nc.scalar.activation(y[:, c, :], yp[c % 2][:, :], ACT.Copy).then_inc(s_yc, 1)

            def step(i, par, nxt, far):
                e = 2 * i + par
                for f in range(KF):
                    n = KF * e + f
                    act.wait_ge(s_gu, n + 1)
                    act.wait_ge(s_af, past(n - 1))
                    nc.scalar.activation(sg[f % 2][:, :], gp[f % 2][:, :], ACT.Silu).then_inc(s_sg, 1)
                    if nxt and f < 2:
                        hi_weight(act, f, *nxt)
                if nxt:
                    hi_x(*nxt, 0)
                    hi_x(*nxt, 1)
                for c in range(CT):
                    store_y(i, par, c)
                    if nxt and c + 2 < KD:
                        hi_x(*nxt, c + 2)
                if nxt:
                    hi_weight(act, 2, *nxt)

            for w in range(3):
                hi_weight(act, w, 0, 0)
            for k in range(KD):
                hi_x(0, 0, k)
            rounds_ahead(act, E, step)

        @block.vector
        def _(dve):
            def lo_x(i, par):
                e = 2 * i + par
                for k in range(KD):
                    dve.wait_ge(s_xh, KD * e + k + 1)
                    nc.vector.tensor_tensor(out=xT[1][:, k, :], in0=tp[k % 2][:, :],
                                            in1=xT[0][:, k, :].bitcast(F32), op=ALU.subtract).then_inc(s_xl, 1)

            def step(i, par, nxt, far):
                e = 2 * i + par
                for f in range(KF):
                    n = KF * e + f
                    dve.wait_ge(s_sg, n + 1)
                    dve.wait_ge(s_al, past(n - 1))
                    nc.vector.tensor_tensor(out=af[f % 2][:, :], in0=up[f % 2][:, :], in1=sg[f % 2][:, :],
                                            op=ALU.mult).then_inc(s_af, 1)
                    dve.wait_ge(s_af, n + 1)
                    dve.wait_ge(s_y, CT * e)
                    nc.vector.tensor_copy(aT[0][:, f, :], af[f % 2][:, :]).then_inc(s_ah, 1)
                    dve.wait_ge(s_ah, n + 1)
                    nc.vector.tensor_tensor(out=aT[1][:, f, :], in0=af[f % 2][:, :],
                                            in1=aT[0][:, f, :].bitcast(F32), op=ALU.subtract).then_inc(s_al, 1)
                    if nxt and f < 2:
                        lo_weight(dve, f, *nxt)
                if nxt:
                    lo_x(*nxt)
                    lo_weight(dve, 2, *nxt)

            for w in range(3):
                lo_weight(dve, w, 0, 0)
            lo_x(0, 0)
            rounds_ahead(dve, E, step)

        @block.tensor
        def _(pe):
            pe.wait_ge(s_const, 16)

            def turn(i, par, k):
                e = 2 * i + par
                pe.wait_ge(s_xg[par], 16 * CT * (i + 1))
                pe.wait_ge(s_xl, past(KD * e + k - 1))
                for c in range(CT):
                    last = nc.tensor.transpose(tp[k % 2][:, c * CW:(c + 1) * CW],
                                               xg[par][:, c, k * P:(k + 1) * P],
                                               ident[0:CW, 0:CW])
                last.then_inc(s_tp, 1)

            def gate_up(i, par):
                e = 2 * i + par
                pe.wait_ge(s_lo, 3 * e + 2)
                for f in range(KF):
                    n = KF * e + f
                    pe.wait_ge(s_af, past(n - 1))
                    for w, out in ((0, gp), (1, up)):
                        for k in range(KD):
                            if f == 0 and w == 0:
                                pe.wait_ge(s_xl, KD * e + k + 1)
                            last = matmul3(nc, out[f % 2][:, :],
                                           [s[:, k, f * P:(f + 1) * P] for s in split[w][par]],
                                           [s[:, k, :] for s in xT], k == 0, k == KD - 1)
                    last.then_inc(s_gu, 1)

            def down(i, par, c):
                e = 2 * i + par
                n = CT * e + c
                if c == 0:
                    pe.wait_ge(s_lo, 3 * e + 3)
                pe.wait_ge(s_yc, past(n - 1))
                for f in range(KF):
                    if c == 0:
                        pe.wait_ge(s_al, KF * e + f + 1)
                    last = matmul3(nc, yp[c % 2][:, :],
                                   [a[:, f, c * CW:(c + 1) * CW] for a in aT],
                                   [s[:, f, :] for s in split[2][par]], f == 0, f == KF - 1)
                last.then_inc(s_y, 1)

            def step(i, par, nxt, far):
                if nxt:
                    turn(*nxt, 0)
                    turn(*nxt, 1)
                for c in range(CT):
                    down(i, par, c)
                    if nxt and c + 2 < KD:
                        turn(*nxt, c + 2)
                if nxt:
                    gate_up(*nxt)

            for k in range(KD):
                turn(0, 0, k)
            gate_up(0, 0)
            rounds_ahead(pe, E, step)


def qkv(nc, name, moved, x_in, xn_in, y, slot_in, gate_in, wT, bias, cst, x_out, q_out, k_out, v_out):
    S = Space(nc, name)
    sb, ps, sem = S.sb, S.ps, S.sem
    with S.ctx:
        ident = sb("ident", [P, P])
        eps = sb("eps", [P, 1])
        cos = sb("cos", [P, L])
        sin = sb("sin", [P, L])
        wraw = sb("wraw", [P, KD, D])
        w = [S.pair(sb, f"w{m}", [P, KD, D], F32R) for m in range(3)]
        bqk = [sb(f"b{m}", [P, KD]) for m in range(2)]
        bv = sb("bv", [P, D])
        x = S.pair(sb, "x", [P, TJ, D])
        xn = sb("xn", [P, TJ, D])
        yg = sb("yg", [P, TJ, D])
        xa = sb("xa", [P, TJ, D])
        slot = S.pair(sb, "slot", [P, TJ], I32)
        gateh = S.pair(sb, "gateh", [P, TJ])
        stats = S.pair(sb, "stats", [P, 6])
        mv = sb("mv", [P, TJ, 2])
        std = sb("std", [P, TJ])
        rstd = sb("rstd", [P, TJ])
        xT = [S.pair(sb, f"xT{par}", [P, KD, GROUP], F32R) for par in range(2)]
        qb = S.pair(sb, "qb", [P, GROUP])
        qs = S.pair(sb, "qs", [P, GROUP])
        qc = S.pair(sb, "qc", [P, GROUP])
        qh = S.pair(sb, "qh", [P, GROUP], F32R)
        ql = S.pair(sb, "ql", [P, GROUP], F32R)
        v = S.pair(sb, "v", [P, NH, 2 * HD])
        tp = S.pair(ps, "tp", [P, KD, P])
        pp = S.pair(ps, "pp", [P, GROUP])
        vp = S.pair(ps, "vp", [P, D])

        s_const = sem("s_const")
        s_wraw = sem("s_wraw")
        s_w = sem("s_w")
        s_memset = sem("s_memset")
        s_x = S.pair(sem, "s_x")
        s_xn_in = sem("s_xn_in")
        s_meta = S.pair(sem, "s_meta")
        s_yg = moved[0]
        s_half = sem("s_half")
        s_x1 = sem("s_x1")
        s_x1_stored = S.pair(sem, "s_x1_stored")
        s_stats = sem("s_stats")
        s_mv = sem("s_mv")
        s_std = sem("s_std")
        s_rstd = sem("s_rstd")
        s_xa = sem("s_xa")
        s_tp = sem("s_tp")
        s_xh = sem("s_xh")
        s_xl = sem("s_xl")
        s_pp = sem("s_pp")
        s_qb = sem("s_qb")
        s_qs = sem("s_qs")
        s_qc = sem("s_qc")
        s_rot = sem("s_rot")
        s_qh = sem("s_qh")
        s_ql = sem("s_ql")
        s_q_stored = S.pair(sem, "s_q_stored")
        s_vp = sem("s_vp")
        s_v = sem("s_v")
        s_v_stored = S.pair(sem, "s_v_stored")
        block = S.block()
        met = (s_const, 96)
        NQ = 2 * KD
        SWAP = [(d + HD // 2) % HD for d in range(HD)]

        def rows(ap, i, par):
            return tiles(ap[bass.ds((2 * i + par) * GROUP, GROUP), :])

        def meta(ap, i, par):
            return ap[bass.ds(2 * i + par, 1), :, :].rearrange("o p j -> (o p) j")

        @block.sync
        def _(sp):
            for dst, src in ((ident, cst["ident"]), (cos, cst["cos"]), (sin, cst["sin"])):
                sp.dma_start(dst[:, :], src).then_inc(s_const, 16)
            for m in range(2):
                sp.dma_start(bqk[m][:, :], bias[m]).then_inc(s_const, 16)
            sp.dma_start(bv[:, :], bias[2].rearrange("(o n) -> o n", o=1).broadcast_to([P, D])).then_inc(s_const, 16)

            def load(i, par):
                r = 2 * i + par
                work_out(sp, 16 * TJ * (r - 1))
                sp.wait_ge(*met)
                sp.wait_ge(s_yg, past(16 * TJ * (r - 1)))
                sp.wait_ge(s_x1, past(TJ * (r - 1)))
                sp.dma_start(slot[par][:, :], meta(slot_in, i, par)).then_inc(s_meta[par], 16)
                sp.dma_start(gateh[par][:, :], meta(gate_in, i, par)).then_inc(s_meta[par], 16)
                sp.wait_ge(s_x1_stored[par], 16 * i)
                sp.wait_ge(s_xa, past(TJ * (r - 1)))
                sp.dma_start(x[par][:, :, :], rows(x_in, i, par)).then_inc(s_x[par], 16)
                sp.wait_ge(s_half, r)
                sp.dma_start(xn[:, :, :], rows(xn_in, i, par)).then_inc(s_xn_in, 16)

            load(0, 0)
            for m in range(3):
                sp.wait_ge(s_w, 2 * m)
                sp.dma_start(wraw[:, :, :], wT[m].rearrange("(k p) n -> p k n", p=P)).then_inc(s_wraw, 16)

            def step(i, par, nxt, far):
                r = 2 * i + par
                if nxt:
                    load(*nxt)
                sp.wait_ge(s_x1, TJ * (r + 1))
                sp.dma_start(rows(x_out, i, par), x[par][:, :, :]).then_inc(s_x1_stored[par], 16)

            rounds_ahead(sp, NG, step)
            for par in range(2):
                sp.wait_ge(s_x1_stored[par], 16 * (NG // 2))

        @block.gpsimd
        def _(pool):
            nc.gpsimd.memset(eps[:, :], EPS).then_inc(s_memset, 1)
            for b in range(2):
                nc.gpsimd.memset(v[b][:, :, HD:2 * HD], 1.0).then_inc(s_memset, 1)

            def gather(i, par):
                r = 2 * i + par
                work_out(pool, 32 * (i + 1), TJ * r)
                pool.wait_ge(*met)
                pool.wait_ge(s_meta[par], 32 * (i + 1))
                pool.wait_ge(s_x1, TJ * r)
                for j in range(TJ):
                    nc.gpsimd.indirect_dma_start(
                        out=yg[:, j, :], out_offset=None, in_=y,
                        in_offset=bass.IndirectOffsetOnAxis(ap=slot[par][:, j:j + 1], axis=0),
                        bounds_check=NOSLOT, oob_is_err=False).then_inc(s_yg, 16)

            def turn(i, par):
                for t in range(NQ):
                    n = NQ * (2 * i + par) + t
                    pool.wait_ge(s_qb, n + 1)
                    pool.wait_ge(s_ql, past(n - 1))
                    nc.gpsimd.tensor_tensor(out=qc[t % 2][:, :], in0=qb[t % 2][:, :],
                                            in1=cos[:, par * GROUP:(par + 1) * GROUP], op=ALU.mult).then_inc(s_qc, 1)
                    pool.wait_ge(s_qs, n + 1)
                    nc.gpsimd.tensor_tensor(out=qs[t % 2][:, :], in0=qs[t % 2][:, :],
                                            in1=sin[:, par * GROUP:(par + 1) * GROUP], op=ALU.mult).then_inc(s_qc, 1)

            def step(i, par, nxt, far):
                if nxt:
                    gather(*nxt)
                turn(i, par)

            pool.wait_ge(s_const, 96)
            gather(0, 0)
            rounds_ahead(pool, NG, step)

        @block.scalar
        def _(act):
            act.wait_ge(s_memset, 3)
            act.wait_ge(s_const, 96)
            for m in range(3):
                act.wait_ge(s_wraw, 16 * (m + 1))
                nc.scalar.activation(w[m][0][:, :, :], wraw[:, :, :], ACT.Copy).then_inc(s_w, 1)
                act.wait_ge(s_w, 2 * m + 2)

            def norm(i, par):
                r = 2 * i + par
                act.wait_ge(s_mv, TJ * (r + 1))
                nc.scalar.activation(std[:, :], mv[:, :, 1], ACT.Sqrt, bias=eps[:, 0:1]).then_inc(s_std, 1)

            def hi_x(i, par, j):
                n = TJ * (2 * i + par) + j
                act.wait_ge(s_tp, n + 1)
                act.wait_ge(s_vp, past(TJ * (2 * i + par - 1)))
                nc.scalar.activation(xT[par][0][:, :, j * P:(j + 1) * P], tp[j % 2][:, :, :],
                                     ACT.Copy).then_inc(s_xh, 1)

            def copy_q(i, par, t):
                n = NQ * (2 * i + par) + t
                act.wait_ge(s_pp, n + 1)
                act.wait_ge(s_qc, past(2 * (n - 1)))
                nc.scalar.activation(qb[t % 2][:, :], pp[t % 2][:, :], ACT.Identity,
                                     bias=bqk[t // KD][:, t % KD:t % KD + 1]).then_inc(s_qb, 1)

            def store_q(i, par, t):
                r = 2 * i + par
                n = NQ * r + t
                act.wait_ge(s_ql, n + 1)
                out = (q_out, k_out)[t // KD]
                h0 = (t % KD) * P
                for part, s in ((0, qh), (1, ql)):
                    act.dma_start(out[part, bass.ds(i, 1), h0:h0 + P, par * GROUP:(par + 1) * GROUP].rearrange(
                        "o d q -> (o d) q"), s[t % 2][:, :].bitcast(F32)).then_inc(s_q_stored[t % 2], 16)

            def store_v(i, par, j):
                r = 2 * i + par
                n = TJ * r + j
                act.wait_ge(s_v, n + 1)
                act.dma_start(v_out[bass.ds(i, 1), :, par * GROUP + j * P:par * GROUP + (j + 1) * P, :].rearrange(
                    "o g t c -> t (o g) c"), v[j % 2][:, :, :].rearrange("p (g h) c -> p g (h c)", h=2)).then_inc(
                        s_v_stored[j % 2], 16)

            def step(i, par, nxt, far):
                copy_q(i, par, 0)
                for t in range(NQ):
                    if t + 1 < NQ:
                        copy_q(i, par, t + 1)
                    store_q(i, par, t)
                    if nxt and t == 3:
                        norm(*nxt)
                    if nxt and t >= 4:
                        hi_x(*nxt, t - 4)
                for j in range(TJ):
                    store_v(i, par, j)

            norm(0, 0)
            for j in range(TJ):
                hi_x(0, 0, j)
            rounds_ahead(act, NG, step)
            for b in range(2):
                act.wait_ge(s_q_stored[b], 32 * NG * NQ // 2)
                act.wait_ge(s_v_stored[b], 16 * NG * TJ // 2)

        @block.vector
        def _(dve):
            dve.wait_ge(s_const, 96)
            dve.wait_ge(s_memset, 3)
            for m in range(3):
                dve.wait_ge(s_w, 2 * m + 1)
                nc.vector.tensor_tensor(out=w[m][1][:, :, :], in0=wraw[:, :, :], in1=w[m][0][:, :, :].bitcast(F32),
                                        op=ALU.subtract).then_inc(s_w, 1)

            def combine(i, par):
                r = 2 * i + par
                dve.wait_ge(s_x[par], 16 * (i + 1))
                dve.wait_ge(s_xn_in, 16 * (r + 1))
                nc.vector.scalar_tensor_tensor(x[par][:, :, :].rearrange("p j n -> p (j n)"),
                                               xn[:, :, :].rearrange("p j n -> p (j n)"), 0.5,
                                               x[par][:, :, :].rearrange("p j n -> p (j n)"),
                                               ALU.mult, ALU.add).then_inc(s_half, 1)
                dve.wait_ge(s_half, r + 1)
                dve.wait_ge(s_yg, 16 * TJ * (r + 1))
                dve.wait_ge(s_meta[par], 32 * (i + 1))
                for j in range(TJ):
                    n = TJ * r + j
                    nc.vector.scalar_tensor_tensor(x[par][:, j, :], yg[:, j, :], gateh[par][:, j:j + 1],
                                                   x[par][:, j, :], ALU.mult, ALU.add).then_inc(s_x1, 1)
                    dve.wait_ge(s_x1, n + 1)
                    dve.wait_ge(s_mv, past(n - 1))
                    nc.vector.bn_stats(stats[j % 2][:, :], x[par][:, j, :]).then_inc(s_stats, 1)
                    work_out(dve, n + 1, r, TJ * r)
                    dve.wait_ge(*met)
                    dve.wait_ge(s_stats, n + 1)
                    dve.wait_ge(s_std, r)
                    dve.wait_ge(s_xa, TJ * r)
                    nc.vector.bn_aggr(mv[:, j, :], stats[j % 2][:, :]).then_inc(s_mv, 1)

            def normalise(i, par):
                r = 2 * i + par
                dve.wait_ge(s_std, r + 1)
                dve.wait_ge(s_mv, TJ * (r + 1))
                nc.vector.reciprocal(rstd[:, :], std[:, :]).then_inc(s_rstd, 1)
                dve.wait_ge(s_rstd, r + 1)
                dve.wait_ge(s_tp, TJ * r)
                for j in range(TJ):
                    nc.vector.tensor_scalar(xa[:, j, :], x[par][:, j, :], mv[:, j, 0:1], rstd[:, j:j + 1],
                                            ALU.subtract, ALU.mult).then_inc(s_xa, 1)

            def lo_x(i, par, j):
                n = TJ * (2 * i + par) + j
                dve.wait_ge(s_xh, n + 1)
                nc.vector.tensor_tensor(out=xT[par][1][:, :, j * P:(j + 1) * P], in0=tp[j % 2][:, :, :],
                                        in1=xT[par][0][:, :, j * P:(j + 1) * P].bitcast(F32),
                                        op=ALU.subtract).then_inc(s_xl, 1)

            def swap(i, par, t):
                n = NQ * (2 * i + par) + t
                work_out(dve, n + 1, n - 1)
                dve.wait_ge(*met)
                dve.wait_ge(s_qb, n + 1)
                dve.wait_ge(s_rot, past(n - 1))
                nc.vector.stream_shuffle(qs[t % 2][:, :], qb[t % 2][:, :], SWAP).then_inc(s_qs, 1)

            def rotate(i, par, t):
                n = NQ * (2 * i + par) + t
                dve.wait_ge(s_qc, 2 * (n + 1))
                uses = (NQ // 2) * (2 * i + par) + t // 2
                dve.wait_ge(s_q_stored[t % 2], 32 * uses)
                nc.vector.tensor_tensor(out=qc[t % 2][:, :], in0=qc[t % 2][:, :], in1=qs[t % 2][:, :],
                                        op=ALU.add).then_inc(s_rot, 1)
                dve.wait_ge(s_rot, n + 1)
                nc.vector.tensor_copy(qh[t % 2][:, :], qc[t % 2][:, :]).then_inc(s_qh, 1)
                dve.wait_ge(s_qh, n + 1)
                nc.vector.tensor_tensor(out=ql[t % 2][:, :], in0=qc[t % 2][:, :], in1=qh[t % 2][:, :].bitcast(F32),
                                        op=ALU.subtract).then_inc(s_ql, 1)
                dve.wait_ge(s_ql, n + 1)

            def copy_v(i, par, j):
                n = TJ * (2 * i + par) + j
                dve.wait_ge(s_vp, n + 1)
                dve.wait_ge(s_v_stored[j % 2], 16 * ((TJ // 2) * (2 * i + par) + j // 2))
                nc.vector.tensor_tensor(out=v[j % 2][:, :, 0:HD],
                                        in0=vp[j % 2][:, :].rearrange("p (h d) -> p h d", h=NH),
                                        in1=bv[:, :].rearrange("p (h d) -> p h d", h=NH), op=ALU.add).then_inc(s_v, 1)

            def step(i, par, nxt, far):
                swap(i, par, 0)
                for t in range(NQ):
                    if t + 1 < NQ:
                        swap(i, par, t + 1)
                    rotate(i, par, t)
                    if nxt and t == 2:
                        combine(*nxt)
                    if nxt and t == 3:
                        normalise(*nxt)
                    if nxt and t >= 4:
                        lo_x(*nxt, t - 4)
                for j in range(TJ):
                    copy_v(i, par, j)

            combine(0, 0)
            normalise(0, 0)
            for j in range(TJ):
                lo_x(0, 0, j)
            rounds_ahead(dve, NG, step)

        @block.tensor
        def _(pe):
            pe.wait_ge(s_const, 96)
            pe.wait_ge(s_w, 6)

            def turn(i, par, j):
                n = TJ * (2 * i + par) + j
                pe.wait_ge(s_xa, n + 1)
                pe.wait_ge(s_xl, past(n - 1))
                for k in range(KD):
                    last = nc.tensor.transpose(tp[j % 2][:, k, :], xa[:, j, k * P:(k + 1) * P], ident[:, :])
                last.then_inc(s_tp, 1)

            def project(i, par, t):
                n = NQ * (2 * i + par) + t
                pe.wait_ge(s_qb, past(n - 1))
                m, c = t // KD, t % KD
                for k in range(KD):
                    last = matmul3(nc, pp[t % 2][:, :], [s[:, k, c * P:(c + 1) * P] for s in w[m]],
                                   [s[:, k, :] for s in xT[par]], k == 0, k == KD - 1)
                last.then_inc(s_pp, 1)

            def values(i, par, j):
                n = TJ * (2 * i + par) + j
                pe.wait_ge(s_v, past(n - 1))
                for k in range(KD):
                    last = matmul3(nc, vp[j % 2][:, :], [s[:, k, j * P:(j + 1) * P] for s in xT[par]],
                                   [s[:, k, :] for s in w[2]], k == 0, k == KD - 1)
                last.then_inc(s_vp, 1)

            def step(i, par, nxt, far):
                r = 2 * i + par
                pe.wait_ge(s_xl, TJ * (r + 1))
                for t in range(NQ):
                    project(i, par, t)
                    if nxt and t >= 4:
                        turn(*nxt, t - 4)
                for j in range(TJ):
                    values(i, par, j)

            for j in range(TJ):
                turn(0, 0, j)
            rounds_ahead(pe, NG, step)


def attention(nc, name, q_in, k_in, v_in, cst, ao_out, sum_out):
    S = Space(nc, name)
    sb, ps, sem = S.sb, S.ps, S.sem
    NP = B * NH // 2
    KT = L // P
    HALF = L // 2
    SCALE = 1.0 / float(HD) ** 0.5
    NM = 2 * KT * 2
    MAXES = [(0, 0, 0), (2, 2, 2), (2, 2, 2), (2, 2, 2), (2, 2, 2), (2, 2, 2), (2, 0, 0), (0, 0, 0)]
    assert sum(map(sum, MAXES)) == NM
    with S.ctx:
        ident = sb("ident", [P, P])
        identb = sb("identb", [P, P], BF16)
        qst = [S.pair(sb, f"q{h}", [P, L], F32R) for h in range(2)]
        kst = [S.pair(sb, f"k{h}", [P, L], F32R) for h in range(2)]
        v = S.pair(sb, "v", [P, KT, 2, 2 * HD])
        pr = [S.pair(sb, f"p{h}", [P, L]) for h in range(2)]
        halves = [sb(f"halves{h}", [P, KT, 2]) for h in range(2)]
        big = [sb(f"big{h}", [P, KT]) for h in range(2)]
        parts = [sb(f"parts{h}", [P, KT, HD], BF16) for h in range(2)]
        o = S.pair(sb, "o", [P, L])
        st = [ps(f"st{h}", [P, L]) for h in range(2)]
        mx = ps("mx", [P, L])
        op = ps("op", [P, L])

        s_const = sem("s_const")
        s_memset = sem("s_memset")
        s_identb = sem("s_identb")
        s_in = S.pair(sem, "s_in")
        s_mx = sem("s_mx")
        s_max = sem("s_max")
        s_big = sem("s_big")
        s_mhi = sem("s_mhi")
        s_mlo = sem("s_mlo")
        s_row = sem("s_row")
        s_rowq0 = sem("s_rowq0")
        s_rowq1 = sem("s_rowq1")
        s_st = [sem(f"s_st{h}") for h in range(2)]
        s_exp = [sem(f"s_exp{h}") for h in range(2)]
        s_pv = sem("s_pv")
        s_o = sem("s_o")
        s_o_stored = S.pair(sem, "s_o_stored")
        block = S.block()
        N_IN = 2 * 6 + 1

        @block.sync
        def _(sp):
            sp.dma_start(ident[:, :], cst["ident"]).then_inc(s_const, 16)
            sp.wait_ge(s_memset, 6)

            def load(pi, par):
                p = 2 * pi + par
                for h in range(2):
                    sp.wait_ge(s_st[h], past(KT * (p - 1)))
                for h in range(2):
                    row = p * (2 * HD) + h * HD
                    for blk, (qp, kp) in enumerate(((0, 0), (0, 1), (1, 0))):
                        for dst, src, part in ((qst, q_in, qp), (kst, k_in, kp)):
                            sp.dma_start(dst[h][par][blk * HD:(blk + 1) * HD, :].bitcast(F32),
                                         src[part, bass.ds(row, HD), :]).then_inc(s_in[par], 16)
                sp.wait_ge(s_pv, past(KT * (p - 1)))
                sp.dma_start(v[par][:, :, :, :].rearrange("p t h c -> p t (h c)"), v_in[bass.ds(p, 1), :, :].rearrange(
                    "o (t p) c -> p (o t) c", p=P)).then_inc(s_in[par], 16)

            def store(p, par):
                sp.wait_ge(s_o, p + 1)
                for h in range(2):
                    sp.dma_start(ao_out[bass.ds(p * (2 * HD) + h * HD, HD), :],
                                 o[par][2 * h * HD:(2 * h + 1) * HD, :]).then_inc(s_o_stored[par], 16)
                    sp.dma_start(sum_out[bass.ds(2 * p + h, 1), :],
                                 o[par][(2 * h + 1) * HD:(2 * h + 1) * HD + 1, :]).then_inc(s_o_stored[par], 16)

            def step(i, par, nxt, far):
                if nxt:
                    load(*nxt)
                if after_first(i, par):
                    store(2 * i + par - 1, 1 - par)

            load(0, 0)
            rounds_ahead(sp, NP, step)
            store(NP - 1, 1)
            for par in range(2):
                sp.wait_ge(s_o_stored[par], 64 * (NP // 2))

        @block.gpsimd
        def _(pool):
            for h in range(2):
                nc.gpsimd.memset(parts[h][:, :, :], 0.0).then_inc(s_memset, 1)
            pool.wait_ge(s_memset, 2)
            for h in range(2):
                for par in range(2):
                    nc.gpsimd.memset(kst[h][par][3 * HD:4 * HD, :].bitcast(F32), -1.0).then_inc(s_memset, 1)

        @block.scalar
        def _(act):
            def exps(p, kt, h):
                n = KT * p + kt
                act.wait_ge(s_st[h], n + 1)
                act.wait_ge(s_pv, past(n - 1))
                nc.scalar.activation(pr[h][kt % 2][:, :], st[h][:, :], ACT.Exp, scale=SCALE).then_inc(s_exp[h], 1)

            def copy_row(i, par):
                act.wait_ge(s_row, 2 * i + par + 1)
                nc.scalar.activation(qst[1][par][3 * HD:4 * HD, :], mx[2 * HD:3 * HD, :],
                                     ACT.Copy).then_inc(s_rowq1, 1)

            def step(i, par, nxt, far):
                p = 2 * i + par
                for kt in range(1, KT):
                    for h in range(2):
                        exps(p, kt, h)
                if nxt:
                    copy_row(*nxt)
                    for h in range(2):
                        exps(p + 1, 0, h)
                act.wait_ge(s_pv, KT * (p + 1))
                act.wait_ge(s_o_stored[par], 64 * i)
                nc.scalar.activation(o[par][:, :], op[:, :], ACT.Copy).then_inc(s_o, 1)

            copy_row(0, 0)
            for h in range(2):
                exps(0, 0, h)
            rounds_ahead(act, NP, step)

        @block.vector
        def _(dve):
            dve.wait_ge(s_const, 16)
            dve.wait_ge(s_memset, 6)
            nc.vector.tensor_copy(identb[:, :], ident[:, :]).then_inc(s_identb, 1)

            def maxima(pi, par):
                p = 2 * pi + par
                for n in range(NM):
                    h, qt, c = n // (2 * KT), n // 2 % KT, n % 2
                    dve.wait_ge(s_mx, NM * p + n + 1)
                    nc.vector.tensor_reduce(out=halves[h][:, qt, c:c + 1], in_=mx[:, c * HALF:(c + 1) * HALF],
                                            axis=AX.X, op=ALU.max).then_inc(s_max, 1)
                dve.wait_ge(s_max, NM * (p + 1))
                for h in range(2):
                    nc.vector.tensor_tensor(out=big[h][:, :], in0=halves[h][:, :, 0], in1=halves[h][:, :, 1],
                                            op=ALU.max).then_inc(s_big, 1)
                dve.wait_ge(s_big, 2 * p + 2)
                for h in range(2):
                    nc.vector.tensor_copy(parts[h][:, :, 0], big[h][:, :]).then_inc(s_mhi, 1)
                dve.wait_ge(s_mhi, 2 * p + 2)
                for h in range(2):
                    nc.vector.tensor_tensor(out=parts[h][:, :, 1], in0=big[h][:, :], in1=parts[h][:, :, 0],
                                            op=ALU.subtract).then_inc(s_mlo, 1)
                dve.wait_ge(s_row, p + 1)
                nc.vector.tensor_copy(qst[0][par][3 * HD:4 * HD, :], mx[3 * HD:4 * HD, :]).then_inc(s_rowq0, 1)

            def step(i, par, nxt, far):
                if nxt:
                    maxima(*nxt)

            maxima(0, 0)
            rounds_ahead(dve, NP, step)

        @block.tensor
        def _(pe):
            pe.wait_ge(s_const, 16)
            pe.wait_ge(s_memset, 6)
            pe.wait_ge(s_identb, 1)

            def rough(pi, par, n):
                p = 2 * pi + par
                h, qt, c = n // (2 * KT), n // 2 % KT, n % 2
                if n == 0:
                    pe.wait_ge(s_in[par], 16 * N_IN * (pi + 1))
                    pe.wait_ge(s_rowq0, p)
                    pe.wait_ge(s_rowq1, p)
                pe.wait_ge(s_max, past(NM * p + n - 1))
                nc.tensor.matmul(mx[:, c * HALF:(c + 1) * HALF], qst[h][par][0:3 * HD, qt * P:(qt + 1) * P],
                                 kst[h][par][0:3 * HD, c * HALF:(c + 1) * HALF],
                                 start=True, stop=True).then_inc(s_mx, 1)

            def row(pi, par):
                p = 2 * pi + par
                pe.wait_ge(s_max, NM * (p + 1))
                pe.wait_ge(s_mlo, 2 * (p + 1))
                for h in range(2):
                    out = mx[(3 - h) * HD:(4 - h) * HD, :]
                    for qt in range(KT):
                        last = nc.tensor.matmul(out[:, qt * P:(qt + 1) * P], parts[h][:, qt, :], identb[:, :],
                                                start=True, stop=True)
                last.then_inc(s_row, 1)

            def scores(p, par, kt, h):
                n = KT * p + kt
                if kt == 0:
                    pe.wait_ge((s_rowq0, s_rowq1)[h], p + 1)
                pe.wait_ge(s_exp[h], n)
                for c in range(2):
                    last = nc.tensor.matmul(st[h][:, c * HALF:(c + 1) * HALF],
                                            kst[h][par][:, kt * P:(kt + 1) * P],
                                            qst[h][par][:, c * HALF:(c + 1) * HALF], start=True, stop=True)
                last.then_inc(s_st[h], 1)

            def products(p, par, kt, c):
                if c == 0:
                    for h in range(2):
                        pe.wait_ge(s_exp[h], KT * p + kt + 1)
                    if kt == 0:
                        pe.wait_ge(s_o, p)
                for h in range(2):
                    last = nc.tensor.matmul(op[2 * h * HD:2 * (h + 1) * HD, c * HALF:(c + 1) * HALF],
                                            v[par][:, kt, h, :], pr[h][kt % 2][:, c * HALF:(c + 1) * HALF],
                                            start=kt == 0, stop=kt == KT - 1)
                if c == 1:
                    last.then_inc(s_pv, 1)

            for n in range(NM):
                rough(0, 0, n)
            row(0, 0)

            def step(i, par, nxt, far):
                p = 2 * i + par
                n = 0
                for kt in range(KT):
                    if kt + 1 < KT:
                        for h in range(2):
                            scores(p, par, kt + 1, h)
                    elif nxt:
                        row(*nxt)
                    for part in range(3):
                        if part:
                            products(p, par, kt, part - 1)
                        if part == 1 and nxt and kt == KT - 1:
                            for h in range(2):
                                scores(p + 1, nxt[1], 0, h)
                        for _ in range(MAXES[kt][part]):
                            if nxt:
                                rough(*nxt, n)
                            n += 1

            for h in range(2):
                scores(0, 0, 0, h)
            rounds_ahead(pe, NP, step)


def combine(nc, name, moved, x_in, xn_in, y, slot_in, gate_in, x_out):
    S = Space(nc, name)
    sb, sem = S.sb, S.sem
    with S.ctx:
        x = S.pair(sb, "x", [P, TJ, D])
        xn = S.pair(sb, "xn", [P, TJ, D])
        yg = S.pair(sb, "yg", [P, TJ, D])
        slot = S.pair(sb, "slot", [P, TJ], I32)
        gateh = S.pair(sb, "gateh", [P, TJ])
        s_meta = S.pair(sem, "s_meta")
        s_x = S.pair(sem, "s_x")
        s_yg = moved
        s_half = sem("s_half")
        s_x3 = sem("s_x3")
        s_stored = S.pair(sem, "s_stored")
        block = S.block()
        met = (s_meta[0], 32)

        def rows(ap, i, par):
            return tiles(ap[bass.ds((2 * i + par) * GROUP, GROUP), :])

        def meta(ap, i, par):
            return ap[bass.ds(2 * i + par, 1), :, :].rearrange("o p j -> (o p) j")

        @block.sync
        def _(sp):
            def load(i, par):
                work_out(sp, TJ * (2 * i + par - 1))
                if not isinstance(i, int):
                    sp.wait_ge(*met)
                sp.wait_ge(s_x3, past(TJ * (2 * i + par - 1)))
                sp.wait_ge(s_stored[par], 16 * i)
                sp.dma_start(slot[par][:, :], meta(slot_in, i, par)).then_inc(s_meta[par], 16)
                sp.dma_start(gateh[par][:, :], meta(gate_in, i, par)).then_inc(s_meta[par], 16)
                sp.dma_start(x[par][:, :, :], rows(x_in, i, par)).then_inc(s_x[par], 16)
                sp.dma_start(xn[par][:, :, :], rows(xn_in, i, par)).then_inc(s_x[par], 16)

            rounds(sp, NG, load)

        @block.gpsimd
        def _(pool):
            def gather(i, par):
                work_out(pool, 32 * (i + 1), TJ * (2 * i + par - 1))
                pool.wait_ge(*met)
                pool.wait_ge(s_meta[par], 32 * (i + 1))
                pool.wait_ge(s_x3, past(TJ * (2 * i + par - 1)))
                for j in range(TJ):
                    nc.gpsimd.indirect_dma_start(
                        out=yg[par][:, j, :], out_offset=None, in_=y,
                        in_offset=bass.IndirectOffsetOnAxis(ap=slot[par][:, j:j + 1], axis=0),
                        bounds_check=NOSLOT, oob_is_err=False).then_inc(s_yg[par], 16)

            rounds(pool, NG, gather)

        @block.vector
        def _(dve):
            def add(i, par):
                r = 2 * i + par
                dve.wait_ge(s_x[par], 32 * (i + 1))
                flat = x[par][:, :, :].rearrange("p j n -> p (j n)")
                nc.vector.scalar_tensor_tensor(flat, xn[par][:, :, :].rearrange("p j n -> p (j n)"), 0.5, flat,
                                               ALU.mult, ALU.add).then_inc(s_half, 1)
                dve.wait_ge(s_half, r + 1)
                dve.wait_ge(s_yg[par], 16 * TJ * (i + 1))
                for j in range(TJ):
                    nc.vector.scalar_tensor_tensor(x[par][:, j, :], yg[par][:, j, :], gateh[par][:, j:j + 1],
                                                   x[par][:, j, :], ALU.mult, ALU.add).then_inc(s_x3, 1)

            rounds(dve, NG, add)

        @block.scalar
        def _(act):
            def store(i, par):
                act.wait_ge(s_x3, TJ * (2 * i + par + 1))
                act.dma_start(rows(x_out, i, par), x[par][:, :, :]).then_inc(s_stored[par], 16)

            rounds(act, NG, store)
            for par in range(2):
                act.wait_ge(s_stored[par], 16 * (NG // 2))


def macaron(nc, x, wq, bq, wk, bk, wv, bv, wo, bo, w_router, w_gate, w_up, w_down,
            c_ident, c_tri, c_iota, c_tok, c_cos, c_sin, out):
    cst = {"ident": c_ident, "tri": c_tri, "iota": c_iota, "tok": c_tok, "cos": c_cos, "sin": c_sin}

    def dram(name, shape, dt=F32):
        return nc.dram_tensor(name, shape, dt, kind="Internal").ap()

    xn = [dram(f"xn{n}", [T + 1, D]) for n in range(2)]
    table = [dram(f"table{n}", [NOSLOT, 1], I32) for n in range(2)]
    y = [dram(f"y{n}", [NOSLOT + 1, D]) for n in range(2)]
    slot = [dram(f"slot{n}", [NG, P, TJ], I32) for n in range(2)]
    gate = [dram(f"gate{n}", [NG, P, TJ]) for n in range(2)]
    x1 = dram("x1", [T, D])
    x2 = dram("x2", [T, D])
    q = dram("q", [2, B, D, L])
    k = dram("k", [2, B, D, L])
    v = dram("v", [B, NH // 2, L, 4 * HD])
    ao = dram("ao", [B, D, L])
    sums = dram("sums", [B * NH, L])
    inverse = dram("inverse", [B, KD, P // HD, 1, L])

    def by_row(ap):
        return ap.rearrange("b d q -> (b d) q")

    moved = {n: [nc.alloc_semaphore(name=f"{n}_moved_{par}") for par in range(2)]
             for n in ("r1", "e1", "qkv", "r2", "e2", "c2")}
    route(nc, "r1", moved["r1"], x, w_router, cst, xn[0], table[0], y[0][NOSLOT:NOSLOT + 1, :], slot[0], gate[0])
    experts(nc, "e1", moved["e1"], xn[0], table[0], w_gate, w_up, w_down, cst, y[0])
    qkv(nc, "qkv", moved["qkv"], x, xn[0], y[0], slot[0], gate[0], (wq, wk, wv), (bq, bk, bv), cst, x1, q, k, v)
    attention(nc, "att", q.rearrange("s b d q -> s (b d) q"), k.rearrange("s b d q -> s (b d) q"),
              v.rearrange("b g t c -> (b g) t c"), cst, by_row(ao), sums)
    route(nc, "r2", moved["r2"], x1, w_router, cst, xn[1], table[1], y[1][NOSLOT:NOSLOT + 1, :], slot[1], gate[1],
          attn=(ao, sums, inverse, wo, bo, x2))
    experts(nc, "e2", moved["e2"], xn[1], table[1], w_gate, w_up, w_down, cst, y[1])
    combine(nc, "c2", moved["c2"], x2, xn[1], y[1], slot[1], gate[1], out)


def constants(np):
    inv = (np.float32(1.0) / np.float32(10000.0) ** (np.arange(0, HD, 2, dtype=np.float32) / np.float32(HD))).astype(np.float32)
    angle = np.arange(L, dtype=np.float32)[None, :] * np.tile(inv, 2 * P // HD)[:, None]
    sign = np.where(np.arange(P) % HD < HD // 2, np.float32(-1.0), np.float32(1.0))[:, None]
    t = np.arange(P)
    return {
        "c_ident": np.eye(P, dtype=np.float32),
        "c_tri": (t[:, None] <= t[None, :]).astype(np.float32),
        "c_iota": np.tile(np.arange(E, dtype=np.float32), (P, 1)),
        "c_tok": (t[:, None] + P * np.arange(TJ)[None, :]).astype(np.float32),
        "c_cos": np.cos(angle).astype(np.float32),
        "c_sin": (sign * np.sin(angle)).astype(np.float32),
    }


def kernel(**inputs):
    import numpy as np
    import concourse.bacc as bacc
    from concourse.bass_utils import run_bass_kernel_spmd

    def w(name, turned=False):
        a = inputs[name]
        return np.ascontiguousarray(np.asarray(a).T if turned else np.asarray(a))

    def by_tile(name):
        return np.ascontiguousarray(np.asarray(inputs[name]).reshape(KD, P).T)

    arrays = {
        "x": w("L0_attn_x").reshape(T, D),
        "wq": w("L0_attn_Wq", True), "bq": by_tile("L0_attn_bq"),
        "wk": w("L0_attn_Wk", True), "bk": by_tile("L0_attn_bk"),
        "wv": w("L0_attn_Wv", True), "bv": w("L0_attn_bv"),
        "wo": w("L0_attn_Wo", True), "bo": w("L0_attn_bo"),
        "w_router": w("L0_ffn_w_router"), "w_gate": w("L0_ffn_w_gate"),
        "w_up": w("L0_ffn_w_up"), "w_down": w("L0_ffn_w_down"),
        **constants(np),
    }
    nc = bacc.Bacc("TRN2", target_bir_lowering=False, num_devices=1)
    aps = {n: nc.dram_tensor(f"in_{n}", a.shape, mybir.dt.from_np(a.dtype), kind="ExternalInput").ap()
           for n, a in arrays.items()}
    out = nc.dram_tensor("out", (T, D), F32, kind="ExternalOutput").ap()
    macaron(nc, **aps, out=out)
    r = run_bass_kernel_spmd(nc, [{f"in_{n}": a for n, a in arrays.items()}], core_ids=[0])
    return r.results[0]["out"].reshape(B, L, D)
```

```python
import concourse.bass as bass
from concourse import mybir
from contextlib import ExitStack

F32 = mybir.dt.float32
F32R = mybir.dt.float32r
BF16 = mybir.dt.bfloat16
I32 = mybir.dt.int32
U32 = mybir.dt.uint32
ALU = mybir.AluOpType
ACT = mybir.ActivationFunctionType
AX = mybir.AxisListType

P = 128
B, L, D = 8, 1024, 512
T = B * L
NH, HD = 16, 32
E, F = 32, 512
C = (5 * T + 4 * E - 1) // (4 * E)
CT = (C + P - 1) // P
CW = 4 * (-(-C // (4 * CT)))
CP = CT * CW
NOSLOT = E * CP
KD = D // P
KF = F // P
TJ = 4
GROUP = TJ * P
NG = T // GROUP
EPS = 1e-5
BANK = 512


def past(count):
    return max(count, 0) if isinstance(count, int) else count


def work_out(eng, *counts):
    for count in counts:
        if not isinstance(count, int):
            eng.compute_val(count)


def rounds(eng, n, body):
    assert n % 2 == 0 and n >= 4
    body(0, 0)
    body(0, 1)
    if n > 4:
        with eng.Fori(1, n // 2 - 1) as i:
            body(i, 0)
            body(i, 1)
    body(n // 2 - 1, 0)
    body(n // 2 - 1, 1)


def after_first(i, par):
    return not isinstance(i, int) or 2 * i + par > 0


def rounds_ahead(eng, n, body):
    def pair(i, more=True):
        body(i, 0, (i, 1), (i + 1, 0) if more else None)
        body(i, 1, (i + 1, 0) if more else None, (i + 1, 1) if more else None)
    pair(0)
    with eng.Fori(1, n // 2 - 1) as i:
        pair(i)
    pair(n // 2 - 1, False)


def rounds_deep(eng, n, body):
    def pair(i, left=2):
        rs = [(i + k // 2, k % 2) if k // 2 <= left else None for k in range(6)]
        body(i, 0, rs[0:5])
        body(i, 1, rs[1:6])
    pair(0)
    with eng.Fori(1, n // 2 - 2) as i:
        pair(i)
    pair(n // 2 - 2, 1)
    pair(n // 2 - 1, 0)


def rounds_by(depth, eng, n, body):
    assert n % depth == 0 and n >= 2 * depth
    for b in range(depth):
        body(0, b, depth)
    with eng.Fori(1, n // depth - 1) as i:
        for b in range(depth):
            body(i, b, depth)
    for b in range(depth):
        body(n // depth - 1, b, depth - 1 - b)


class Chain:
    def __init__(self, sem, steps):
        self.sem, self.steps = sem, steps

    def start(self, eng, r):
        self.eng, self.r, self.k = eng, r, 0

    def link(self, ins):
        ins.then_inc(self.sem, 1)
        self.k += 1
        self.eng.wait_ge(self.sem, self.r * self.steps + self.k)

    def end(self):
        assert self.k == self.steps, self.k


class Space:
    def __init__(self, nc, name):
        self.nc, self.name, self.ctx, self.sems = nc, name, ExitStack(), []

    def sb(self, name, shape, dt=F32):
        return self.ctx.enter_context(self.nc.sbuf_tensor(f"{self.name}_{name}", shape, dt))

    def ps(self, name, shape, dt=F32):
        return self.ctx.enter_context(self.nc.psum_tensor(f"{self.name}_{name}", shape, dt))

    def bank(self, name, n):
        return self.ps(name, [P, BANK])[:, 0:n]

    def sem(self, name):
        self.sems.append(self.ctx.enter_context(self.nc.semaphore(f"{self.name}_{name}")))
        return self.sems[-1]

    def pair(self, make, name, *a):
        return [make(f"{name}_{i}", *a) for i in range(2)]

    def clear(self):
        nums = sorted(s.num for s in self.sems)
        lo = nums[0]
        for a, b in zip(nums, nums[1:] + [None]):
            if b != a + 1:
                self.nc.all_engine_barrier(sems_to_clear=range(lo, a + 1))
                lo = b

    def block(self):
        self.ctx.callback(self.clear)
        return self.ctx.enter_context(self.nc.Block())


def matmul3(nc, out, lhs, rhs, start, stop):
    nc.tensor.matmul(out, lhs[0], rhs[0], start=start, stop=False)
    nc.tensor.matmul(out, lhs[0], rhs[1], start=False, stop=False)
    return nc.tensor.matmul(out, lhs[1], rhs[0], start=False, stop=stop)


def tiles(ap):
    return ap.rearrange("(j p) n -> p j n", p=P)


def route(nc, name, moved, x_in, wr, cst, xn_out, table, y_zero, slot_out, gate_out, attn=None):
    S = Space(nc, name)
    sb, ps, sem = S.sb, S.ps, S.sem
    with S.ctx:
        ident = sb("ident", [P, P])
        trif = sb("trif", [P, P])
        tri = sb("tri", [P, P], BF16)
        ones = sb("ones", [P, P], BF16)
        iota = sb("iota", [P, E])
        tokf = sb("tokf", [P, TJ])
        wr_sb = sb("wr", [P, KD, E])
        unset = sb("unset", [P, NOSLOT // P], I32)
        zrow = sb("zrow", [1, D])
        eps = sb("eps", [P, 1])
        run = sb("run", [P, E], BF16)
        x = S.pair(sb, "x", [P, TJ, D])
        xn = S.pair(sb, "xn", [P, TJ, D])
        xnT = S.pair(sb, "xnT", [P, KD, P])
        stats = S.pair(sb, "stats", [P, 6])
        mv = sb("mv", [P, TJ, 2])
        std = sb("std", [P, TJ])
        rstd = sb("rstd", [P, TJ])
        top = sb("top", [P, TJ, 8])
        topi = sb("topi", [P, TJ, 8], U32)
        shifted = sb("shifted", [P, TJ, E])
        ex = sb("ex", [P, TJ, E])
        den = sb("den", [P, TJ])
        gate = sb("gate", [P, TJ])
        idxf = sb("idxf", [P, TJ])
        onehot = sb("onehot", [P, TJ, E], BF16)
        picked = sb("picked", [P, TJ, E])
        pos = sb("pos", [P, TJ])
        ok = sb("ok", [P, TJ])
        slot = sb("slot", [P, TJ])
        slot2 = sb("slot2", [P, TJ])
        seen = sb("seen", [P, E])
        slot_i = S.pair(sb, "slot_i", [P, TJ], I32)
        tok_i = S.pair(sb, "tok_i", [P, TJ], I32)
        gateh = S.pair(sb, "gateh", [P, TJ])
        tp = S.pair(ps, "tp", [P, KD, P])
        logits = S.bank("logits", TJ * E).rearrange("p (j e) -> p j e", e=E)
        posp = S.bank("posp", TJ * E).rearrange("p (j e) -> p j e", e=E)

        s_const = sem("s_const")
        s_memset = sem("s_memset")
        s_setup = sem("s_setup")
        s_unset = sem("s_unset")
        s_x = S.pair(sem, "s_x")
        s_stats = sem("s_stats")
        s_mv = sem("s_mv")
        s_std = sem("s_std")
        s_rstd = sem("s_rstd")
        s_xn = sem("s_xn")
        s_xn_stored = S.pair(sem, "s_xn_stored")
        s_tp = sem("s_tp")
        s_xnT = sem("s_xnT")
        s_logits = sem("s_logits")
        s_top = sem("s_top")
        s_shifted = sem("s_shifted")
        s_exp = sem("s_exp")
        s_onehot = sem("s_onehot")
        s_pos = sem("s_pos")
        s_slots = sem("s_slots")
        s_run = sem("s_run")
        s_scat = moved
        s_meta = S.pair(sem, "s_meta")
        pick = Chain(sem("s_pick"), 4)
        place = Chain(sem("s_place"), 8)
        n_const = 6
        if attn:
            ao_in, sums_in, inverse, woT, bo, x_out = attn
            bo_sb = sb("bo", [P, D])
            wraw = sb("wraw", [P, KD, D])
            wo = S.pair(sb, "wo", [P, KD, D], F32R)
            sums = sb("sums", [B * NH, L])
            aof = S.pair(sb, "aof", [P, KD, GROUP])
            inv = S.pair(sb, "inv", [P, KD, GROUP])
            s_sums = sem("s_sums")
            s_inv = sem("s_inv")
            s_inv_stored = sem("s_inv_stored")
            s_ao = sem("s_ao")
            ao = [S.pair(sb, f"ao{par}", [P, KD, GROUP], F32R) for par in range(2)]
            op = [ps(f"op{j}", [P, D]) for j in range(TJ)]
            s_ao_in = S.pair(sem, "s_ao_in")
            s_ao_hi = sem("s_ao_hi")
            s_ao_lo = sem("s_ao_lo")
            s_wo = sem("s_wo")
            s_xb = sem("s_xb")
            s_op = sem("s_op")
            s_x2 = sem("s_x2")
            s_x2_stored = S.pair(sem, "s_x2_stored")
            n_const = 8
        block = S.block()
        met = (s_const, 16 * n_const)

        def x_ap(ap, i, par):
            return tiles(ap[bass.ds((2 * i + par) * GROUP, GROUP), :])

        def ao_ap(ap, i, par):
            return ap[bass.ds(i, 1), :, par * GROUP:(par + 1) * GROUP].rearrange(
                "o (k p) q -> p (o k) q", p=P)

        @block.sync
        def _(sp):
            if attn:
                sp.dma_start(sums[:, :], sums_in).then_inc(s_sums, 16)
            sp.dma_start(ident[:, :], cst["ident"]).then_inc(s_const, 16)
            sp.dma_start(trif[:, :], cst["tri"]).then_inc(s_const, 16)
            sp.dma_start(iota[:, :], cst["iota"]).then_inc(s_const, 16)
            sp.dma_start(tokf[:, :], cst["tok"]).then_inc(s_const, 16)
            sp.dma_start(wr_sb[:, :, :], wr.rearrange("(k p) e -> p k e", p=P)).then_inc(s_const, 16)
            if attn:
                sp.dma_start(bo_sb[:, :], bo.rearrange("(o n) -> o n", o=1).broadcast_to([P, D])).then_inc(s_const, 16)
                sp.dma_start(wraw[:, :, :], woT.rearrange("(k p) n -> p k n", p=P)).then_inc(s_const, 16)
            sp.wait_ge(s_memset, 5)
            sp.dma_start(table[0:NOSLOT, :].rearrange("(p n) o -> p (n o)", p=P), unset[:, :]).then_inc(s_unset, 16)
            sp.dma_start(xn_out[T:T + 1, :], zrow[:, :]).then_inc(s_unset, 16)
            sp.dma_start(y_zero, zrow[:, :]).then_inc(s_const, 16)

            def load(i, par):
                if attn:
                    work_out(sp, 16 * i)
                    sp.wait_ge(*met)
                    sp.wait_ge(s_x2_stored[par], 16 * i)
                sp.wait_ge(s_xn, past(TJ * (2 * i + par - 1)))
                sp.dma_start(x[par][:, :, :], x_ap(x_in, i, par)).then_inc(s_x[par], 16)

            def load_ao(i, par):
                sp.wait_ge(s_ao_lo, past(2 * i + par - 1))
                sp.dma_start(aof[par][:, :, :], ao_ap(ao_in, i, par)).then_inc(s_ao_in[par], 16)

            def load_inv(i, par):
                sp.wait_ge(s_ao_lo, past(2 * i + par - 1))
                for h in range(P // HD):
                    sp.dma_start(inv[par][h * HD:(h + 1) * HD, :, :],
                                 inverse[bass.ds(i, 1), :, h, :, par * GROUP:(par + 1) * GROUP].rearrange(
                                     "b k o q -> (b o) k q").broadcast_to([HD, KD, GROUP])).then_inc(s_ao_in[par], 16)

            def store_x2(i, par):
                sp.wait_ge(s_x2, TJ * (2 * i + par + 1))
                sp.dma_start(x_ap(x_out, i, par), x[par][:, :, :]).then_inc(s_x2_stored[par], 16)

            def store_xn(i, par):
                sp.wait_ge(s_xn, TJ * (2 * i + par + 1))
                sp.dma_start(x_ap(xn_out, i, par), xn[par][:, :, :]).then_inc(s_xn_stored[par], 16)

            def step(i, par, ahead):
                if attn and ahead[4]:
                    load_ao(*ahead[4])
                    load_inv(*ahead[4])
                if attn and ahead[1]:
                    store_xn(*ahead[1])
                if ahead[3]:
                    load(*ahead[3])
                if ahead[2]:
                    (store_x2 if attn else store_xn)(*ahead[2])

            if attn:
                load_ao(0, 0)
                sp.wait_ge(s_inv, 1)
                sp.dma_start(inverse.rearrange("b k h o q -> (b k h o) q"), sums[:, :]).then_inc(s_inv_stored, 16)
            load(0, 0)
            if attn:
                sp.wait_ge(s_inv_stored, 16)
                load_inv(0, 0)
                load_ao(0, 1)
                load_inv(0, 1)
            load(0, 1)
            if attn:
                for par in range(2):
                    load_ao(1, par)
                    load_inv(1, par)
                store_x2(0, 0)
            store_xn(0, 0)
            load(1, 0)
            (store_x2 if attn else store_xn)(0, 1)
            rounds_deep(sp, NG, step)
            for par in range(2):
                sp.wait_ge(s_xn_stored[par], 16 * (NG // 2))
                if attn:
                    sp.wait_ge(s_x2_stored[par], 16 * (NG // 2))
            sp.wait_ge(s_const, 16 * n_const)
            sp.wait_ge(s_unset, 32)

        @block.gpsimd
        def _(pool):
            nc.gpsimd.memset(ones[:, :], 1.0).then_inc(s_memset, 1)
            nc.gpsimd.memset(unset[:, :], T).then_inc(s_memset, 1)
            nc.gpsimd.memset(zrow[:, :], 0.0).then_inc(s_memset, 1)
            nc.gpsimd.memset(eps[:, :], EPS).then_inc(s_memset, 1)
            nc.gpsimd.memset(run[:, :], 0.0).then_inc(s_memset, 1)
            pool.wait_ge(s_unset, 32)

            def divide(i, par):
                pool.wait_ge(s_ao_in[par], 16 * (1 + P // HD) * (i + 1))
                nc.gpsimd.tensor_tensor(out=aof[par][:, :, :], in0=aof[par][:, :, :], in1=inv[par][:, :, :],
                                        op=ALU.mult).then_inc(s_ao, 1)

            def lo_ao(i, par):
                pool.wait_ge(s_ao_hi, 2 * i + par + 1)
                nc.gpsimd.tensor_tensor(out=ao[par][1][:, :, :], in0=aof[par][:, :, :],
                                        in1=ao[par][0][:, :, :].bitcast(F32), op=ALU.subtract).then_inc(s_ao_lo, 1)

            def scatter(r, par):
                work_out(pool, r + 1)
                pool.wait_ge(*met)
                pool.wait_ge(s_slots, r + 1)
                for j in range(TJ):
                    nc.gpsimd.indirect_dma_start(
                        out=table[0:NOSLOT, :], out_offset=bass.IndirectOffsetOnAxis(ap=slot_i[par][:, j:j + 1], axis=0),
                        in_=tok_i[par][:, j:j + 1], in_offset=None,
                        bounds_check=NOSLOT - 1, oob_is_err=False).then_inc(s_scat[par], 16)

            def step(i, par, ahead):
                if attn and ahead[3]:
                    divide(*ahead[3])
                if after_first(i, par):
                    scatter(2 * i + par - 1, 1 - par)
                if attn and ahead[3]:
                    lo_ao(*ahead[3])

            if attn:
                pool.wait_ge(s_const, 16 * n_const)
                for i, par in ((0, 0), (0, 1), (1, 0)):
                    divide(i, par)
                    lo_ao(i, par)
            rounds_deep(pool, NG, step)
            scatter(NG - 1, 1)
            for par in range(2):
                pool.wait_ge(s_scat[par], 16 * TJ * (NG // 2))

        @block.scalar
        def _(act):
            act.wait_ge(s_memset, 5)

            def norm(i, par):
                r = 2 * i + par
                act.wait_ge(s_mv, TJ * (r + 1))
                nc.scalar.activation(std[:, :], mv[:, :, 1], ACT.Sqrt, bias=eps[:, 0:1]).then_inc(s_std, 1)

            def copies(i, par, js):
                for j in js:
                    n = TJ * (2 * i + par) + j
                    act.wait_ge(s_tp, n + 1)
                    act.wait_ge(s_logits, past(n - 1))
                    nc.scalar.activation(xnT[j % 2][:, :, :], tp[j % 2][:, :, :], ACT.Copy).then_inc(s_xnT, 1)

            def exps(i, par):
                r = 2 * i + par
                act.wait_ge(s_shifted, r + 1)
                act.wait_ge(pick.sem, pick.steps * r)
                nc.scalar.activation(ex[:, :, :], shifted[:, :, :], ACT.Exp).then_inc(s_exp, 1)

            def hi_ao(i, par):
                act.wait_ge(s_ao, 2 * i + par + 1)
                act.wait_ge(s_op, past(TJ * (2 * i + par - 1)))
                nc.scalar.activation(ao[par][0][:, :, :], aof[par][:, :, :], ACT.Copy).then_inc(s_ao_hi, 1)

            def meta(r, par):
                work_out(act, r + 1)
                act.wait_ge(*met)
                act.wait_ge(s_slots, r + 1)
                act.dma_start(slot_out[bass.ds(r, 1), :, :].rearrange("o p j -> (o p) j"),
                              slot_i[par][:, :]).then_inc(s_meta[par], 16)
                act.dma_start(gate_out[bass.ds(r, 1), :, :].rearrange("o p j -> (o p) j"),
                              gateh[par][:, :]).then_inc(s_meta[par], 16)

            def step(i, par, ahead):
                if after_first(i, par):
                    meta(2 * i + par - 1, 1 - par)
                exps(i, par)
                if ahead[1]:
                    copies(*ahead[1], (0, 1))
                if attn and ahead[3]:
                    hi_ao(*ahead[3])
                if ahead[2] and not attn:
                    norm(*ahead[2])
                if ahead[1]:
                    copies(*ahead[1], (2, 3))
                if ahead[2] and attn:
                    norm(*ahead[2])

            if attn:
                hi_ao(0, 0)
                hi_ao(0, 1)
            norm(0, 0)
            norm(0, 1)
            if attn:
                hi_ao(1, 0)
            copies(0, 0, range(TJ))
            rounds_deep(act, NG, step)
            meta(NG - 1, 1)
            for par in range(2):
                act.wait_ge(s_meta[par], 32 * (NG // 2))

        @block.vector
        def _(dve):
            if attn:
                dve.wait_ge(s_sums, 16)
                nc.vector.reciprocal(sums[:, :], sums[:, :]).then_inc(s_inv, 1)
            dve.wait_ge(s_const, 16 * n_const)
            dve.wait_ge(s_memset, 5)
            nc.vector.tensor_copy(tri[:, :], trif[:, :]).then_inc(s_setup, 1)
            if attn:
                nc.vector.tensor_copy(wo[0][:, :, :], wraw[:, :, :]).then_inc(s_wo, 1)
                dve.wait_ge(s_wo, 1)
                nc.vector.tensor_tensor(out=wo[1][:, :, :], in0=wraw[:, :, :], in1=wo[0][:, :, :].bitcast(F32),
                                        op=ALU.subtract).then_inc(s_wo, 1)

            def bias(i, par):
                dve.wait_ge(s_x[par], 16 * (i + 1))
                nc.vector.tensor_tensor(out=x[par][:, :, :], in0=x[par][:, :, :],
                                        in1=bo_sb[:, :].unsqueeze(1).broadcast_to([P, TJ, D]),
                                        op=ALU.add).then_inc(s_xb, 1)

            def measure(i, par, js):
                r = 2 * i + par
                dve.wait_ge(s_x[par], 16 * (i + 1))
                if attn:
                    dve.wait_ge(s_xb, r + 1)
                for j in js:
                    n = TJ * r + j
                    if attn:
                        dve.wait_ge(s_op, n + 1)
                        nc.vector.tensor_tensor(out=x[par][:, j, :], in0=x[par][:, j, :], in1=op[j][:, :],
                                                op=ALU.add).then_inc(s_x2, 1)
                        dve.wait_ge(s_x2, n + 1)
                    dve.wait_ge(s_mv, past(n - 1))
                    nc.vector.bn_stats(stats[j % 2][:, :], x[par][:, j, :]).then_inc(s_stats, 1)
                    work_out(dve, n + 1, r, TJ * r)
                    dve.wait_ge(*met)
                    dve.wait_ge(s_stats, n + 1)
                    dve.wait_ge(s_std, r)
                    dve.wait_ge(s_xn, TJ * r)
                    nc.vector.bn_aggr(mv[:, j, :], stats[j % 2][:, :]).then_inc(s_mv, 1)

            def normalise(i, par):
                r = 2 * i + par
                dve.wait_ge(s_std, r + 1)
                dve.wait_ge(s_mv, TJ * (r + 1))
                nc.vector.reciprocal(rstd[:, :], std[:, :]).then_inc(s_rstd, 1)
                dve.wait_ge(s_rstd, r + 1)
                dve.wait_ge(s_xn_stored[par], 16 * i)
                dve.wait_ge(s_tp, past(TJ * r - TJ))
                for j in range(TJ):
                    nc.vector.tensor_scalar(xn[par][:, j, :], x[par][:, j, :], mv[:, j, 0:1], rstd[:, j:j + 1],
                                            ALU.subtract, ALU.mult).then_inc(s_xn, 1)

            def choose(i, par):
                r = 2 * i + par
                work_out(dve, TJ * (r + 1))
                dve.wait_ge(*met)
                dve.wait_ge(s_logits, TJ * (r + 1))
                for j in range(TJ):
                    nc.vector.max(top[:, j, :], logits[:, j, :]).then_inc(s_top, 1)
                work_out(dve, 2 * TJ * r + TJ)
                dve.wait_ge(*met)
                dve.wait_ge(s_top, 2 * TJ * r + TJ)
                for j in range(TJ):
                    nc.vector.max_index(topi[:, j, :], top[:, j, :], logits[:, j, :]).then_inc(s_top, 1)
                nc.vector.tensor_tensor(out=shifted[:, :, :], in0=logits[:, :, :],
                                        in1=top[:, :, 0:1].broadcast_to([P, TJ, E]),
                                        op=ALU.subtract).then_inc(s_shifted, 1)
                dve.wait_ge(s_top, 2 * TJ * (r + 1))
                dve.wait_ge(s_shifted, r + 1)
                pick.start(dve, r)
                pick.link(nc.vector.tensor_copy(idxf[:, :], topi[:, :, 0]))
                dve.wait_ge(s_pos, r)
                nc.vector.tensor_tensor(out=onehot[:, :, :], in0=iota[:, :].unsqueeze(1).broadcast_to([P, TJ, E]),
                                        in1=idxf[:, :].unsqueeze(2).broadcast_to([P, TJ, E]),
                                        op=ALU.is_equal).then_inc(s_onehot, 1)

            def gates(i, par):
                r = 2 * i + par
                dve.wait_ge(s_exp, r + 1)
                pick.link(nc.vector.tensor_reduce(out=den[:, :], in_=ex[:, :, :], axis=AX.X, op=ALU.add))
                pick.link(nc.vector.reciprocal(gate[:, :], den[:, :]))
                dve.wait_ge(s_onehot, r + 1)
                pick.link(nc.vector.tensor_reduce(out=seen[:, :], in_=onehot[:, :, :].rearrange("p j e -> p e j"),
                                                  axis=AX.X, op=ALU.add))

            def slots(i, par):
                r = 2 * i + par
                dve.wait_ge(s_pos, r + 1)
                nc.vector.tensor_tensor(out=run[:, :], in0=run[:, :], in1=seen[:, :], op=ALU.add).then_inc(s_run, 1)
                place.start(dve, r)
                place.link(nc.vector.tensor_tensor(out=picked[:, :, :], in0=posp[:, :, :], in1=onehot[:, :, :],
                                                   op=ALU.mult))
                place.link(nc.vector.tensor_reduce(out=pos[:, :], in_=picked[:, :, :], axis=AX.X, op=ALU.add))
                place.link(nc.vector.tensor_scalar(ok[:, :], pos[:, :], float(C), None, ALU.is_le))
                place.link(nc.vector.scalar_tensor_tensor(slot[:, :], idxf[:, :], float(CP), pos[:, :],
                                                          ALU.mult, ALU.add))
                place.link(nc.vector.scalar_tensor_tensor(slot2[:, :], slot[:, :], -1.0 - NOSLOT, ok[:, :],
                                                          ALU.add, ALU.mult))
                dve.wait_ge(s_scat[par], 16 * TJ * i)
                dve.wait_ge(s_meta[par], 32 * i)
                place.link(nc.vector.tensor_scalar(slot_i[par][:, :], slot2[:, :], float(NOSLOT), None, ALU.add))
                place.link(nc.vector.tensor_copy(tok_i[par][:, :], tokf[:, :]))
                place.link(nc.vector.tensor_scalar(tokf[:, :], tokf[:, :], float(GROUP), None, ALU.add))
                nc.vector.scalar_tensor_tensor(gateh[par][:, :], gate[:, :], 0.5, ok[:, :],
                                               ALU.mult, ALU.mult).then_inc(s_slots, 1)
                work_out(dve, r + 1, r + 1)
                dve.wait_ge(*met)
                dve.wait_ge(s_slots, r + 1)
                dve.wait_ge(s_run, r + 1)

            def step(i, par, ahead):
                if attn and ahead[1]:
                    normalise(*ahead[1])
                choose(i, par)
                if attn:
                    gates(i, par)
                    if ahead[2]:
                        bias(*ahead[2])
                        measure(*ahead[2], (0, 1))
                    slots(i, par)
                    if ahead[2]:
                        measure(*ahead[2], (2, 3))
                else:
                    if ahead[2]:
                        measure(*ahead[2], (0, 1))
                    gates(i, par)
                    if ahead[2]:
                        measure(*ahead[2], (2, 3))
                    slots(i, par)
                    if ahead[2]:
                        normalise(*ahead[2])

            for par in range(2):
                if attn:
                    bias(0, par)
                measure(0, par, range(TJ))
                if not attn or par == 0:
                    normalise(0, par)
            rounds_deep(dve, NG, step)

        @block.tensor
        def _(pe):
            pe.wait_ge(s_const, 16 * n_const)
            pe.wait_ge(s_memset, 5)
            pe.wait_ge(s_setup, 1)
            if attn:
                pe.wait_ge(s_wo, 2)

            def project(i, par, j):
                r = 2 * i + par
                n = TJ * r + j
                pe.wait_ge(s_ao_lo, r + 1)
                pe.wait_ge(s_x2, past(n - TJ + 1))
                for k in range(KD):
                    last = matmul3(nc, op[j][:, :], [a[:, k, j * P:(j + 1) * P] for a in ao[par]],
                                   [w[:, k, :] for w in wo], k == 0, k == KD - 1)
                last.then_inc(s_op, 1)

            def turn(i, par, j):
                n = TJ * (2 * i + par) + j
                pe.wait_ge(s_xn, n + 1)
                pe.wait_ge(s_xnT, past(n - 1))
                for k in range(KD):
                    last = nc.tensor.transpose(tp[j % 2][:, k, :], xn[par][:, j, k * P:(k + 1) * P], ident[:, :])
                last.then_inc(s_tp, 1)

            def products(i, par, j):
                r = 2 * i + par
                pe.wait_ge(s_xnT, TJ * r + j + 1)
                pe.wait_ge(s_shifted, r)
                pe.wait_ge(s_top, 2 * TJ * r)
                for k in range(KD):
                    last = nc.tensor.matmul(logits[:, j, :], xnT[j % 2][:, k, :], wr_sb[:, k, :],
                                            start=k == 0, stop=k == KD - 1)
                last.then_inc(s_logits, 1)

            def positions(i, par):
                r = 2 * i + par
                pe.wait_ge(s_onehot, r + 1)
                pe.wait_ge(s_run, r)
                pe.wait_ge(s_slots, r)
                for j in range(TJ):
                    nc.tensor.matmul(posp[:, j, :], tri[:, :], onehot[:, j, :], start=True, stop=False)
                    for before in range(j):
                        nc.tensor.matmul(posp[:, j, :], ones[:, :], onehot[:, before, :], start=False, stop=False)
                    last = nc.tensor.matmul(posp[:, j, :], ones[:, :], run[:, :], start=False, stop=True)
                last.then_inc(s_pos, 1)

            def step(i, par, ahead):
                for j in range(TJ + 1):
                    if attn and ahead[2] and j < TJ:
                        project(*ahead[2], j)
                    if ahead[1] and j < TJ:
                        turn(*ahead[1], j)
                    if j == (1 if attn else 0):
                        positions(i, par)
                    if ahead[1] and j > 0:
                        products(*ahead[1], j - 1)

            if attn:
                for par in range(2):
                    for j in range(TJ):
                        project(0, par, j)
            for j in range(TJ + 1):
                if j < TJ:
                    turn(0, 0, j)
                if j > 0:
                    products(0, 0, j - 1)
            rounds_deep(pe, NG, step)


def experts(nc, name, moved, xn, table, wg, wu, wd, cst, y_out):
    S = Space(nc, name)
    sb, ps, sem = S.sb, S.ps, S.sem
    with S.ctx:
        ident = sb("ident", [P, P])
        raw = [S.pair(sb, f"raw{w}", [P, KD, F]) for w in range(3)]
        split = [[S.pair(sb, f"w{w}_{par}", [P, KD, F], F32R) for par in range(2)] for w in range(3)]
        idx = S.pair(sb, "idx", [CW, CT], I32)
        xg = S.pair(sb, "xg", [CW, CT, D])
        xT = S.pair(sb, "xT", [P, KD, CP], F32R)
        sg = S.pair(sb, "sg", [P, CP])
        af = S.pair(sb, "af", [P, CP])
        aT = S.pair(sb, "aT", [P, KF, CP], F32R)
        y = sb("y", [CW, CT, D])
        tp = S.pair(S.bank, "tp", CP)
        gp = S.pair(S.bank, "gp", CP)
        up = S.pair(S.bank, "up", CP)
        yp = S.pair(ps, "yp", [CW, D])

        s_const = sem("s_const")
        s_raw = [S.pair(sem, f"s_raw{w}") for w in range(3)]
        s_hi = sem("s_hi")
        s_lo = sem("s_lo")
        s_idx = S.pair(sem, "s_idx")
        s_xg = moved
        s_tp = sem("s_tp")
        s_xh = sem("s_xh")
        s_xl = sem("s_xl")
        s_gu = sem("s_gu")
        s_sg = sem("s_sg")
        s_af = sem("s_af")
        s_ah = sem("s_ah")
        s_al = sem("s_al")
        s_y = sem("s_y")
        s_yc = sem("s_yc")
        s_stored = sem("s_stored")
        block = S.block()
        met = (s_const, 16)
        weights = [wg, wu, wd]

        def w_ap(w, e):
            return weights[w][bass.ds(e, 1), :, :].rearrange("o (k p) f -> p (o k) f", p=P)

        def load_raw(sp, i, par):
            e = 2 * i + par
            for w in range(3):
                sp.wait_ge(s_hi, past(3 * (e - 2) + w + 1))
                sp.wait_ge(s_lo, past(3 * (e - 2) + w + 1))
                sp.dma_start(raw[w][par][:, :, :], w_ap(w, e)).then_inc(s_raw[w][par], 16)

        @block.sync
        def _(sp):
            sp.dma_start(ident[:, :], cst["ident"]).then_inc(s_const, 16)

            def load_idx(i, par):
                sp.wait_ge(s_xg[par], 16 * CT * i)
                sp.dma_start(idx[par][:, :], table[bass.ds((2 * i + par) * CP, CP), :].rearrange(
                    "(p c) o -> p (c o)", p=CW)).then_inc(s_idx[par], 16)

            def store(i, par):
                e = 2 * i + par
                sp.wait_ge(s_yc, CT * (e + 1))
                sp.dma_start(y_out[bass.ds(e * CP, CP), :].rearrange("(p c) n -> p (c n)", p=CW),
                             y[:, :, :].rearrange("p c n -> p (c n)")).then_inc(s_stored, 16)

            def step(i, par, nxt, far):
                if far:
                    load_idx(*far)
                    load_raw(sp, *far)
                store(i, par)

            load_idx(0, 0)
            load_idx(0, 1)
            load_raw(sp, 0, 0)
            sp.wait_ge(s_xg[0], 16 * CT)
            load_raw(sp, 0, 1)
            rounds_ahead(sp, E, step)
            sp.wait_ge(s_stored, 16 * E)

        @block.gpsimd
        def _(pool):
            def gather(i, par):
                work_out(pool, 16 * (i + 1), KD * (2 * i + par - 1))
                pool.wait_ge(*met)
                pool.wait_ge(s_idx[par], 16 * (i + 1))
                pool.wait_ge(s_tp, past(KD * (2 * i + par - 1)))
                for c in range(CT):
                    nc.gpsimd.indirect_dma_start(
                        out=xg[par][:, c, :], out_offset=None, in_=xn,
                        in_offset=bass.IndirectOffsetOnAxis(ap=idx[par][:, c:c + 1], axis=0),
                        bounds_check=T, oob_is_err=False).then_inc(s_xg[par], 16)

            rounds(pool, E, gather)

        def hi_weight(act, w, i, par):
            e = 2 * i + par
            act.wait_ge(s_raw[w][par], 16 * (i + 1))
            act.wait_ge(s_gu, past(KF * (e - 1)))
            act.wait_ge(s_y, past(CT * (e - 1)))
            nc.scalar.activation(split[w][par][0][:, :, :], raw[w][par][:, :, :], ACT.Copy).then_inc(s_hi, 1)

        def lo_weight(dve, w, i, par):
            e = 2 * i + par
            dve.wait_ge(s_hi, 3 * e + w + 1)
            nc.vector.tensor_tensor(out=split[w][par][1][:, :, :], in0=raw[w][par][:, :, :],
                                    in1=split[w][par][0][:, :, :].bitcast(F32), op=ALU.subtract).then_inc(s_lo, 1)

        @block.scalar
        def _(act):
            def hi_x(i, par, k):
                e = 2 * i + par
                act.wait_ge(s_tp, KD * e + k + 1)
                act.wait_ge(s_gu, KF * e)
                nc.scalar.activation(xT[0][:, k, :], tp[k % 2][:, :], ACT.Copy).then_inc(s_xh, 1)

            def store_y(i, par, c):
                e = 2 * i + par
                act.wait_ge(s_y, CT * e + c + 1)
                act.wait_ge(s_stored, 16 * e)
                nc.scalar.activation(y[:, c, :], yp[c % 2][:, :], ACT.Copy).then_inc(s_yc, 1)

            def step(i, par, nxt, far):
                e = 2 * i + par
                for f in range(KF):
                    n = KF * e + f
                    act.wait_ge(s_gu, n + 1)
                    act.wait_ge(s_af, past(n - 1))
                    nc.scalar.activation(sg[f % 2][:, :], gp[f % 2][:, :], ACT.Silu).then_inc(s_sg, 1)
                    if nxt and f < 2:
                        hi_weight(act, f, *nxt)
                if nxt:
                    hi_x(*nxt, 0)
                    hi_x(*nxt, 1)
                for c in range(CT):
                    store_y(i, par, c)
                    if nxt and c + 2 < KD:
                        hi_x(*nxt, c + 2)
                if nxt:
                    hi_weight(act, 2, *nxt)

            for w in range(3):
                hi_weight(act, w, 0, 0)
            for k in range(KD):
                hi_x(0, 0, k)
            rounds_ahead(act, E, step)

        @block.vector
        def _(dve):
            def lo_x(i, par):
                e = 2 * i + par
                for k in range(KD):
                    dve.wait_ge(s_xh, KD * e + k + 1)
                    nc.vector.tensor_tensor(out=xT[1][:, k, :], in0=tp[k % 2][:, :],
                                            in1=xT[0][:, k, :].bitcast(F32), op=ALU.subtract).then_inc(s_xl, 1)

            def step(i, par, nxt, far):
                e = 2 * i + par
                for f in range(KF):
                    n = KF * e + f
                    dve.wait_ge(s_sg, n + 1)
                    dve.wait_ge(s_al, past(n - 1))
                    nc.vector.tensor_tensor(out=af[f % 2][:, :], in0=up[f % 2][:, :], in1=sg[f % 2][:, :],
                                            op=ALU.mult).then_inc(s_af, 1)
                    dve.wait_ge(s_af, n + 1)
                    dve.wait_ge(s_y, CT * e)
                    nc.vector.tensor_copy(aT[0][:, f, :], af[f % 2][:, :]).then_inc(s_ah, 1)
                    dve.wait_ge(s_ah, n + 1)
                    nc.vector.tensor_tensor(out=aT[1][:, f, :], in0=af[f % 2][:, :],
                                            in1=aT[0][:, f, :].bitcast(F32), op=ALU.subtract).then_inc(s_al, 1)
                    if nxt and f < 2:
                        lo_weight(dve, f, *nxt)
                if nxt:
                    lo_x(*nxt)
                    lo_weight(dve, 2, *nxt)

            for w in range(3):
                lo_weight(dve, w, 0, 0)
            lo_x(0, 0)
            rounds_ahead(dve, E, step)

        @block.tensor
        def _(pe):
            pe.wait_ge(s_const, 16)

            def turn(i, par, k):
                e = 2 * i + par
                pe.wait_ge(s_xg[par], 16 * CT * (i + 1))
                pe.wait_ge(s_xl, past(KD * e + k - 1))
                for c in range(CT):
                    last = nc.tensor.transpose(tp[k % 2][:, c * CW:(c + 1) * CW],
                                               xg[par][:, c, k * P:(k + 1) * P],
                                               ident[0:CW, 0:CW])
                last.then_inc(s_tp, 1)

            def gate_up(i, par):
                e = 2 * i + par
                pe.wait_ge(s_lo, 3 * e + 2)
                for f in range(KF):
                    n = KF * e + f
                    pe.wait_ge(s_af, past(n - 1))
                    for w, out in ((0, gp), (1, up)):
                        for k in range(KD):
                            if f == 0 and w == 0:
                                pe.wait_ge(s_xl, KD * e + k + 1)
                            last = matmul3(nc, out[f % 2][:, :],
                                           [s[:, k, f * P:(f + 1) * P] for s in split[w][par]],
                                           [s[:, k, :] for s in xT], k == 0, k == KD - 1)
                    last.then_inc(s_gu, 1)

            def down(i, par, c):
                e = 2 * i + par
                n = CT * e + c
                if c == 0:
                    pe.wait_ge(s_lo, 3 * e + 3)
                pe.wait_ge(s_yc, past(n - 1))
                for f in range(KF):
                    if c == 0:
                        pe.wait_ge(s_al, KF * e + f + 1)
                    last = matmul3(nc, yp[c % 2][:, :],
                                   [a[:, f, c * CW:(c + 1) * CW] for a in aT],
                                   [s[:, f, :] for s in split[2][par]], f == 0, f == KF - 1)
                last.then_inc(s_y, 1)

            def step(i, par, nxt, far):
                if nxt:
                    turn(*nxt, 0)
                    turn(*nxt, 1)
                for c in range(CT):
                    down(i, par, c)
                    if nxt and c + 2 < KD:
                        turn(*nxt, c + 2)
                if nxt:
                    gate_up(*nxt)

            for k in range(KD):
                turn(0, 0, k)
            gate_up(0, 0)
            rounds_ahead(pe, E, step)


def qkv(nc, name, moved, x_in, xn_in, y, slot_in, gate_in, wT, bias, cst, x_out, q_out, k_out, v_out):
    S = Space(nc, name)
    sb, ps, sem = S.sb, S.ps, S.sem
    NB = 4
    with S.ctx:
        ident = sb("ident", [P, P])
        eps = sb("eps", [P, 1])
        cos = sb("cos", [P, L])
        sin = sb("sin", [P, L])
        w = [S.pair(sb, f"w{m}", [P, KD, D], F32R) for m in range(3)]
        bqk = [sb(f"b{m}", [P, KD]) for m in range(2)]
        bv = sb("bv", [P, D])
        x = S.pair(sb, "x", [P, TJ, D])
        xn = sb("xn", [P, TJ, D])
        yg = sb("yg", [P, TJ, D])
        xa = sb("xa", [P, TJ, D])
        spare = sb("spare", [P, KD, D])
        wraw = [spare, xa, x[1]]
        slot = S.pair(sb, "slot", [P, TJ], I32)
        gateh = S.pair(sb, "gateh", [P, TJ])
        stats = S.pair(sb, "stats", [P, 6])
        mv = sb("mv", [P, TJ, 2])
        std = sb("std", [P, TJ])
        rstd = sb("rstd", [P, TJ])
        xT = [S.pair(sb, f"xT{par}", [P, KD, GROUP], F32R) for par in range(2)]
        qb = [sb(f"qb{t}", [P, GROUP]) for t in range(NB)]
        qs = [sb(f"qs{t}", [P, GROUP]) for t in range(NB)]
        qc = [sb(f"qc{t}", [P, GROUP]) for t in range(NB)]
        qh = [sb(f"qh{t}", [P, GROUP], F32R) for t in range(NB)]
        ql = [sb(f"ql{t}", [P, GROUP], F32R) for t in range(NB)]
        v = [sb(f"v{j}", [P, NH, 2 * HD]) for j in range(TJ)]
        tp = S.pair(ps, "tp", [P, KD, P])
        pp = [ps(f"pp{t}", [P, GROUP]) for t in range(NB)]
        vp = S.pair(ps, "vp", [P, D])

        s_const = sem("s_const")
        s_wraw = [sem(f"s_wraw{m}") for m in range(3)]
        s_wh = sem("s_wh")
        s_w = sem("s_w")
        s_memset = sem("s_memset")
        s_x = S.pair(sem, "s_x")
        s_xn_in = sem("s_xn_in")
        s_meta = S.pair(sem, "s_meta")
        s_yg = moved[0]
        s_half = sem("s_half")
        s_x1 = sem("s_x1")
        s_x1_stored = S.pair(sem, "s_x1_stored")
        s_stats = sem("s_stats")
        s_mv = sem("s_mv")
        s_std = sem("s_std")
        s_rstd = sem("s_rstd")
        s_xa = sem("s_xa")
        s_tp = sem("s_tp")
        s_xh = sem("s_xh")
        s_xl = sem("s_xl")
        s_pp = sem("s_pp")
        s_qb = sem("s_qb")
        s_qs = sem("s_qs")
        s_qc = sem("s_qc")
        s_rot = sem("s_rot")
        s_qh = sem("s_qh")
        s_ql = sem("s_ql")
        s_q_stored = [sem(f"s_q_stored{t}") for t in range(NB)]
        s_vp = sem("s_vp")
        s_v = sem("s_v")
        s_v_stored = [sem(f"s_v_stored{j}") for j in range(TJ)]
        block = S.block()
        met = (s_const, 96)
        NQ = 2 * KD
        SWAP = [(d + HD // 2) % HD for d in range(HD)]

        def rows(ap, i, par):
            return tiles(ap[bass.ds((2 * i + par) * GROUP, GROUP), :])

        def meta(ap, i, par):
            return ap[bass.ds(2 * i + par, 1), :, :].rearrange("o p j -> (o p) j")

        @block.sync
        def _(sp):
            for dst, src in ((ident, cst["ident"]), (cos, cst["cos"]), (sin, cst["sin"])):
                sp.dma_start(dst[:, :], src).then_inc(s_const, 16)
            for m in range(2):
                sp.dma_start(bqk[m][:, :], bias[m]).then_inc(s_const, 16)
            sp.dma_start(bv[:, :], bias[2].rearrange("(o n) -> o n", o=1).broadcast_to([P, D])).then_inc(s_const, 16)

            def load(i, par):
                r = 2 * i + par
                work_out(sp, 16 * TJ * (r - 1))
                sp.wait_ge(*met)
                sp.wait_ge(s_yg, past(16 * TJ * (r - 1)))
                sp.wait_ge(s_x1, past(TJ * (r - 1)))
                sp.dma_start(slot[par][:, :], meta(slot_in, i, par)).then_inc(s_meta[par], 16)
                sp.dma_start(gateh[par][:, :], meta(gate_in, i, par)).then_inc(s_meta[par], 16)
                sp.wait_ge(s_x1_stored[par], 16 * i)
                sp.wait_ge(s_xa, past(TJ * (r - 1)))
                sp.dma_start(x[par][:, :, :], rows(x_in, i, par)).then_inc(s_x[par], 16)

            def load_xn(i, par):
                sp.wait_ge(s_half, 2 * i + par)
                sp.dma_start(xn[:, :, :], rows(xn_in, i, par)).then_inc(s_xn_in, 16)

            def store_x(i, par):
                sp.wait_ge(s_x1, TJ * (2 * i + par + 1))
                sp.dma_start(rows(x_out, i, par), x[par][:, :, :]).then_inc(s_x1_stored[par], 16)

            def store_q(i, par, t):
                sp.wait_ge(s_ql, NQ * (2 * i + par) + t + 1)
                out = (q_out, k_out)[t // KD]
                h0 = (t % KD) * P
                for part, s in ((0, qh), (1, ql)):
                    sp.dma_start(out[part, bass.ds(i, 1), h0:h0 + P, par * GROUP:(par + 1) * GROUP].rearrange(
                        "o d q -> (o d) q"), s[t % NB][:, :].bitcast(F32)).then_inc(s_q_stored[t % NB], 16)

            def store_v(i, par, j):
                sp.wait_ge(s_v, TJ * (2 * i + par) + j + 1)
                sp.dma_start(v_out[bass.ds(i, 1), :, par * GROUP + j * P:par * GROUP + (j + 1) * P, :].rearrange(
                    "o g t c -> t (o g) c"), v[j][:, :, :].rearrange("p (g h) c -> p g (h c)", h=2)).then_inc(
                        s_v_stored[j], 16)

            load(0, 0)
            load_xn(0, 0)
            for m in range(3):
                sp.dma_start(wraw[m][:, :, :], wT[m].rearrange("(k p) n -> p k n", p=P)).then_inc(s_wraw[m], 16)
            sp.wait_ge(s_w, 3)
            load(0, 1)
            load_xn(0, 1)
            store_x(0, 0)

            def step(i, par, nxt, far):
                if far:
                    load(*far)
                for turn in range(NQ + TJ):
                    if far and turn == 0:
                        load_xn(*far)
                    if nxt and turn == 2:
                        store_x(*nxt)
                    if 2 <= turn < NQ + 2:
                        store_q(i, par, turn - 2)
                    if turn >= NQ:
                        store_v(i, par, turn - NQ)

            rounds_ahead(sp, NG, step)
            for par in range(2):
                sp.wait_ge(s_x1_stored[par], 16 * (NG // 2))
            for t in range(NB):
                sp.wait_ge(s_q_stored[t], 32 * NG * NQ // NB)
            for j in range(TJ):
                sp.wait_ge(s_v_stored[j], 16 * NG)

        @block.gpsimd
        def _(pool):
            nc.gpsimd.memset(eps[:, :], EPS).then_inc(s_memset, 1)
            for b in range(TJ):
                nc.gpsimd.memset(v[b][:, :, HD:2 * HD], 1.0).then_inc(s_memset, 1)

            def gather(i, par):
                r = 2 * i + par
                work_out(pool, 32 * (i + 1), TJ * r)
                pool.wait_ge(*met)
                pool.wait_ge(s_meta[par], 32 * (i + 1))
                pool.wait_ge(s_x1, TJ * r)
                for j in range(TJ):
                    nc.gpsimd.indirect_dma_start(
                        out=yg[:, j, :], out_offset=None, in_=y,
                        in_offset=bass.IndirectOffsetOnAxis(ap=slot[par][:, j:j + 1], axis=0),
                        bounds_check=NOSLOT, oob_is_err=False).then_inc(s_yg, 16)

            def turn(i, par, t):
                n = NQ * (2 * i + par) + t
                pool.wait_ge(s_qb, n + 1)
                pool.wait_ge(s_ql, past(n - NB + 1))
                nc.gpsimd.tensor_tensor(out=qc[t % NB][:, :], in0=qb[t % NB][:, :],
                                        in1=cos[:, par * GROUP:(par + 1) * GROUP], op=ALU.mult).then_inc(s_qc, 1)
                pool.wait_ge(s_qs, n + 1)
                nc.gpsimd.tensor_tensor(out=qs[t % NB][:, :], in0=qs[t % NB][:, :],
                                        in1=sin[:, par * GROUP:(par + 1) * GROUP], op=ALU.mult).then_inc(s_qc, 1)

            def step(i, par, nxt, far):
                for t in range(NQ):
                    turn(i, par, t)
                if far:
                    gather(*far)

            pool.wait_ge(s_const, 96)
            gather(0, 0)
            gather(0, 1)
            rounds_ahead(pool, NG, step)

        @block.scalar
        def _(act):
            act.wait_ge(s_memset, 1 + TJ)
            act.wait_ge(s_const, 96)
            for m in range(3):
                act.wait_ge(s_wraw[m], 16)
                nc.scalar.activation(w[m][0][:, :, :], wraw[m][:, :, :], ACT.Copy).then_inc(s_wh, 1)

            def norm(i, par):
                r = 2 * i + par
                act.wait_ge(s_mv, TJ * (r + 1))
                nc.scalar.activation(std[:, :], mv[:, :, 1], ACT.Sqrt, bias=eps[:, 0:1]).then_inc(s_std, 1)

            def hi_x(i, par, j):
                n = TJ * (2 * i + par) + j
                act.wait_ge(s_tp, n + 1)
                act.wait_ge(s_vp, past(TJ * (2 * i + par - 1)))
                nc.scalar.activation(xT[par][0][:, :, j * P:(j + 1) * P], tp[j % 2][:, :, :],
                                     ACT.Copy).then_inc(s_xh, 1)

            def copy_q(i, par, t):
                n = NQ * (2 * i + par) + t
                act.wait_ge(s_pp, n + 1)
                act.wait_ge(s_qc, past(2 * (n - NB + 1)))
                nc.scalar.activation(qb[t % NB][:, :], pp[t % NB][:, :], ACT.Identity,
                                     bias=bqk[t // KD][:, t % KD:t % KD + 1]).then_inc(s_qb, 1)

            def hi_q(i, par, t):
                r = 2 * i + par
                act.wait_ge(s_rot, NQ * r + t + 1)
                act.wait_ge(s_q_stored[t % NB], 32 * (NQ // NB * r + t // NB))
                nc.scalar.activation(qh[t % NB][:, :], qc[t % NB][:, :], ACT.Copy).then_inc(s_qh, 1)

            def step(i, par, nxt, far):
                for t in range(NQ):
                    if nxt and t >= 5:
                        hi_x(*nxt, t - 5)
                    copy_q(i, par, t)
                    if t >= 2:
                        hi_q(i, par, t - 2)
                    if nxt and t == 2:
                        norm(*nxt)
                if nxt:
                    hi_x(*nxt, 3)
                hi_q(i, par, NQ - 2)
                hi_q(i, par, NQ - 1)

            norm(0, 0)
            for j in range(TJ):
                hi_x(0, 0, j)
            rounds_ahead(act, NG, step)

        @block.vector
        def _(dve):
            dve.wait_ge(s_const, 96)
            dve.wait_ge(s_memset, 1 + TJ)
            for m in range(3):
                dve.wait_ge(s_wh, m + 1)
                nc.vector.tensor_tensor(out=w[m][1][:, :, :], in0=wraw[m][:, :, :], in1=w[m][0][:, :, :].bitcast(F32),
                                        op=ALU.subtract).then_inc(s_w, 1)

            def half(i, par):
                r = 2 * i + par
                dve.wait_ge(s_x[par], 16 * (i + 1))
                dve.wait_ge(s_xn_in, 16 * (r + 1))
                nc.vector.scalar_tensor_tensor(x[par][:, :, :].rearrange("p j n -> p (j n)"),
                                               xn[:, :, :].rearrange("p j n -> p (j n)"), 0.5,
                                               x[par][:, :, :].rearrange("p j n -> p (j n)"),
                                               ALU.mult, ALU.add).then_inc(s_half, 1)

            def add_y(i, par, js):
                r = 2 * i + par
                dve.wait_ge(s_half, r + 1)
                dve.wait_ge(s_yg, 16 * TJ * (r + 1))
                dve.wait_ge(s_meta[par], 32 * (i + 1))
                for j in js:
                    nc.vector.scalar_tensor_tensor(x[par][:, j, :], yg[:, j, :], gateh[par][:, j:j + 1],
                                                   x[par][:, j, :], ALU.mult, ALU.add).then_inc(s_x1, 1)
                for j in js:
                    dve.wait_ge(s_x1, TJ * r + j + 1)
                    dve.wait_ge(s_mv, past(TJ * r + j - 1))
                    nc.vector.bn_stats(stats[j % 2][:, :], x[par][:, j, :]).then_inc(s_stats, 1)
                for j in js:
                    work_out(dve, TJ * r + j + 1, r, TJ * r)
                    dve.wait_ge(*met)
                    dve.wait_ge(s_stats, TJ * r + j + 1)
                    dve.wait_ge(s_std, r)
                    dve.wait_ge(s_xa, TJ * r)
                    nc.vector.bn_aggr(mv[:, j, :], stats[j % 2][:, :]).then_inc(s_mv, 1)

            def normalise(i, par):
                r = 2 * i + par
                dve.wait_ge(s_std, r + 1)
                dve.wait_ge(s_mv, TJ * (r + 1))
                nc.vector.reciprocal(rstd[:, :], std[:, :]).then_inc(s_rstd, 1)
                dve.wait_ge(s_rstd, r + 1)
                dve.wait_ge(s_tp, TJ * r)
                for j in range(TJ):
                    nc.vector.tensor_scalar(xa[:, j, :], x[par][:, j, :], mv[:, j, 0:1], rstd[:, j:j + 1],
                                            ALU.subtract, ALU.mult).then_inc(s_xa, 1)

            def lo_x(i, par, j):
                n = TJ * (2 * i + par) + j
                dve.wait_ge(s_xh, n + 1)
                nc.vector.tensor_tensor(out=xT[par][1][:, :, j * P:(j + 1) * P], in0=tp[j % 2][:, :, :],
                                        in1=xT[par][0][:, :, j * P:(j + 1) * P].bitcast(F32),
                                        op=ALU.subtract).then_inc(s_xl, 1)

            def swap(i, par, t):
                n = NQ * (2 * i + par) + t
                work_out(dve, n + 1, n - NB + 1)
                dve.wait_ge(*met)
                dve.wait_ge(s_qb, n + 1)
                dve.wait_ge(s_rot, past(n - NB + 1))
                nc.vector.stream_shuffle(qs[t % NB][:, :], qb[t % NB][:, :], SWAP).then_inc(s_qs, 1)

            def rotate(i, par, t):
                n = NQ * (2 * i + par) + t
                dve.wait_ge(s_qc, 2 * (n + 1))
                nc.vector.tensor_tensor(out=qc[t % NB][:, :], in0=qc[t % NB][:, :], in1=qs[t % NB][:, :],
                                        op=ALU.add).then_inc(s_rot, 1)

            def lo_q(i, par, t):
                r = 2 * i + par
                dve.wait_ge(s_qh, NQ * r + t + 1)
                dve.wait_ge(s_q_stored[t % NB], 32 * (NQ // NB * r + t // NB))
                nc.vector.tensor_tensor(out=ql[t % NB][:, :], in0=qc[t % NB][:, :], in1=qh[t % NB][:, :].bitcast(F32),
                                        op=ALU.subtract).then_inc(s_ql, 1)

            def copy_v(i, par, j):
                n = TJ * (2 * i + par) + j
                dve.wait_ge(s_vp, n + 1)
                dve.wait_ge(s_v_stored[j], 16 * (2 * i + par))
                nc.vector.tensor_tensor(out=v[j][:, :, 0:HD],
                                        in0=vp[j % 2][:, :].rearrange("p (h d) -> p h d", h=NH),
                                        in1=bv[:, :].rearrange("p (h d) -> p h d", h=NH), op=ALU.add).then_inc(s_v, 1)

            def step(i, par, nxt, far):
                for t in range(NQ + TJ):
                    if nxt and t == 3:
                        normalise(*nxt)
                    if nxt and 5 <= t < 5 + TJ:
                        lo_x(*nxt, t - 5)
                    if t < NQ:
                        swap(i, par, t)
                    if 1 <= t < NQ + 1:
                        rotate(i, par, t - 1)
                    if 2 <= t < NQ + 2:
                        lo_q(i, par, t - 2)
                    if t >= NQ:
                        copy_v(i, par, t - NQ)
                    if nxt and t == 1:
                        add_y(*nxt, (2, 3))
                    if far and t == NQ + 1:
                        half(*far)
                    if far and t == NQ + 3:
                        add_y(*far, (0, 1))

            half(0, 0)
            add_y(0, 0, (0, 1))
            add_y(0, 0, (2, 3))
            normalise(0, 0)
            for j in range(TJ):
                lo_x(0, 0, j)
            half(0, 1)
            add_y(0, 1, (0, 1))
            rounds_ahead(dve, NG, step)

        @block.tensor
        def _(pe):
            pe.wait_ge(s_const, 96)
            pe.wait_ge(s_w, 3)

            def turn(i, par, j):
                n = TJ * (2 * i + par) + j
                pe.wait_ge(s_xa, n + 1)
                pe.wait_ge(s_xl, past(n - 1))
                for k in range(KD):
                    last = nc.tensor.transpose(tp[j % 2][:, k, :], xa[:, j, k * P:(k + 1) * P], ident[:, :])
                last.then_inc(s_tp, 1)

            def project(i, par, t):
                n = NQ * (2 * i + par) + t
                pe.wait_ge(s_qb, past(n - NB + 1))
                m, c = t // KD, t % KD
                for k in range(KD):
                    last = matmul3(nc, pp[t % NB][:, :], [s[:, k, c * P:(c + 1) * P] for s in w[m]],
                                   [s[:, k, :] for s in xT[par]], k == 0, k == KD - 1)
                last.then_inc(s_pp, 1)

            def values(i, par, j):
                n = TJ * (2 * i + par) + j
                pe.wait_ge(s_v, past(n - 1))
                for k in range(KD):
                    last = matmul3(nc, vp[j % 2][:, :], [s[:, k, j * P:(j + 1) * P] for s in xT[par]],
                                   [s[:, k, :] for s in w[2]], k == 0, k == KD - 1)
                last.then_inc(s_vp, 1)

            def step(i, par, nxt, far):
                r = 2 * i + par
                pe.wait_ge(s_xl, TJ * (r + 1))
                for t in range(NQ):
                    project(i, par, t)
                    if nxt and t >= 4:
                        turn(*nxt, t - 4)
                for j in range(TJ):
                    values(i, par, j)

            for j in range(TJ):
                turn(0, 0, j)
            rounds_ahead(pe, NG, step)


def attention(nc, name, q_in, k_in, v_in, cst, ao_out, sum_out):
    S = Space(nc, name)
    sb, ps, sem = S.sb, S.ps, S.sem
    NP = B * NH // 2
    KT = L // P
    HALF = L // 2
    SCALE = 1.0 / float(HD) ** 0.5
    NM = 2 * KT * 2
    MAXES = 5 * [(1, 1, 2, 1)] + [(1, 1, 0, 0), (0, 0, 0, 0), (0, 1, 2, 2)]
    FIRST = sum(MAXES[-1])
    assert sum(map(sum, MAXES)) == NM
    DEPTH = 4
    assert sum(map(sum, MAXES)) == NM
    with S.ctx:
        ident = sb("ident", [P, P])
        identb = sb("identb", [P, P], BF16)
        qst = [sb(f"q{b}", [P, 2, L], F32R) for b in range(DEPTH)]
        kst = [sb(f"k{b}", [P, 2, L], F32R) for b in range(DEPTH)]
        v = [sb(f"v{b}", [P, KT, 2, 2 * HD]) for b in range(DEPTH)]
        pr = [S.pair(sb, f"p{h}", [P, L]) for h in range(2)]
        halves = [sb(f"halves{h}", [P, KT, 2]) for h in range(2)]
        big = [sb(f"big{h}", [P, KT]) for h in range(2)]
        parts = [sb(f"parts{h}", [P, KT, HD], BF16) for h in range(2)]
        o = S.pair(sb, "o", [P, L])
        st = [ps(f"st{h}", [P, L]) for h in range(2)]
        mx = ps("mx", [P, L])
        op = ps("op", [P, L])

        s_const = sem("s_const")
        s_memset = sem("s_memset")
        s_identb = sem("s_identb")
        s_in = [sem(f"s_in{b}") for b in range(DEPTH)]
        s_mx = sem("s_mx")
        s_max = sem("s_max")
        s_big = sem("s_big")
        s_mhi = sem("s_mhi")
        s_mlo = sem("s_mlo")
        s_row = sem("s_row")
        s_rowq0 = sem("s_rowq0")
        s_rowq1 = sem("s_rowq1")
        s_st = [sem(f"s_st{h}") for h in range(2)]
        s_exp = [sem(f"s_exp{h}") for h in range(2)]
        s_pv = sem("s_pv")
        s_o = sem("s_o")
        s_o_stored = S.pair(sem, "s_o_stored")
        block = S.block()
        N_OUT = 4
        N_IN = 6 + 1

        def ahead(i, b, k):
            return i + (b + k) // DEPTH, (b + k) % DEPTH

        @block.sync
        def _(sp):
            sp.dma_start(ident[:, :], cst["ident"]).then_inc(s_const, 16)

            def load(i, b):
                p = DEPTH * i + b
                for h in range(2):
                    sp.wait_ge(s_st[h], past(KT * (p - DEPTH + 1)))
                for blk, (qp, kp) in enumerate(((0, 0), (0, 1), (1, 0))):
                    for dst, src, part in ((qst, q_in, qp), (kst, k_in, kp)):
                        sp.dma_start(dst[b][blk * HD:(blk + 1) * HD, :, :].bitcast(F32),
                                     src[part, bass.ds(p * (2 * HD), 2 * HD), :].rearrange(
                                         "(h d) q -> d h q", h=2)).then_inc(s_in[b], 16)
                sp.wait_ge(s_pv, past(KT * (p - DEPTH + 1)))
                sp.dma_start(v[b][:, :, :, :].rearrange("p t h c -> p t (h c)"), v_in[bass.ds(p, 1), :, :].rearrange(
                    "o (t p) c -> p (o t) c", p=P)).then_inc(s_in[b], 16)

            def store(p, par):
                sp.wait_ge(s_o, p + 1)
                for h in range(2):
                    sp.dma_start(ao_out[bass.ds(p * (2 * HD) + h * HD, HD), :],
                                 o[par][2 * h * HD:(2 * h + 1) * HD, :]).then_inc(s_o_stored[par], 16)
                    sp.dma_start(sum_out[bass.ds(2 * p + h, 1), :],
                                 o[par][(2 * h + 1) * HD:(2 * h + 1) * HD + 1, :]).then_inc(s_o_stored[par], 16)

            def step(i, b, left):
                if left >= 2:
                    load(*ahead(i, b, 2))
                if not isinstance(i, int) or i + b > 0:
                    store(DEPTH * i + b - 1, (b + 1) % 2)

            load(0, 0)
            load(0, 1)
            rounds_by(DEPTH, sp, NP, step)
            store(NP - 1, 1)
            for par in range(2):
                sp.wait_ge(s_o_stored[par], 16 * N_OUT * (NP // 2))

        @block.gpsimd
        def _(pool):
            for h in range(2):
                nc.gpsimd.memset(parts[h][:, :, :], 0.0).then_inc(s_memset, 1)
            pool.wait_ge(s_memset, 2)
            for h in range(2):
                for b in range(DEPTH):
                    nc.gpsimd.memset(kst[b][3 * HD:4 * HD, h, :].bitcast(F32), -1.0).then_inc(s_memset, 1)

        @block.scalar
        def _(act):
            def exps(p, kt, h):
                n = KT * p + kt
                act.wait_ge(s_st[h], n + 1)
                act.wait_ge(s_pv, past(n - 1))
                nc.scalar.activation(pr[h][kt % 2][:, :], st[h][:, :], ACT.Exp, scale=SCALE).then_inc(s_exp[h], 1)

            def copy_row(i, b):
                act.wait_ge(s_row, DEPTH * i + b + 1)
                nc.scalar.activation(qst[b][3 * HD:4 * HD, 1, :], mx[2 * HD:3 * HD, :],
                                     ACT.Copy).then_inc(s_rowq1, 1)

            def step(i, b, left):
                p = DEPTH * i + b
                par = b % 2
                for kt in range(1, KT):
                    exps(p, kt, 0)
                    if left and kt == KT - 1:
                        copy_row(*ahead(i, b, 1))
                    exps(p, kt, 1)
                if left:
                    for h in range(2):
                        exps(p + 1, 0, h)
                act.wait_ge(s_pv, KT * (p + 1))
                act.wait_ge(s_o_stored[par], 16 * N_OUT * (DEPTH // 2 * i + b // 2))
                nc.scalar.activation(o[par][:, :], op[:, :], ACT.Copy).then_inc(s_o, 1)

            copy_row(0, 0)
            for h in range(2):
                exps(0, 0, h)
            rounds_by(DEPTH, act, NP, step)

        @block.vector
        def _(dve):
            dve.wait_ge(s_const, 16)
            dve.wait_ge(s_memset, 2 + 2 * DEPTH)
            nc.vector.tensor_copy(identb[:, :], ident[:, :]).then_inc(s_identb, 1)

            def maxima(i, b):
                p = DEPTH * i + b
                for n in range(NM):
                    h, qt, c = n // (2 * KT), n // 2 % KT, n % 2
                    dve.wait_ge(s_mx, NM * p + n + 1)
                    nc.vector.tensor_reduce(out=halves[h][:, qt, c:c + 1], in_=mx[:, c * HALF:(c + 1) * HALF],
                                            axis=AX.X, op=ALU.max).then_inc(s_max, 1)
                dve.wait_ge(s_max, NM * (p + 1))
                for h in range(2):
                    nc.vector.tensor_tensor(out=big[h][:, :], in0=halves[h][:, :, 0], in1=halves[h][:, :, 1],
                                            op=ALU.max).then_inc(s_big, 1)
                dve.wait_ge(s_big, 2 * p + 2)
                for h in range(2):
                    nc.vector.tensor_copy(parts[h][:, :, 0], big[h][:, :]).then_inc(s_mhi, 1)
                dve.wait_ge(s_mhi, 2 * p + 2)
                for h in range(2):
                    nc.vector.tensor_tensor(out=parts[h][:, :, 1], in0=big[h][:, :], in1=parts[h][:, :, 0],
                                            op=ALU.subtract).then_inc(s_mlo, 1)
                dve.wait_ge(s_row, p + 1)
                nc.vector.tensor_copy(qst[b][3 * HD:4 * HD, 0, :], mx[3 * HD:4 * HD, :]).then_inc(s_rowq0, 1)

            def step(i, b, left):
                if left:
                    maxima(*ahead(i, b, 1))

            maxima(0, 0)
            rounds_by(DEPTH, dve, NP, step)

        @block.tensor
        def _(pe):
            pe.wait_ge(s_const, 16)
            pe.wait_ge(s_memset, 2 + 2 * DEPTH)
            pe.wait_ge(s_identb, 1)

            def rough(i, b, n):
                p = DEPTH * i + b
                h, qt, c = n // (2 * KT), n // 2 % KT, n % 2
                if n == 0:
                    pe.wait_ge(s_in[b], 16 * N_IN * (i + 1))
                    pe.wait_ge(s_rowq0, p)
                    pe.wait_ge(s_rowq1, p)
                pe.wait_ge(s_max, past(NM * p + n - 1))
                nc.tensor.matmul(mx[:, c * HALF:(c + 1) * HALF], qst[b][0:3 * HD, h, qt * P:(qt + 1) * P],
                                 kst[b][0:3 * HD, h, c * HALF:(c + 1) * HALF],
                                 start=True, stop=True).then_inc(s_mx, 1)

            def row(i, b):
                p = DEPTH * i + b
                pe.wait_ge(s_max, NM * (p + 1))
                pe.wait_ge(s_mlo, 2 * (p + 1))
                for h in range(2):
                    out = mx[(3 - h) * HD:(4 - h) * HD, :]
                    for qt in range(KT):
                        last = nc.tensor.matmul(out[:, qt * P:(qt + 1) * P], parts[h][:, qt, :], identb[:, :],
                                                start=True, stop=True)
                last.then_inc(s_row, 1)

            def scores(p, b, kt, h):
                n = KT * p + kt
                if kt == 0:
                    pe.wait_ge((s_rowq0, s_rowq1)[h], p + 1)
                pe.wait_ge(s_exp[h], n)
                for c in range(2):
                    last = nc.tensor.matmul(st[h][:, c * HALF:(c + 1) * HALF],
                                            kst[b][:, h, kt * P:(kt + 1) * P],
                                            qst[b][:, h, c * HALF:(c + 1) * HALF], start=True, stop=True)
                last.then_inc(s_st[h], 1)

            def products(p, b, kt, c):
                if c == 0:
                    for h in range(2):
                        pe.wait_ge(s_exp[h], KT * p + kt + 1)
                    if kt == 0:
                        pe.wait_ge(s_o, p)
                for h in range(2):
                    last = nc.tensor.matmul(op[2 * h * HD:2 * (h + 1) * HD, c * HALF:(c + 1) * HALF],
                                            v[b][:, kt, h, :], pr[h][kt % 2][:, c * HALF:(c + 1) * HALF],
                                            start=kt == 0, stop=kt == KT - 1)
                if c == 1:
                    last.then_inc(s_pv, 1)

            for n in range(NM):
                rough(0, 0, n)
            row(0, 0)

            def step(i, b, left):
                p = DEPTH * i + b
                nxt = ahead(i, b, 1)
                n = FIRST
                for kt in range(KT):
                    if kt == KT - 1:
                        n = 0
                    for part in range(4):
                        if part >= 2:
                            products(p, b, kt, part - 2)
                        elif kt + 1 < KT:
                            scores(p, b, kt + 1, part)
                        elif left:
                            scores(p + 1, nxt[1], 0, part)
                        if left and kt == KT - 2 and part == 1:
                            row(*nxt)
                        for _ in range(MAXES[kt][part]):
                            if kt == KT - 1:
                                if left >= 2:
                                    rough(*ahead(i, b, 2), n)
                            elif left:
                                rough(*nxt, n)
                            n += 1

            for h in range(2):
                scores(0, 0, 0, h)
            for n in range(FIRST):
                rough(0, 1, n)
            rounds_by(DEPTH, pe, NP, step)


def combine(nc, name, moved, x_in, xn_in, y, slot_in, gate_in, x_out):
    S = Space(nc, name)
    sb, sem = S.sb, S.sem
    with S.ctx:
        x = S.pair(sb, "x", [P, TJ, D])
        xn = S.pair(sb, "xn", [P, TJ, D])
        yg = S.pair(sb, "yg", [P, TJ, D])
        slot = S.pair(sb, "slot", [P, TJ], I32)
        gateh = S.pair(sb, "gateh", [P, TJ])
        s_meta = S.pair(sem, "s_meta")
        s_x = S.pair(sem, "s_x")
        s_yg = moved
        s_half = sem("s_half")
        s_x3 = sem("s_x3")
        s_stored = S.pair(sem, "s_stored")
        block = S.block()
        met = (s_meta[0], 32)

        def rows(ap, i, par):
            return tiles(ap[bass.ds((2 * i + par) * GROUP, GROUP), :])

        def meta(ap, i, par):
            return ap[bass.ds(2 * i + par, 1), :, :].rearrange("o p j -> (o p) j")

        @block.sync
        def _(sp):
            def load(i, par):
                work_out(sp, TJ * (2 * i + par - 1))
                if not isinstance(i, int):
                    sp.wait_ge(*met)
                sp.wait_ge(s_x3, past(TJ * (2 * i + par - 1)))
                sp.wait_ge(s_stored[par], 16 * i)
                sp.dma_start(slot[par][:, :], meta(slot_in, i, par)).then_inc(s_meta[par], 16)
                sp.dma_start(gateh[par][:, :], meta(gate_in, i, par)).then_inc(s_meta[par], 16)
                sp.dma_start(x[par][:, :, :], rows(x_in, i, par)).then_inc(s_x[par], 16)
                sp.dma_start(xn[par][:, :, :], rows(xn_in, i, par)).then_inc(s_x[par], 16)

            rounds(sp, NG, load)

        @block.gpsimd
        def _(pool):
            def gather(i, par):
                work_out(pool, 32 * (i + 1), TJ * (2 * i + par - 1))
                pool.wait_ge(*met)
                pool.wait_ge(s_meta[par], 32 * (i + 1))
                pool.wait_ge(s_x3, past(TJ * (2 * i + par - 1)))
                for j in range(TJ):
                    nc.gpsimd.indirect_dma_start(
                        out=yg[par][:, j, :], out_offset=None, in_=y,
                        in_offset=bass.IndirectOffsetOnAxis(ap=slot[par][:, j:j + 1], axis=0),
                        bounds_check=NOSLOT, oob_is_err=False).then_inc(s_yg[par], 16)

            rounds(pool, NG, gather)

        @block.vector
        def _(dve):
            def add(i, par):
                r = 2 * i + par
                dve.wait_ge(s_x[par], 32 * (i + 1))
                flat = x[par][:, :, :].rearrange("p j n -> p (j n)")
                nc.vector.scalar_tensor_tensor(flat, xn[par][:, :, :].rearrange("p j n -> p (j n)"), 0.5, flat,
                                               ALU.mult, ALU.add).then_inc(s_half, 1)
                dve.wait_ge(s_half, r + 1)
                dve.wait_ge(s_yg[par], 16 * TJ * (i + 1))
                for j in range(TJ):
                    nc.vector.scalar_tensor_tensor(x[par][:, j, :], yg[par][:, j, :], gateh[par][:, j:j + 1],
                                                   x[par][:, j, :], ALU.mult, ALU.add).then_inc(s_x3, 1)

            rounds(dve, NG, add)

        @block.scalar
        def _(act):
            def store(i, par):
                act.wait_ge(s_x3, TJ * (2 * i + par + 1))
                act.dma_start(rows(x_out, i, par), x[par][:, :, :]).then_inc(s_stored[par], 16)

            rounds(act, NG, store)
            for par in range(2):
                act.wait_ge(s_stored[par], 16 * (NG // 2))


def macaron(nc, x, wq, bq, wk, bk, wv, bv, wo, bo, w_router, w_gate, w_up, w_down,
            c_ident, c_tri, c_iota, c_tok, c_cos, c_sin, out):
    cst = {"ident": c_ident, "tri": c_tri, "iota": c_iota, "tok": c_tok, "cos": c_cos, "sin": c_sin}

    def dram(name, shape, dt=F32):
        return nc.dram_tensor(name, shape, dt, kind="Internal").ap()

    xn = [dram(f"xn{n}", [T + 1, D]) for n in range(2)]
    table = [dram(f"table{n}", [NOSLOT, 1], I32) for n in range(2)]
    y = [dram(f"y{n}", [NOSLOT + 1, D]) for n in range(2)]
    slot = [dram(f"slot{n}", [NG, P, TJ], I32) for n in range(2)]
    gate = [dram(f"gate{n}", [NG, P, TJ]) for n in range(2)]
    x1 = dram("x1", [T, D])
    x2 = dram("x2", [T, D])
    q = dram("q", [2, B, D, L])
    k = dram("k", [2, B, D, L])
    v = dram("v", [B, NH // 2, L, 4 * HD])
    ao = dram("ao", [B, D, L])
    sums = dram("sums", [B * NH, L])
    inverse = dram("inverse", [B, KD, P // HD, 1, L])

    def by_row(ap):
        return ap.rearrange("b d q -> (b d) q")

    moved = {n: [nc.alloc_semaphore(name=f"{n}_moved_{par}") for par in range(2)]
             for n in ("r1", "e1", "qkv", "r2", "e2", "c2")}
    route(nc, "r1", moved["r1"], x, w_router, cst, xn[0], table[0], y[0][NOSLOT:NOSLOT + 1, :], slot[0], gate[0])
    experts(nc, "e1", moved["e1"], xn[0], table[0], w_gate, w_up, w_down, cst, y[0])
    qkv(nc, "qkv", moved["qkv"], x, xn[0], y[0], slot[0], gate[0], (wq, wk, wv), (bq, bk, bv), cst, x1, q, k, v)
    attention(nc, "att", q.rearrange("s b d q -> s (b d) q"), k.rearrange("s b d q -> s (b d) q"),
              v.rearrange("b g t c -> (b g) t c"), cst, by_row(ao), sums)
    route(nc, "r2", moved["r2"], x1, w_router, cst, xn[1], table[1], y[1][NOSLOT:NOSLOT + 1, :], slot[1], gate[1],
          attn=(ao, sums, inverse, wo, bo, x2))
    experts(nc, "e2", moved["e2"], xn[1], table[1], w_gate, w_up, w_down, cst, y[1])
    combine(nc, "c2", moved["c2"], x2, xn[1], y[1], slot[1], gate[1], out)


def constants(np):
    inv = (np.float32(1.0) / np.float32(10000.0) ** (np.arange(0, HD, 2, dtype=np.float32) / np.float32(HD))).astype(np.float32)
    angle = np.arange(L, dtype=np.float32)[None, :] * np.tile(inv, 2 * P // HD)[:, None]
    sign = np.where(np.arange(P) % HD < HD // 2, np.float32(-1.0), np.float32(1.0))[:, None]
    t = np.arange(P)
    return {
        "c_ident": np.eye(P, dtype=np.float32),
        "c_tri": (t[:, None] <= t[None, :]).astype(np.float32),
        "c_iota": np.tile(np.arange(E, dtype=np.float32), (P, 1)),
        "c_tok": (t[:, None] + P * np.arange(TJ)[None, :]).astype(np.float32),
        "c_cos": np.cos(angle).astype(np.float32),
        "c_sin": (sign * np.sin(angle)).astype(np.float32),
    }


def kernel(**inputs):
    import numpy as np
    import concourse.bacc as bacc
    from concourse.bass_utils import run_bass_kernel_spmd

    def w(name, turned=False):
        a = inputs[name]
        return np.ascontiguousarray(np.asarray(a).T if turned else np.asarray(a))

    def by_tile(name):
        return np.ascontiguousarray(np.asarray(inputs[name]).reshape(KD, P).T)

    arrays = {
        "x": w("L0_attn_x").reshape(T, D),
        "wq": w("L0_attn_Wq", True), "bq": by_tile("L0_attn_bq"),
        "wk": w("L0_attn_Wk", True), "bk": by_tile("L0_attn_bk"),
        "wv": w("L0_attn_Wv", True), "bv": w("L0_attn_bv"),
        "wo": w("L0_attn_Wo", True), "bo": w("L0_attn_bo"),
        "w_router": w("L0_ffn_w_router"), "w_gate": w("L0_ffn_w_gate"),
        "w_up": w("L0_ffn_w_up"), "w_down": w("L0_ffn_w_down"),
        **constants(np),
    }
    nc = bacc.Bacc("TRN2", target_bir_lowering=False, num_devices=1)
    aps = {n: nc.dram_tensor(f"in_{n}", a.shape, mybir.dt.from_np(a.dtype), kind="ExternalInput").ap()
           for n, a in arrays.items()}
    out = nc.dram_tensor("out", (T, D), F32, kind="ExternalOutput").ap()
    macaron(nc, **aps, out=out)
    r = run_bass_kernel_spmd(nc, [{f"in_{n}": a for n, a in arrays.items()}], core_ids=[0])
    return r.results[0]["out"].reshape(B, L, D)
```
